# Optimizing a Trainium2 kernel written in Bass

```python
import numpy as np
import jax
import jax.numpy as jnp

def _softmax(x, axis=-1):
    return jax.nn.softmax(x, axis=axis)

def _gelu(x):
    return jax.nn.gelu(x, approximate=True)

def _silu(x):
    return jax.nn.silu(x)

def _sigmoid(x):
    return jax.nn.sigmoid(x)

def _layernorm(x, axis=-1, eps=1e-05):
    m = jnp.mean(x, axis=axis, keepdims=True)
    v = jnp.var(x, axis=axis, keepdims=True)
    return (x - m) / jnp.sqrt(v + eps)

def _scatter_add(tgt, idx, src, axis=0):
    return tgt.at[idx].add(src)

def _segment_sum(src, seg, n):
    return jax.ops.segment_sum(src, seg, n)
kernel_name = 'mk_decoder_preln_d2_seqx_r8_0beab3'

def setup_inputs(seed: int=0):
    np.random.seed(seed)
    _w = jnp.asarray

    def _rec_inputs():
        import jax
        import jax.numpy as jnp
        _rk = jax.random.key(seed)
        x = 7.22e-05 + 1 * jax.random.normal(jax.random.fold_in(_rk, 1), (4, 256, 256), jnp.float32)
        _lenS = 256 - jax.random.randint(jax.random.fold_in(_rk, 7), (4,), 0, max(1, 256 // 4) + 1, jnp.int32)
        _lenS2 = 256 - jax.random.randint(jax.random.fold_in(_rk, 8), (4,), 0, max(1, 256 // 4) + 1, jnp.int32)
        _ctx_2048P = jax.random.normal(jax.random.fold_in(_rk, 11), (4, 16, 256), jnp.float32)
        _ctx_2048c = jax.random.dirichlet(jax.random.fold_in(_rk, 511), 0.3 * jnp.ones((16,), jnp.float32), (4, 256))
        _ctx_2048t = jnp.einsum('bsk,bkd->bsd', _ctx_2048c, _ctx_2048P)
        _ctx_2048t = _ctx_2048t * jax.lax.rsqrt(jnp.mean(jnp.square(_ctx_2048t)) + 1e-12) * 0.953939
        ctx_2048 = 4.13588e-05 + 0.999923 * (_ctx_2048t + 0.3 * jax.random.normal(jax.random.fold_in(_rk, 611), (4, 256, 256), jnp.float32))
        return (x, ctx_2048)
    x, ctx_2048 = _rec_inputs()

    def _L0_attn_setup():
        import jax, jax.numpy as jnp
        import numpy as np
        HIDDEN = 256
        NUM_HEADS = 16
        NUM_KV_HEADS = 4
        HEAD_DIM = HIDDEN // NUM_HEADS
        Q_PER_KV = NUM_HEADS // NUM_KV_HEADS
        GROUP_SIZE = (Q_PER_KV + 2) * HEAD_DIM
        TOTAL_PROJ = NUM_KV_HEADS * GROUP_SIZE
        SEQ, BATCH = (256, 2)
        key = jax.random.key(seed)
        k1, k2, k3 = jax.random.split(key, 3)
        x = jax.random.normal(k1, (SEQ, BATCH, HIDDEN), dtype=jnp.float32)
        weight_qkv = jax.random.normal(k2, (TOTAL_PROJ, HIDDEN), dtype=jnp.float32) * 0.02
        weight_proj = jax.random.normal(k3, (HIDDEN, NUM_HEADS * HEAD_DIM), dtype=jnp.float32) * 0.02
        return {'x': x, 'weight_qkv': weight_qkv, 'weight_proj': weight_proj}
    _L0_attn_all = _L0_attn_setup()
    _L0_attn_in = {k: v for k, v in _L0_attn_all.items() if k in ('weight_qkv', 'weight_proj')}
    del _L0_attn_all

    def _L0_xattn_setup():
        import jax, jax.numpy as jnp
        import numpy as np
        BS, S, DK = (8, 64, 256)
        key = jax.random.key(seed)
        kq, kk, kv = jax.random.split(key, 3)
        q = jax.random.normal(kq, (BS, S, DK), dtype=jnp.float32)
        k = jax.random.normal(kk, (BS, S, DK), dtype=jnp.float32)
        v = jax.random.normal(kv, (BS, S, DK), dtype=jnp.float32)
        return {'q': q, 'k': k, 'v': v}
    _L0_xattn_all = _L0_xattn_setup()
    _L0_xattn_in = {k: v for k, v in _L0_xattn_all.items() if k in ()}
    del _L0_xattn_all

    def _L0_ffn_setup():
        import jax, jax.numpy as jnp
        import numpy as np
        EPS = 1e-05

        def _act_quant(x):
            scale = 127.0 / jnp.clip(jnp.max(jnp.abs(x), axis=-1, keepdims=True), EPS)
            return jnp.clip(jnp.round(x * scale), -128.0, 127.0) / scale

        def _weight_quant(w):
            scale = 1.0 / jnp.clip(jnp.mean(jnp.abs(w)), EPS)
            return jnp.clip(jnp.round(w * scale), -1.0, 1.0) / scale

        def _bitlinear(x, w):
            xq = x + jax.lax.stop_gradient(_act_quant(x) - x)
            wq = w + jax.lax.stop_gradient(_weight_quant(w) - w)
            return jnp.einsum('bsd,hd->bsh', xq, wq)
        key = jax.random.key(seed)
        k1, k2, k3 = jax.random.split(key, 3)
        B, S, D, H = (4, 512, 256, 1024)
        x = jax.random.normal(k1, (B, S, D), dtype=jnp.float32)
        w1 = jax.random.normal(k2, (H, D), dtype=jnp.float32) * (1.0 / np.sqrt(D))
        w2 = jax.random.normal(k3, (D, H), dtype=jnp.float32) * (1.0 / np.sqrt(H))
        return {'x': x, 'w1': w1, 'w2': w2}
    _L0_ffn_all = _L0_ffn_setup()
    _L0_ffn_in = {k: v for k, v in _L0_ffn_all.items() if k in ('w1', 'w2')}
    del _L0_ffn_all

    def _L1_attn_setup():
        import jax, jax.numpy as jnp
        import numpy as np
        import math
        D_MODEL = 256
        N_HEADS = 16
        Q_PROJ = D_MODEL // 4
        KV_PROJ = D_MODEL // 4
        DH = D_MODEL // N_HEADS
        LN_EPS = 1e-05

        def _layernorm(x, gamma, beta):
            mu = jnp.mean(x, axis=-1, keepdims=True)
            var = jnp.var(x, axis=-1, keepdims=True)
            return (x - mu) * jax.lax.rsqrt(var + LN_EPS) * gamma + beta
        key = jax.random.key(seed)
        ks = jax.random.split(key, 7)
        B, S = (2, 256)
        x = jax.random.normal(ks[0], (B, S, D_MODEL), dtype=jnp.float32)
        W_dq = 0.01 * jax.random.normal(ks[1], (D_MODEL, Q_PROJ), dtype=jnp.float32)
        W_uq = 0.01 * jax.random.normal(ks[2], (Q_PROJ, D_MODEL), dtype=jnp.float32)
        W_dkv = 0.01 * jax.random.normal(ks[3], (D_MODEL, KV_PROJ), dtype=jnp.float32)
        W_ukv = 0.01 * jax.random.normal(ks[4], (KV_PROJ, 2 * D_MODEL), dtype=jnp.float32)
        W_o = 0.01 * jax.random.normal(ks[5], (D_MODEL, D_MODEL), dtype=jnp.float32)
        q_ln_g = jnp.ones((Q_PROJ,), jnp.float32)
        q_ln_b = jnp.zeros((Q_PROJ,), jnp.float32)
        kv_ln_g = jnp.ones((KV_PROJ,), jnp.float32)
        kv_ln_b = jnp.zeros((KV_PROJ,), jnp.float32)
        return {'x': x, 'W_dq': W_dq, 'W_uq': W_uq, 'q_ln_g': q_ln_g, 'q_ln_b': q_ln_b, 'W_dkv': W_dkv, 'W_ukv': W_ukv, 'kv_ln_g': kv_ln_g, 'kv_ln_b': kv_ln_b, 'W_o': W_o}
    _L1_attn_all = _L1_attn_setup()
    _L1_attn_in = {k: v for k, v in _L1_attn_all.items() if k in ('W_dq', 'W_uq', 'q_ln_g', 'q_ln_b', 'W_dkv', 'W_ukv', 'kv_ln_g', 'kv_ln_b', 'W_o')}
    del _L1_attn_all

    def _L1_xattn_setup():
        import jax, jax.numpy as jnp
        import numpy as np
        D_MODEL = 256
        NUM_HEADS = 16
        HEAD_DIM = D_MODEL // NUM_HEADS

        def _fq_sym(x, axis):
            s = jnp.max(jnp.abs(x), axis=axis, keepdims=True) / 127.0
            s = jnp.maximum(s, 1e-08)
            q = jnp.clip(jnp.round(x / s), -127.0, 127.0) * s
            return x + jax.lax.stop_gradient(q - x)

        def _fq_unsigned(x, axis):
            s = jnp.max(x, axis=axis, keepdims=True) / 255.0
            s = jnp.maximum(s, 1e-08)
            q = jnp.clip(jnp.round(x / s), 0.0, 255.0) * s
            return x + jax.lax.stop_gradient(q - x)
        key = jax.random.key(seed)
        ks = jax.random.split(key, 8)
        B, N, M, C = (2, 256, 64, D_MODEL)
        return {'x': jax.random.normal(ks[0], (B, N, C), jnp.float32), 'cond': jax.random.normal(ks[1], (B, M, C), jnp.float32), 'Wq': jax.random.normal(ks[2], (C, C), jnp.float32) * 0.02, 'bq': jnp.zeros((C,), jnp.float32), 'Wkv': jax.random.normal(ks[3], (C, 2 * C), jnp.float32) * 0.02, 'bkv': jnp.zeros((2 * C,), jnp.float32), 'Wp': jax.random.normal(ks[4], (C, C), jnp.float32) * 0.02, 'bp': jnp.zeros((C,), jnp.float32)}
    _L1_xattn_all = _L1_xattn_setup()
    _L1_xattn_in = {k: v for k, v in _L1_xattn_all.items() if k in ('Wq', 'bq', 'Wkv', 'bkv', 'Wp', 'bp')}
    del _L1_xattn_all

    def _L1_ffn_setup():
        import jax, jax.numpy as jnp
        import numpy as np
        B, S, H = (2, 128, 256)
        I = 128
        E = 32
        Z = 32
        K = 8
        SCALE = 1.5
        CAP = 128
        EPS = 1e-20

        def _moe_forward(x, w_cls, bias, w_gate_up, w_down):
            T = x.shape[0] * x.shape[1]
            xf = x.reshape(T, H)
            logits = xf.astype(jnp.float32) @ w_cls.T
            scores = jax.nn.softmax(logits, axis=-1)
            _, topk_idx = jax.lax.top_k(scores + bias[None, :], K)
            w = jnp.take_along_axis(scores, topk_idx, axis=-1)
            w = w / (w.sum(-1, keepdims=True) + EPS) * SCALE
            routed = topk_idx < E
            w_r = jnp.where(routed, w, 0.0)
            w_z = jnp.where(routed, 0.0, w)
            N = T * K
            flat_ids = jnp.where(routed, topk_idx, E).reshape(-1)
            x_exp = jnp.repeat(xf, K, axis=0)
            order = jnp.argsort(flat_ids)
            ids_s = flat_ids[order]
            counts = jax.ops.segment_sum(jnp.ones(N, jnp.int32), flat_ids, num_segments=E + 1)
            starts = jnp.cumsum(counts) - counts
            pos = jnp.arange(N) - starts[ids_s]
            buf = jnp.zeros((E, CAP, H), xf.dtype).at[ids_s, pos].set(x_exp[order], mode='drop')
            gu = jnp.einsum('ech,ehf->ecf', buf, w_gate_up)
            g, u = jnp.split(gu, 2, axis=-1)
            act = jax.nn.silu(g) * u
            y = jnp.einsum('eci,eih->ech', act, w_down)
            valid = (ids_s < E) & (pos < CAP)
            y_tok = jnp.where(valid[:, None], y[jnp.clip(ids_s, 0, E - 1), jnp.clip(pos, 0, CAP - 1)], 0.0)
            y_exp = jnp.zeros((N, H), xf.dtype).at[order].set(y_tok).reshape(T, K, H)
            routed_out = jnp.einsum('tk,tkh->th', w_r, y_exp)
            out = routed_out * (1.0 + w_z.sum(-1, keepdims=True))
            return out.reshape(x.shape)
        key = jax.random.key(seed)
        ks = jax.random.split(key, 5)
        x = jax.random.normal(ks[0], (B, S, H), jnp.float32)
        w_cls = jax.random.normal(ks[1], (E + Z, H), jnp.float32) / np.float32(np.sqrt(H))
        bias = jax.random.normal(ks[2], (E + Z,), jnp.float32) * 0.02
        w_gate_up = jax.random.normal(ks[3], (E, H, 2 * I), jnp.float32) * 0.02
        w_down = jax.random.normal(ks[4], (E, I, H), jnp.float32) * 0.02
        return {'x': x, 'w_cls': w_cls, 'bias': bias, 'w_gate_up': w_gate_up, 'w_down': w_down}
    _L1_ffn_all = _L1_ffn_setup()
    _L1_ffn_in = {k: v for k, v in _L1_ffn_all.items() if k in ('w_cls', 'bias', 'w_gate_up', 'w_down')}
    del _L1_ffn_all
    return {'x': x, 'ctx_2048': ctx_2048, 'L0_attn_weight_qkv': _L0_attn_in['weight_qkv'], 'L0_attn_weight_proj': _L0_attn_in['weight_proj'], 'L0_ffn_w1': _L0_ffn_in['w1'], 'L0_ffn_w2': _L0_ffn_in['w2'], 'L1_attn_W_dq': _L1_attn_in['W_dq'], 'L1_attn_W_uq': _L1_attn_in['W_uq'], 'L1_attn_q_ln_g': _L1_attn_in['q_ln_g'], 'L1_attn_q_ln_b': _L1_attn_in['q_ln_b'], 'L1_attn_W_dkv': _L1_attn_in['W_dkv'], 'L1_attn_W_ukv': _L1_attn_in['W_ukv'], 'L1_attn_kv_ln_g': _L1_attn_in['kv_ln_g'], 'L1_attn_kv_ln_b': _L1_attn_in['kv_ln_b'], 'L1_attn_W_o': _L1_attn_in['W_o'], 'L1_xattn_Wq': _L1_xattn_in['Wq'], 'L1_xattn_bq': _L1_xattn_in['bq'], 'L1_xattn_Wkv': _L1_xattn_in['Wkv'], 'L1_xattn_bkv': _L1_xattn_in['bkv'], 'L1_xattn_Wp': _L1_xattn_in['Wp'], 'L1_xattn_bp': _L1_xattn_in['bp'], 'L1_ffn_w_cls': _L1_ffn_in['w_cls'], 'L1_ffn_bias': _L1_ffn_in['bias'], 'L1_ffn_w_gate_up': _L1_ffn_in['w_gate_up'], 'L1_ffn_w_down': _L1_ffn_in['w_down']}

def reference(x, ctx_2048, L0_attn_weight_qkv, L0_attn_weight_proj, L0_ffn_w1, L0_ffn_w2, L1_attn_W_dq, L1_attn_W_uq, L1_attn_q_ln_g, L1_attn_q_ln_b, L1_attn_W_dkv, L1_attn_W_ukv, L1_attn_kv_ln_g, L1_attn_kv_ln_b, L1_attn_W_o, L1_xattn_Wq, L1_xattn_bq, L1_xattn_Wkv, L1_xattn_bkv, L1_xattn_Wp, L1_xattn_bp, L1_ffn_w_cls, L1_ffn_bias, L1_ffn_w_gate_up, L1_ffn_w_down):
    import jax
    import jax.numpy as jnp

    def _L0_attn_ref(x, weight_qkv, weight_proj):
        import jax, jax.numpy as jnp
        import numpy as np
        HIDDEN = 256
        NUM_HEADS = 16
        NUM_KV_HEADS = 4
        HEAD_DIM = HIDDEN // NUM_HEADS
        Q_PER_KV = NUM_HEADS // NUM_KV_HEADS
        GROUP_SIZE = (Q_PER_KV + 2) * HEAD_DIM
        TOTAL_PROJ = NUM_KV_HEADS * GROUP_SIZE
        SEQ, BATCH = (256, 2)
        seq, batch, hidden = x.shape
        q_size = Q_PER_KV * HEAD_DIM
        qkv = x.reshape(-1, hidden) @ weight_qkv.T
        qkv = qkv.reshape(-1, NUM_KV_HEADS, GROUP_SIZE)
        q = qkv[:, :, :q_size].reshape(seq, batch, NUM_HEADS, HEAD_DIM)
        k = qkv[:, :, q_size:q_size + HEAD_DIM].reshape(seq, batch, NUM_KV_HEADS, HEAD_DIM)
        v = qkv[:, :, q_size + HEAD_DIM:].reshape(seq, batch, NUM_KV_HEADS, HEAD_DIM)
        k = jnp.repeat(k, Q_PER_KV, axis=2)
        v = jnp.repeat(v, Q_PER_KV, axis=2)
        q = q.transpose(1, 2, 0, 3)
        k = k.transpose(1, 2, 0, 3)
        v = v.transpose(1, 2, 0, 3)
        scale = 1.0 / np.sqrt(HEAD_DIM)
        scores = jnp.einsum('bhqd,bhkd->bhqk', q, k) * scale
        causal = jnp.tril(jnp.ones((seq, seq), dtype=bool))
        scores = jnp.where(causal, scores, jnp.float32(-jnp.inf))
        probs = jax.nn.softmax(scores, axis=-1)
        attn = jnp.einsum('bhqk,bhkd->bhqd', probs, v)
        attn = attn.transpose(2, 0, 1, 3).reshape(seq * batch, NUM_HEADS * HEAD_DIM)
        out = attn @ weight_proj.T
        return out.reshape(seq, batch, hidden)

    def _L0_xattn_ref(q, k, v):
        import jax, jax.numpy as jnp
        import numpy as np
        BS, S, DK = (8, 64, 256)
        dk = q.shape[-1]
        scale = 1.0 / jnp.sqrt(jnp.asarray(dk, dtype=q.dtype))
        scaled = jnp.einsum('bsd,bse->bde', q, k) * scale
        attn = jax.nn.softmax(scaled, axis=1)
        out = jnp.einsum('bde,bse->bsd', attn, v)
        return out

    def _L0_ffn_ref(x, w1, w2):
        import jax, jax.numpy as jnp
        import numpy as np
        EPS = 1e-05

        def _act_quant(x):
            scale = 127.0 / jnp.clip(jnp.max(jnp.abs(x), axis=-1, keepdims=True), EPS)
            return jnp.clip(jnp.round(x * scale), -128.0, 127.0) / scale

        def _weight_quant(w):
            scale = 1.0 / jnp.clip(jnp.mean(jnp.abs(w)), EPS)
            return jnp.clip(jnp.round(w * scale), -1.0, 1.0) / scale

        def _bitlinear(x, w):
            xq = x + jax.lax.stop_gradient(_act_quant(x) - x)
            wq = w + jax.lax.stop_gradient(_weight_quant(w) - w)
            return jnp.einsum('bsd,hd->bsh', xq, wq)
        h = _bitlinear(x, w1)
        h = jax.nn.gelu(h)
        return _bitlinear(h, w2)

    def _L1_attn_ref(x, W_dq, W_uq, q_ln_g, q_ln_b, W_dkv, W_ukv, kv_ln_g, kv_ln_b, W_o):
        import jax, jax.numpy as jnp
        import numpy as np
        import math
        D_MODEL = 256
        N_HEADS = 16
        Q_PROJ = D_MODEL // 4
        KV_PROJ = D_MODEL // 4
        DH = D_MODEL // N_HEADS
        LN_EPS = 1e-05

        def _layernorm(x, gamma, beta):
            mu = jnp.mean(x, axis=-1, keepdims=True)
            var = jnp.var(x, axis=-1, keepdims=True)
            return (x - mu) * jax.lax.rsqrt(var + LN_EPS) * gamma + beta
        B, S, D = x.shape
        H, dh = (N_HEADS, DH)
        cq = _layernorm(x @ W_dq, q_ln_g, q_ln_b)
        Q = cq @ W_uq
        ckv = _layernorm(x @ W_dkv, kv_ln_g, kv_ln_b)
        KV = ckv @ W_ukv
        K, V = (KV[..., :D], KV[..., D:])
        q = Q.reshape(B, S, H, dh).transpose(0, 2, 1, 3)
        k = K.reshape(B, S, H, dh).transpose(0, 2, 1, 3)
        v = V.reshape(B, S, H, dh).transpose(0, 2, 1, 3)
        scores = jnp.einsum('bhqd,bhkd->bhqk', q, k) / math.sqrt(float(dh))
        causal = jnp.tril(jnp.ones((S, S), dtype=bool))
        scores = jnp.where(causal, scores, -jnp.inf)
        attn = jax.nn.softmax(scores, axis=-1)
        o = jnp.einsum('bhqk,bhkd->bhqd', attn, v)
        o = o.transpose(0, 2, 1, 3).reshape(B, S, D)
        return o @ W_o.T

    def _L1_xattn_ref(x, cond, Wq, bq, Wkv, bkv, Wp, bp):
        import jax, jax.numpy as jnp
        import numpy as np
        D_MODEL = 256
        NUM_HEADS = 16
        HEAD_DIM = D_MODEL // NUM_HEADS

        def _fq_sym(x, axis):
            s = jnp.max(jnp.abs(x), axis=axis, keepdims=True) / 127.0
            s = jnp.maximum(s, 1e-08)
            q = jnp.clip(jnp.round(x / s), -127.0, 127.0) * s
            return x + jax.lax.stop_gradient(q - x)

        def _fq_unsigned(x, axis):
            s = jnp.max(x, axis=axis, keepdims=True) / 255.0
            s = jnp.maximum(s, 1e-08)
            q = jnp.clip(jnp.round(x / s), 0.0, 255.0) * s
            return x + jax.lax.stop_gradient(q - x)
        B, N, C = x.shape
        H, hd = (NUM_HEADS, HEAD_DIM)
        q = (x @ Wq + bq).reshape(1, B * N, H, hd)
        kv = (cond @ Wkv + bkv).reshape(1, -1, 2, H, hd)
        k, v = (kv[:, :, 0], kv[:, :, 1])
        scale = 1.0 / np.sqrt(hd).astype(np.float32)
        q = jnp.transpose(q * scale, (0, 2, 1, 3))
        k = jnp.transpose(k, (0, 2, 1, 3))
        v = jnp.transpose(v, (0, 2, 1, 3))
        q = _fq_sym(q, axis=-1)
        k = _fq_sym(k, axis=-1)
        v = _fq_sym(v, axis=2)
        attn = jnp.einsum('bhqd,bhkd->bhqk', q, k)
        attn = jax.nn.softmax(attn.astype(jnp.float32), axis=-1)
        attn = _fq_unsigned(attn, axis=-1)
        out = jnp.einsum('bhqk,bhkd->bhqd', attn, v)
        out = jnp.transpose(out, (0, 2, 1, 3)).reshape(B, N, C)
        return out @ Wp + bp

    def _L1_ffn_ref(x, w_cls, bias, w_gate_up, w_down):
        import jax, jax.numpy as jnp
        import numpy as np
        B, S, H = (2, 128, 256)
        I = 128
        E = 32
        Z = 32
        K = 8
        SCALE = 1.5
        CAP = 128
        EPS = 1e-20

        def _moe_forward(x, w_cls, bias, w_gate_up, w_down):
            T = x.shape[0] * x.shape[1]
            xf = x.reshape(T, H)
            logits = xf.astype(jnp.float32) @ w_cls.T
            scores = jax.nn.softmax(logits, axis=-1)
            _, topk_idx = jax.lax.top_k(scores + bias[None, :], K)
            w = jnp.take_along_axis(scores, topk_idx, axis=-1)
            w = w / (w.sum(-1, keepdims=True) + EPS) * SCALE
            routed = topk_idx < E
            w_r = jnp.where(routed, w, 0.0)
            w_z = jnp.where(routed, 0.0, w)
            N = T * K
            flat_ids = jnp.where(routed, topk_idx, E).reshape(-1)
            x_exp = jnp.repeat(xf, K, axis=0)
            order = jnp.argsort(flat_ids)
            ids_s = flat_ids[order]
            counts = jax.ops.segment_sum(jnp.ones(N, jnp.int32), flat_ids, num_segments=E + 1)
            starts = jnp.cumsum(counts) - counts
            pos = jnp.arange(N) - starts[ids_s]
            buf = jnp.zeros((E, CAP, H), xf.dtype).at[ids_s, pos].set(x_exp[order], mode='drop')
            gu = jnp.einsum('ech,ehf->ecf', buf, w_gate_up)
            g, u = jnp.split(gu, 2, axis=-1)
            act = jax.nn.silu(g) * u
            y = jnp.einsum('eci,eih->ech', act, w_down)
            valid = (ids_s < E) & (pos < CAP)
            y_tok = jnp.where(valid[:, None], y[jnp.clip(ids_s, 0, E - 1), jnp.clip(pos, 0, CAP - 1)], 0.0)
            y_exp = jnp.zeros((N, H), xf.dtype).at[order].set(y_tok).reshape(T, K, H)
            routed_out = jnp.einsum('tk,tkh->th', w_r, y_exp)
            out = routed_out * (1.0 + w_z.sum(-1, keepdims=True))
            return out.reshape(x.shape)
        return _moe_forward(x, w_cls, bias, w_gate_up, w_down)
    x = x + _L0_attn_ref(_layernorm(x, axis=-1), L0_attn_weight_qkv, L0_attn_weight_proj)
    x = x + _L0_xattn_ref(_layernorm(x, axis=-1), ctx_2048, ctx_2048)
    x = x + _L0_ffn_ref(_layernorm(x, axis=-1), L0_ffn_w1, L0_ffn_w2)
    x = x + _L1_attn_ref(_layernorm(x, axis=-1), L1_attn_W_dq, L1_attn_W_uq, L1_attn_q_ln_g, L1_attn_q_ln_b, L1_attn_W_dkv, L1_attn_W_ukv, L1_attn_kv_ln_g, L1_attn_kv_ln_b, L1_attn_W_o)
    x = x + _L1_xattn_ref(_layernorm(x, axis=-1), ctx_2048, L1_xattn_Wq, L1_xattn_bq, L1_xattn_Wkv, L1_xattn_bkv, L1_xattn_Wp, L1_xattn_bp)
    x = x + _L1_ffn_ref(_layernorm(x, axis=-1), L1_ffn_w_cls, L1_ffn_bias, L1_ffn_w_gate_up, L1_ffn_w_down)
    return x

_drawn_inputs = setup_inputs


def setup_inputs(seed=0):
    import zlib

    import numpy as np

    out = dict(_drawn_inputs(seed))
    spreads = {'L1_attn_q_ln_g': (1.0, 0.6),
     'L1_attn_q_ln_b': (0.0, 0.8),
     'L1_attn_kv_ln_g': (1.0, 0.6),
     'L1_attn_kv_ln_b': (0.0, 0.8),
     'L1_xattn_bq': (0.0, 0.8),
     'L1_xattn_bkv': (0.0, 0.317),
     'L1_xattn_bp': (0.0, 0.1)}
    factors = {'L1_attn_W_dq': 8.0,
     'L1_attn_W_uq': 8.0,
     'L1_attn_W_dkv': 8.0,
     'L1_attn_W_ukv': 8.0,
     'L1_attn_W_o': 8.0,
     'L1_xattn_Wq': 8.0,
     'L1_xattn_Wkv': 2.72,
     'L1_ffn_w_cls': 8.0,
     'L1_ffn_bias': 8.0,
     'L1_ffn_w_gate_up': 8.0,
     'L1_ffn_w_down': 8.0}
    for name, (base, spread) in spreads.items():
        noise = np.random.default_rng([zlib.crc32(name.encode()), seed]).standard_normal(out[name].shape)
        drawn = base * np.exp(spread * noise) if base else spread * noise
        out[name] = jnp.asarray(drawn.astype(out[name].dtype))
    for name, factor in factors.items():
        out[name] = (out[name] * factor).astype(out[name].dtype)
    return out
```

```python
import concourse.bass as bass
from concourse import mybir
from contextlib import ExitStack

F32 = mybir.dt.float32
BF16 = mybir.dt.bfloat16
I16 = mybir.dt.int16
U32 = mybir.dt.uint32
ALU = mybir.AluOpType
ACT = mybir.ActivationFunctionType
AX = mybir.AxisListType

P = 128
NB, SEQ, D = 4, 256, 256
NT = NB * SEQ // P
KD = D // P
H, HD = 16, 16
FF = 1024
KF = FF // P
LOW = 64
NE, NROUTE, TOPK, CAP = 32, 64, 8, 128
SLOTS = NE * CAP
ROUND = 12582912.0
NEG = -1.0e30
YGN = 8
LN255 = 5.541263545158426
EPS = 1e-5
PARITY_ORDER = [0, 2, 4, 6, 1, 3, 5, 7]
IN_ORDER = list(range(NT))


def decoder_kernel(nc, x_in, ctx_in, ctxT_in, wqkvT_in, wprojT_in, w1T_in, w2T_in, wdq_in, wuq_in, qg_in, qb_in,
                   wdkv_in, wukv_in, kvg_in, kvb_in, woT_in, wq_in, bq_in, wkv_in, bkv_in, wp_in, bp_in,
                   wclsT_in, rbias_in, wgu_in, wdown_in, out, stages=6):
    es = ExitStack()
    with es:
        def sb(name, shape, dt=F32):
            return es.enter_context(nc.sbuf_tensor(name, shape, dt))

        def sem(name):
            return es.enter_context(nc.semaphore(name))

        slot_rows = nc.dram_tensor("slot_rows", [SLOTS, D], F32, kind="Internal").ap()
        y_rows = nc.dram_tensor("y_rows", [SLOTS + P, D], F32, kind="Internal").ap()

        ps = es.enter_context(nc.psum_tensor("ps", [P, 8, 512], F32))

        X = sb("X", [P, NT, D])
        XN = sb("XN", [P, NT, D])
        XT = sb("XT", [P, KD, NT * P])
        AT = sb("AT", [P, NT, D])
        stats = sb("stats", [P, NT, 6])
        mv = sb("mv", [P, NT, 2])
        veps = sb("veps", [P, NT])
        rstd = sb("rstd", [P, NT])
        neghalf = sb("neghalf", [P, 16])
        identf = sb("identf", [P, P])
        identb = sb("identb", [P, P], BF16)
        causal = sb("causal", [P, P], BF16)
        onesf = sb("onesf", [P, P])
        zeros = sb("zeros", [P, 4 * D])

        ctx_sb = sb("ctx_sb", [P, NT, D])
        ctxT = sb("ctxT", [P, KD, NT * P])
        wqkvT = sb("wqkvT", [P, KD, 384])
        wprojT = sb("wprojT", [P, KD, D])
        wdown2 = sb("wdown2", [P, KD, 2 * LOW])
        wup = sb("wup", [P, 4, 4, 32])
        wuv = sb("wuv", [P, D])
        lng = sb("lng", [P, 1])
        lnb = sb("lnb", [P, 1])
        woT = sb("woT", [P, KD, D])
        wq5 = sb("wq5", [P, KD, D])
        wkv5 = sb("wkv5", [P, KD, 2 * D])
        wp5 = sb("wp5", [P, KD, D])
        wclsT = sb("wclsT", [P, KD, NROUTE])
        bqr = sb("bqr", [P, D])
        bkvr = sb("bkvr", [P, 2 * D])
        bpr = sb("bpr", [P, D])
        rbias = sb("rbias", [P, NROUTE])

        A = sb("A", [P, 16384])
        qkv = A[:, 0:3072].rearrange("p (t c) -> p t c", t=NT)
        prod = [A[:, 3072 + 2560 * j:3072 + 2560 * (j + 1)].rearrange("p (s c) -> p s c", s=10) for j in range(2)]
        w1stage = A[:, 8192:10240].rearrange("p (k c) -> p k c", k=KD)
        w2stage = A[:, 10240:12288].rearrange("p (k c) -> p k c", k=KF)
        QT4 = A[:, 0:4096].rearrange("p (g c) -> p g c", g=4)
        KT4 = A[:, 4096:8192].rearrange("p (g c) -> p g c", g=4)
        V4 = A[:, 8192:8192 + 2176].rearrange("p (t h c) -> p t h c", t=NT, h=H)
        E4 = A[:, 10368:10368 + 1536].rearrange("p (b j c) -> p b j c", b=2, j=2)
        PT4 = A[:, 11904:11904 + 1536].rearrange("p (b j c) -> p b j c", b=2, j=2)
        CN = A[:, 13440:13440 + 1024].rearrange("p (t c) -> p t c", t=NT)
        CNT = A[:, 14464:14464 + 1024]
        QT5 = A[:, 0:8192].bitcast(BF16).rearrange("p (h c) -> p h c", h=H)
        KT5 = A[:, 8192:16384].bitcast(BF16).rearrange("p (h c) -> p h c", h=H)
        WG = A[:, 0:4096].rearrange("p (s k c) -> p s k c", s=8, k=KD)
        WD = A[:, 4096:6144].rearrange("p (s c) -> p s c", s=8)
        XE = A[:, 6144:7168].rearrange("p (s c) -> p s c", s=4)
        XET = A[:, 7168:7680].rearrange("p (s k c) -> p s k c", s=2, k=KD)
        SG = A[:, 7680:7936].rearrange("p (s c) -> p s c", s=2)
        HE = A[:, 7936:8192].rearrange("p (s c) -> p s c", s=2)
        YE = A[:, 8192:9216].rearrange("p (s c) -> p s c", s=4)
        YG = A[:, 9216:9216 + YGN * D].rearrange("p (s c) -> p s c", s=YGN)

        w1t = sb("w1t", [P, KD, FF], BF16)
        w2t = sb("w2t", [P, KF, D], BF16)

        SC = sb("SC", [P, 8, 4, H])
        mx1 = sb("mx1", [P, 8, H])
        rs1 = sb("rs1", [P, 8, H])

        E2 = A[:, 4352:5376].rearrange("p (i e c) -> p i e c", i=2, e=2)
        nm2 = sb("nm2", [P, 2, 2])
        b2 = sb("b2", [P, 2, 2])
        sum2 = sb("sum2", [P, 2, 2])
        r2 = sb("r2", [P, 2, 2])

        wsum = sb("wsum", [P, 2])
        wmean = sb("wmean", [P, 2])
        wrec = sb("wrec", [P, 2])
        w127 = sb("w127", [P, 2])
        am3 = sb("am3", [P, NT])
        qs3 = sb("qs3", [P, NT])
        dq3 = sb("dq3", [P, NT])
        QX = sb("QX", [P, NT, D], BF16)
        QXT = A[:, 4096:4352].bitcast(BF16).rearrange("p (s k c) -> p s k c", s=2, k=KD)
        G3 = A[:, 0:2048].rearrange("p (s c) -> p s c", s=2)
        am3b = sb("am3b", [P, NT])
        qs3b = sb("qs3b", [P, NT])
        dq3b = sb("dq3b", [P, NT])
        QH = A[:, 2048:3072].bitcast(BF16).rearrange("p (s c) -> p s c", s=2)
        QHT = A[:, 3072:4096].bitcast(BF16).rearrange("p (s k c) -> p s k c", s=2, k=KF)

        st4 = sb("st4", [P, 2 * NT, 6])
        mv4 = sb("mv4", [P, 2 * NT, 2])
        ve4 = sb("ve4", [P, 2 * NT])
        rs4 = sb("rs4", [P, 2 * NT])
        m4 = sb("m4", [P, 2, 2, 2])
        r4 = sb("r4", [P, 2, 4])

        KV = sb("KV", [P, NT, 2 * D])
        kmax = sb("kmax", [P, NT, H])
        sk = sb("sk", [P, NT, H])
        rk = sb("rk", [P, NT, H])
        kpart = sb("kpart", [P, NT, H, 3, HD], BF16)
        ktmp = sb("ktmp", [P, 2, D])
        vmax = sb("vmax", [P, D])
        vm2 = sb("vm2", [P, KD])
        svrv = sb("svrv", [P, 2, KD])
        svb = sb("svb", [P, 4, P])
        svrow = sb("svrow", [P, 4, P])
        VI = sb("VI", [P, NT, D], BF16)
        sq5 = sb("sq5", [P, NT, H])
        rq5 = sb("rq5", [P, NT, H])
        QI = QX
        QI3 = kpart
        kv_flat = KV[:, :, :].rearrange("p t c -> p (t c)")
        Y5 = kv_flat[:, 0:1024].bitcast(I16).rearrange("p (b c) -> p b c", b=2)
        PI5 = kv_flat[:, 1024:2048].bitcast(BF16).rearrange("p (b c) -> p b c", b=2)
        PT5 = kv_flat[:, 2048:3072].bitcast(BF16).rearrange("p (b k c) -> p b k c", b=2, k=8)
        nm5 = sb("nm5", [P, 4])
        b5 = sb("b5", [P, 4])
        sum5 = sb("sum5", [P, H * NT])
        r5 = sb("r5", [P, NT])

        L6, BI6, RP6, MK6 = (ctx_sb[:, 2 * i:2 * i + 2, :].rearrange("p a (t e) -> p (a t) e", e=NROUTE) for i in range(4))
        s6 = sb("s6", [P, 6, NT])
        top6 = sb("top6", [P, NT, 8])
        mr6 = sb("mr6", [P, NT, NE], BF16)
        cum6 = sb("cum6", [P, NT, NE], BF16)
        lower = sb("lower", [P, P], BF16)
        onesb = sb("onesb", [P, P], BF16)
        base6 = sb("base6", [P, NE])
        va6 = sb("va6", [P, NT, NE])
        key6 = sb("key6", [P, NT, NE])
        keys6 = sb("keys6", [P, NT, 8])
        idxf = sb("idxf", [P, NT, 8])
        idx_put = sb("idx_put", [P, NT * 8], U32)
        idx_get = sb("idx_get", [P, NT * 8], U32)
        eq6 = AT[:, :, :].rearrange("p t (k e) -> p t k e", e=NE)
        wk6 = sb("wk6", [P, NT, 8])

        names = """x_loaded w0_loaded ctx_loaded w_loaded w1_loaded w2_loaded low_loaded zero_rows
            const_ready zeros_ready pads_ready rstd_e rstd_ready stats_ready aggr_ready xn_ready x_ready tp_psum tp_ready
            qkv_psum qkv_ready prod0_ready prod1_ready step1 exp1_ready at_ready proj_psum
            kv_psum kv_copied kv_ready kscale_ready kq_step vmax_ready vmaxT_psum vscale_ready vrow_psum vrow_ready vint_ready
            wabs_ready wtot_psum wscale_ready wq_step w_ternary
            s2_psum nm2_ready bias2_ready exp2_ready r2_ready attn2_ready out2_psum
            dq3_step qx_step qx_ready qxT_psum qxT_ready h3_psum gelu_ready am3_step qh_step qh_ready qhT_psum qhT_ready out3_psum
            low_psum lstats_ready laggr_ready lveps lrstd_ready cn_ready cnT_psum cnT_ready up_psum upq_ready upk_ready v4_psum v4_ready
            s4_psum max4_ready sub4_ready exp4_ready p4T_psum p4T_ready o4_psum r4_ready o4_ready
            q5_psum uq5_ready q5_step q5i_ready q5T_psum q5T_ready k5T_psum k5T_ready pad5_ready xbias_ready
            s5_psum max5_ready bias5_ready exp5_ready pi5_ready p5T_psum p5T_ready p5V_done o5_psum r5_ready o5_ready out5_ready
            lg_psum step6 exp6_ready cnt6_ready pos6_psum idx_ready rows_put
            xeT_psum xeT_ready gu_psum silu_ready he_ready ye_psum ye_ready out_stored""".split()
        S = {n: sem(n) for n in names}
        xe_loaded = [sem(f"xe_loaded{i}") for i in range(4)]
        wg_loaded = [sem(f"wg_loaded{i}") for i in range(8)]
        ye_stored = [sem(f"ye_stored{i}") for i in range(4)]
        yg_loaded = [sem(f"yg_loaded{i}") for i in range(YGN)]

        block = es.enter_context(nc.Block())

        def row(ap):
            return ap.partition_broadcast(P)

        U4 = NB * H // 2
        SUB_READY, P_READY = 10, 13
        S_TERN = [0, KD]

        def qkv_heads(t, lo, n):
            return qkv[:, t, :].rearrange("p (g c) -> p g c", g=4)[:, :, lo:lo + n]

        def score_products(eng, e, j, done):
            for iq in range(4):
                for ik in range(iq + 1):
                    q = qkv_heads(2 * iq + j, 0, 64).rearrange("p g (r d) -> p g r d", d=HD)
                    k = qkv_heads(2 * ik + j, 64, HD).unsqueeze(2).to_broadcast([P, 4, 4, HD])
                    o = prod[j][:, iq * (iq + 1) // 2 + ik, :].rearrange("p (g r d) -> p g r d", g=4, d=HD)
                    e.tensor_tensor(o, q, k, ALU.mult).then_inc(done, 1)

        def value_products(eng, e, j, done):
            for iq in range(4):
                for ik in range(iq + 1):
                    w = SC[:, j * 4 + iq, ik, :].rearrange("p (g r) -> p g r", g=4).unsqueeze(3).to_broadcast([P, 4, 4, HD])
                    vv = qkv_heads(2 * ik + j, 80, HD).unsqueeze(2).to_broadcast([P, 4, 4, HD])
                    o = prod[j][:, iq * (iq + 1) // 2 + ik, :].rearrange("p (g r d) -> p g r d", g=4, d=HD)
                    e.tensor_tensor(o, vv, w, ALU.mult).then_inc(done, 1)

        @block.sync
        def _(sp):
            sp.dma_start(X[:, :, :], x_in.rearrange("b (j p) d -> p (b j) d", p=P)).then_inc(S["x_loaded"], 16)
            sp.dma_start(wqkvT[:, :, :], wqkvT_in.rearrange("(k p) c -> p k c", p=P)).then_inc(S["w0_loaded"], 16)
            sp.dma_start(wprojT[:, :, :], wprojT_in.rearrange("(k p) c -> p k c", p=P)).then_inc(S["w0_loaded"], 16)
            sp.dma_start(ctxT[:, :, :], ctxT_in.rearrange("(k p) c -> p k c", p=P)).then_inc(S["ctx_loaded"], 16)
            sp.dma_start(wkv5[:, :, :], wkv_in.rearrange("(k p) c -> p k c", p=P)).then_inc(S["ctx_loaded"], 16)
            sp.dma_start(bkvr[:, :], row(bkv_in)).then_inc(S["ctx_loaded"], 16)
            sp.dma_start(ctx_sb[:, :, :], ctx_in.rearrange("b (j p) d -> p (b j) d", p=P)).then_inc(S["ctx_loaded"], 16)
            sp.dma_start(w1stage, w1T_in.rearrange("(k p) c -> p k c", p=P)).then_inc(S["w1_loaded"], 16)
            sp.dma_start(w2stage, w2T_in.rearrange("(k p) c -> p k c", p=P)).then_inc(S["w2_loaded"], 16)
            sp.dma_start(wdown2[:, :, 0:LOW], wdq_in.rearrange("(k p) c -> p k c", p=P)).then_inc(S["low_loaded"], 16)
            sp.dma_start(wdown2[:, :, LOW:2 * LOW], wdkv_in.rearrange("(k p) c -> p k c", p=P)).then_inc(S["low_loaded"], 16)
            sp.wait_ge(S["pads_ready"], 1)
            wup_heads = wup[:, :, :, :].rearrange("p g r c -> p (g r) c")
            sp.dma_start(wup_heads[0:LOW, :, 0:HD], wuq_in.rearrange("l (h c) -> l h c", c=HD)).then_inc(S["low_loaded"], 16)
            sp.dma_start(wup_heads[LOW:P, :, 0:HD], wukv_in[:, 0:D].rearrange("l (h c) -> l h c", c=HD)).then_inc(S["low_loaded"], 16)
            sp.dma_start(wuv[LOW:P, :], wukv_in[:, D:2 * D]).then_inc(S["low_loaded"], 16)
            for dst, src in ((lng[0:LOW, :], qg_in), (lng[LOW:P, :], kvg_in), (lnb[0:LOW, :], qb_in), (lnb[LOW:P, :], kvb_in)):
                sp.dma_start(dst, src.rearrange("(p a) -> p a", a=1)).then_inc(S["low_loaded"], 16)
            for dst, src in ((woT, woT_in), (wq5, wq_in), (wp5, wp_in), (wclsT, wclsT_in)):
                sp.dma_start(dst[:, :, :], src.rearrange("(k p) c -> p k c", p=P)).then_inc(S["w_loaded"], 16)
            for dst, src in ((bqr, bq_in), (bpr, bp_in), (rbias, rbias_in)):
                sp.dma_start(dst[:, :], row(src)).then_inc(S["w_loaded"], 16)
            sp.wait_ge(S["zeros_ready"], 1)
            if stages >= 6:
                for c in range(SLOTS // (4 * P)):
                    sp.dma_start(slot_rows[c * 4 * P:(c + 1) * 4 * P, :].rearrange("(p a) d -> p (a d)", a=4), zeros[:, :]).then_inc(S["zero_rows"], 16)
                sp.dma_start(y_rows[SLOTS:SLOTS + P, :], zeros[:, 0:D]).then_inc(S["zero_rows"], 16)

                def load_weights(e):
                    sp.dma_start(WG[:, e % 8, :, :], wgu_in[e, :, :].rearrange("(k p) c -> p k c", p=P)).then_inc(wg_loaded[e % 8], 16)
                    sp.dma_start(WD[:, e % 8, :], wdown_in[e, :, :]).then_inc(wg_loaded[e % 8], 16)

                def load_rows(e):
                    sp.dma_start(XE[:, e % 4, :], slot_rows[e * CAP:(e + 1) * CAP, :]).then_inc(xe_loaded[e % 4], 16)

                sp.wait_ge(S["o5_psum"], H)
                for e in range(8):
                    load_weights(e)
                sp.wait_ge(S["rows_put"], 16 * NT * TOPK)
                for e in range(4):
                    load_rows(e)
                for e in range(NE):
                    if e + 4 < NE:
                        sp.wait_ge(S["xeT_psum"], e + 1)
                        load_rows(e + 4)
                    sp.wait_ge(S["ye_ready"], e + 1)
                    sp.dma_start(y_rows[e * CAP:(e + 1) * CAP, :], YE[:, e % 4, :]).then_inc(ye_stored[e % 4], 16)
                    if e + 8 < NE:
                        load_weights(e + 8)
            out_v = out.rearrange("b (j p) d -> p (b j) d", p=P)
            if stages < 6:
                sp.wait_ge(S["x_ready"], 8 * stages)
                sp.dma_start(out_v, X[:, :, :]).then_inc(S["out_stored"], 16)
                sp.wait_ge(S["out_stored"], 16)
            else:
                for t in range(NT):
                    sp.wait_ge(S["x_ready"], 8 * 5 + TOPK * (t + 1))
                    sp.dma_start(out_v[:, t, :], X[:, t, :]).then_inc(S["out_stored"], 16)
                sp.wait_ge(S["out_stored"], 16 * NT)

        @block.gpsimd
        def _(pool):
            g = nc.gpsimd
            g.memset(identf[:, :], 0.0).then_inc(S["const_ready"], 1)
            g.memset(identb[:, :], 0.0).then_inc(S["const_ready"], 1)
            g.memset(neghalf[:, :], -0.5).then_inc(S["const_ready"], 1)
            g.memset(onesf[:, :], 1.0).then_inc(S["const_ready"], 1)
            g.memset(causal[:, :], 0.0).then_inc(S["const_ready"], 1)
            g.memset(lower[:, :], 1.0).then_inc(S["const_ready"], 1)
            g.memset(onesb[:, :], 1.0).then_inc(S["const_ready"], 1)
            pool.wait_ge(S["const_ready"], 7)
            for m in (identf, identb):
                g.affine_select(out=m[:, :], in_=m[:, :], compare_op=ALU.not_equal, fill=1.0, base=0,
                                pattern=[[-1, P]], channel_multiplier=1).then_inc(S["const_ready"], 1)
            g.affine_select(out=causal[:, :], in_=causal[:, :], compare_op=ALU.is_ge, fill=NEG, base=0,
                            pattern=[[-1, P]], channel_multiplier=1).then_inc(S["const_ready"], 1)
            g.affine_select(out=lower[:, :], in_=lower[:, :], compare_op=ALU.is_gt, fill=0.0, base=0,
                            pattern=[[1, P]], channel_multiplier=-1).then_inc(S["const_ready"], 1)
            g.iota(base6[:, :], pattern=[[-CAP, NE]], base=2 * SLOTS, channel_multiplier=0,
                   allow_small_or_imprecise_dtypes=True).then_inc(S["const_ready"], 1)
            g.memset(SC[:, :, :, :], NEG).then_inc(S["const_ready"], 1)
            g.memset(wup[:, :, :, :], 0.0).then_inc(S["pads_ready"], 1)
            g.memset(zeros[:, :], 0.0).then_inc(S["zeros_ready"], 1)

            def norm_rstd(n):
                for s in range(NT):
                    c = n * NT + s + 1
                    t = (PARITY_ORDER if n == 1 else IN_ORDER)[s]
                    pool.wait_ge(S["aggr_ready"], c)
                    g.tensor_scalar(veps[:, t:t + 1], mv[:, t, 1:2], EPS, None, ALU.add).then_inc(S["rstd_e"], 1)
                    pool.wait_ge(S["rstd_e"], c)
                    g.tensor_tensor(rstd[:, t:t + 1], veps[:, t:t + 1], neghalf[:, 0:1], ALU.pow).then_inc(S["rstd_ready"], 1)

            norm_rstd(0)
            pool.wait_ge(S["qkv_ready"], NT)
            score_products(pool, g, 1, S["prod1_ready"])
            pool.wait_ge(S["step1"], P_READY)
            value_products(pool, g, 1, S["prod1_ready"])
            if stages >= 2:
                norm_rstd(1)
            for t in range(NT):
                pool.wait_ge(S["kv_copied"], t + 1)
                g.tensor_tensor(KV[:, t, :], KV[:, t, :], bkvr[:, :], ALU.add).then_inc(S["kv_ready"], 1)
            for w, (stage, dst, n) in enumerate(((w1stage, w1t, FF * KD), (w2stage, w2t, D * KF))):
                pool.wait_ge(S["wscale_ready"], 2)
                for k in range(stage.shape[1]):
                    c = S_TERN[w] + k
                    g.tensor_scalar(stage[:, k, :], stage[:, k, :], wrec[:, w:w + 1], ROUND, ALU.mult, ALU.add).then_inc(S["wq_step"], 1)
                    pool.wait_ge(S["wq_step"], 3 * c + 1)
                    g.tensor_scalar(stage[:, k, :], stage[:, k, :], -ROUND, None, ALU.add).then_inc(S["wq_step"], 1)
                    pool.wait_ge(S["wq_step"], 3 * c + 2)
                    g.tensor_scalar(dst[:, k, :], stage[:, k, :], 1.0, -1.0, ALU.min, ALU.max).then_inc(S["wq_step"], 1)
            pool.wait_ge(S["wq_step"], 3 * (KD + KF))
            pool.sem_inc(S["w_ternary"], 1)
            if stages >= 3:
                norm_rstd(2)
            for t in range(NT if stages >= 2 else 0):
                c = 8 * t
                kt = KV[:, t, 0:D].rearrange("p (h d) -> p h d", h=H)
                a = ktmp[:, 0, :].rearrange("p (h d) -> p h d", h=H)
                b = ktmp[:, 1, :].rearrange("p (h d) -> p h d", h=H)
                if t == 0:
                    pool.wait_ge(S["kscale_ready"], 3)
                if t > 0:
                    pool.wait_ge(S["kq_step"], c)
                g.tensor_tensor(a, kt, rk[:, t, :].unsqueeze(2).to_broadcast([P, H, HD]), ALU.mult).then_inc(S["kq_step"], 1)
                pool.wait_ge(S["kq_step"], c + 1)
                g.tensor_scalar(b, a, ROUND, -ROUND, ALU.add, ALU.add).then_inc(S["kq_step"], 1)
                pool.wait_ge(S["kq_step"], c + 2)
                g.tensor_tensor(a, b, sk[:, t, :].unsqueeze(2).to_broadcast([P, H, HD]), ALU.mult).then_inc(S["kq_step"], 1)
                pool.wait_ge(S["kq_step"], c + 3)
                g.tensor_copy(kpart[:, t, :, 0, :], a).then_inc(S["kq_step"], 1)
                pool.wait_ge(S["kq_step"], c + 4)
                g.tensor_tensor(b, a, kpart[:, t, :, 0, :], ALU.subtract).then_inc(S["kq_step"], 1)
                pool.wait_ge(S["kq_step"], c + 5)
                g.tensor_copy(kpart[:, t, :, 1, :], b).then_inc(S["kq_step"], 1)
                pool.wait_ge(S["kq_step"], c + 6)
                g.tensor_tensor(a, b, kpart[:, t, :, 1, :], ALU.subtract).then_inc(S["kq_step"], 1)
                pool.wait_ge(S["kq_step"], c + 7)
                g.tensor_copy(kpart[:, t, :, 2, :], a).then_inc(S["kq_step"], 1)
            if stages >= 2:
                pool.wait_ge(S["vrow_ready"], 1)
            rv = svrow[:, 2:4, :].rearrange("p k c -> p (k c)")
            for t in range(NT if stages >= 2 else 0):
                g.tensor_tensor(KV[:, t, D:2 * D], KV[:, t, D:2 * D], rv, ALU.mult).then_inc(S["vint_ready"], 1)
                pool.wait_ge(S["vint_ready"], 2 * t + 1)
                g.tensor_scalar(VI[:, t, :], KV[:, t, D:2 * D], ROUND, -ROUND, ALU.add, ALU.add).then_inc(S["vint_ready"], 1)
            if stages >= 4:
                norm_rstd(3)
            for s in range(NT if stages >= 4 else 0):
                pool.wait_ge(S["laggr_ready"], 2 * (s + 1))
                g.tensor_scalar(ve4[:, 2 * s:2 * s + 2], mv4[:, 2 * s:2 * s + 2, 1], EPS, None, ALU.add).then_inc(S["lveps"], 1)
                pool.wait_ge(S["lveps"], s + 1)
                g.tensor_tensor(rs4[:, 2 * s:2 * s + 2], ve4[:, 2 * s:2 * s + 2], neghalf[:, 0:2], ALU.pow).then_inc(S["lrstd_ready"], 1)
            if stages >= 5:
                norm_rstd(4)
            for t in range(NT if stages >= 5 else 0):
                pool.wait_ge(S["xn_ready"], 4 * NT + t + 1)
                g.tensor_tensor(X[:, t, :], X[:, t, :], bpr[:, :], ALU.add).then_inc(S["xbias_ready"], 1)
            if stages >= 5:
                pool.wait_ge(S["proj_psum"], 2 * NT)
                g.memset(A[:, 0:8192], 0.0).then_inc(S["pad5_ready"], 2)
                g.memset(A[:, 8192:16384], 0.0).then_inc(S["pad5_ready"], 2)
            if stages >= 6:
                norm_rstd(5)
                pool.wait_ge(S["idx_ready"], 1)
                pool.wait_ge(S["zero_rows"], 16 * (SLOTS // (4 * P) + 1))
                for j in range(NT * TOPK):
                    g.indirect_dma_start(out=slot_rows, out_offset=bass.IndirectOffsetOnAxis(ap=idx_put[:, j:j + 1], axis=0),
                                         in_=XN[:, j // TOPK, :], in_offset=None, bounds_check=SLOTS - 1,
                                         oob_is_err=False).then_inc(S["rows_put"], 16)
                for i in range(4):
                    pool.wait_ge(ye_stored[i], 16 * (NE // 4))
                for j in range(NT * TOPK):
                    if j >= YGN:
                        pool.wait_ge(S["x_ready"], 8 * 5 + j - YGN + 1)
                    g.indirect_dma_start(out=YG[:, j % YGN, :], out_offset=None, in_=y_rows[:, :],
                                         in_offset=bass.IndirectOffsetOnAxis(ap=idx_get[:, j:j + 1], axis=0),
                                         bounds_check=SLOTS + P - 1, oob_is_err=False).then_inc(yg_loaded[j % YGN], 16)

        @block.scalar
        def _(act):
            a = nc.scalar

            def copy_T(m, s, t):
                act.wait_ge(S["tp_psum"], m * NT + s + 1)
                a.activation(XT[:, :, t * P:(t + 1) * P], ps[:, s % 2, 0:D].rearrange("p (k c) -> p k c", k=KD), ACT.Copy).then_inc(S["tp_ready"], 1)

            for s in range(NT + 1):
                if s < NT:
                    copy_T(0, s, s)
                if s >= 1:
                    act.wait_ge(S["qkv_psum"], s)
                    a.activation(qkv[:, s - 1, :], ps[:, 2 + (s - 1) % 2, 0:384], ACT.Copy).then_inc(S["qkv_ready"], 1)
            for t in range(NT):
                act.wait_ge(S["kv_psum"], t + 1)
                a.activation(KV[:, t, :], ps[:, 4 + t % 2, :], ACT.Copy).then_inc(S["kv_copied"], 1)
            act.wait_ge(S["step1"], SUB_READY)
            a.activation(SC[:, :, :, :], SC[:, :, :, :], ACT.Exp, scale=0.25).then_inc(S["exp1_ready"], 1)
            for s in range(NT):
                copy_T(1, s, PARITY_ORDER[s])
            if stages >= 2:
                for i in range(NB):
                    act.wait_ge(S["bias2_ready"], i + 1)
                    if i >= 2:
                        act.wait_ge(S["out2_psum"], i - 1)
                    for e in range(2):
                        a.activation(E2[:, i % 2, e, :], ps[:, 2 + i % 2, e * D:(e + 1) * D], ACT.Exp, scale=1.0 / 16, bias=b2[:, i % 2, e:e + 1],
                                     accum_out=sum2[:, i % 2, e:e + 1]).then_inc(S["exp2_ready"], 1)
                act.wait_ge(S["vrow_psum"], 1)
                a.activation(svrow[:, :, :], ps[:, 7, :].rearrange("p (a c) -> p a c", a=4), ACT.Copy).then_inc(S["vrow_ready"], 1)
            if stages >= 3:
                for s in range(NT + 2):
                    if s < NT:
                        act.wait_ge(S["qxT_psum"], s + 1)
                        a.activation(QXT[:, s % 2, :, :], ps[:, s % 2, 0:P].bitcast(BF16).rearrange("p (k c) -> p k c", k=KD), ACT.Copy).then_inc(S["qxT_ready"], 1)
                    if 1 <= s <= NT:
                        u = s - 1
                        act.wait_ge(S["h3_psum"], u + 1)
                        if u >= 2:
                            act.wait_ge(S["qh_step"], 2 * (u - 1))
                        a.activation(G3[:, u % 2, :], ps[:, 2 + 2 * (u % 2):4 + 2 * (u % 2), :], ACT.Gelu_apprx_tanh,
                                     scale=dq3[:, u:u + 1]).then_inc(S["gelu_ready"], 1)
                    if s >= 2:
                        u = s - 2
                        act.wait_ge(S["qhT_psum"], u + 1)
                        a.activation(QHT[:, u % 2, :, :], ps[:, 6, :].bitcast(BF16).rearrange("p (k c) -> p k c", k=KF), ACT.Copy).then_inc(S["qhT_ready"], 1)
            if stages >= 4:
                for s in range(NT):
                    copy_T(2, s, s)
                for s in range(NT):
                    act.wait_ge(S["cnT_psum"], s + 1)
                    a.activation(CNT[:, s * P:(s + 1) * P], ps[:, s % 2, 0:P], ACT.Identity, scale=lng[:, 0:1], bias=lnb[:, 0:1]).then_inc(S["cnT_ready"], 1)
                for j in range(8):
                    act.wait_ge(S["up_psum"], 2 * j + 1)
                    a.activation(QT4[:, j % 4, (j // 4) * 512:(j // 4 + 1) * 512], ps[:, 2 + 2 * (j % 2), :], ACT.Copy).then_inc(S["upq_ready"], 1)
                for t in range(NT):
                    act.wait_ge(S["v4_psum"], t + 1)
                    a.activation(V4[:, t, :, 0:HD], ps[:, 6 + t % 2, 0:D].rearrange("p (h c) -> p h c", h=H), ACT.Copy).then_inc(S["v4_ready"], 1)
                for s in range(U4 + 1):
                    if s < U4:
                        act.wait_ge(S["sub4_ready"], 2 * (s + 1))
                        a.activation(E4[:, s % 2, :, :], E4[:, s % 2, :, :], ACT.Exp, scale=0.25).then_inc(S["exp4_ready"], 1)
                    if s >= 1:
                        u = s - 1
                        act.wait_ge(S["p4T_psum"], u + 1)
                        if u >= 2:
                            act.wait_ge(S["o4_psum"], u - 1)
                        a.activation(PT4[:, u % 2, :, :], ps[:, 4:6, 0:384], ACT.Copy).then_inc(S["p4T_ready"], 1)
                for s in range(NT):
                    copy_T(3, s, s)
            if stages >= 5:
                for s in range(NT):
                    copy_T(4, s, s)
                act.wait_ge(S["pad5_ready"], 4)
                for h in range(H):
                    act.wait_ge(S["k5T_psum"], h + 1)
                    a.activation(KT5[0:48, h, :], ps[0:48, 4 + h % 2, :].bitcast(BF16), ACT.Copy).then_inc(S["k5T_ready"], 1)

                def exps(h, first):
                    for q in range(NT):
                        n = h * NT + q
                        act.wait_ge(S["bias5_ready"], n + 1)
                        if not (first and q < 2):
                            act.wait_ge(S["pi5_ready"], n - 1)
                        a.activation(Y5[:, q % 2, :], ps[:, 2 * (q % 2):2 * (q % 2) + 2, :], ACT.Exp, scale=sq5[:, q, bass.ds(h, 1)],
                                     bias=b5[:, q % 4:q % 4 + 1], accum_out=sum5[:, bass.ds(h * NT + q, 1)]).then_inc(S["exp5_ready"], 1)

                exps(0, True)
                with a.Fori(1, H) as h:
                    exps(h, False)
                for s in range(NT):
                    copy_T(5, s, s)
            if stages >= 6:
                for s in range(NT):
                    copy_T(6, s, s)
                act.wait_ge(S["step6"], 2)
                a.activation(L6[:, :, :], L6[:, :, :], ACT.Exp).then_inc(S["exp6_ready"], 1)
                for s in range(NE + 1):
                    if s < NE:
                        act.wait_ge(S["xeT_psum"], s + 1)
                        if s >= 2:
                            act.wait_ge(S["gu_psum"], s - 1)
                        a.activation(XET[:, s % 2, :, :], ps[:, s % 2, 0:D].rearrange("p (k c) -> p k c", k=KD), ACT.Copy).then_inc(S["xeT_ready"], 1)
                    if s >= 1:
                        e = s - 1
                        act.wait_ge(S["gu_psum"], e + 1)
                        if e >= 2:
                            act.wait_ge(S["he_ready"], e - 1)
                        a.activation(SG[:, e % 2, :], ps[:, 2 + e % 2, 0:CAP], ACT.Silu).then_inc(S["silu_ready"], 1)

        @block.tensor
        def _(pe):
            T = nc.tensor
            pe.wait_ge(S["const_ready"], 13)

            def to_T(m, s, src, ready, count):
                c = m * NT + s + 1
                pe.wait_ge(ready, count)
                if c > 2:
                    pe.wait_ge(S["tp_ready"], c - 2)
                for k in range(KD):
                    last = T.transpose(ps[:, s % 2, k * P:(k + 1) * P], src[:, k * P:(k + 1) * P], identf[:, :])
                last.then_inc(S["tp_psum"], 1)

            def project(m, s, t, bank, w, n, done, free, free_count):
                pe.wait_ge(S["tp_ready"], m * NT + s + 1)
                if free is not None and free_count > 0:
                    pe.wait_ge(free, free_count)
                for k in range(KD):
                    last = T.matmul(ps[:, bank, 0:n], XT[:, k, t * P:(t + 1) * P], w[:, k, 0:n], start=(k == 0), stop=(k == KD - 1))
                last.then_inc(done, 1)

            for s in range(NT + 1):
                if s < NT:
                    to_T(0, s, XN[:, s, :], S["xn_ready"], s + 1)
                if s >= 1:
                    if s == 1:
                        pe.wait_ge(S["w0_loaded"], 32)
                    project(0, s - 1, s - 1, 2 + (s - 1) % 2, wqkvT, 384, S["qkv_psum"], S["qkv_ready"], s - 2)
            pe.wait_ge(S["ctx_loaded"], 64)
            for t in range(NT):
                if t >= 2:
                    pe.wait_ge(S["kv_copied"], t - 1)
                for k in range(KD):
                    last = T.matmul(ps[:, 4 + t % 2, :], ctxT[:, k, t * P:(t + 1) * P], wkv5[:, k, :], start=(k == 0), stop=(k == KD - 1))
                last.then_inc(S["kv_psum"], 1)
            pe.wait_ge(S["wabs_ready"], 2)
            T.matmul(ps[:, 6, 0:2], onesf[:, :], wsum[:, :], start=True, stop=True).then_inc(S["wtot_psum"], 1)
            for s in range(NT + 1):
                if s < NT:
                    to_T(1, s, AT[:, PARITY_ORDER[s], :], S["at_ready"], s + 1)
                if s >= 1:
                    project(1, s - 1, PARITY_ORDER[s - 1], 2 + (s - 1) % 2, wprojT, D, S["proj_psum"], S["x_ready"], s - 2)
            if stages >= 2:
                for s in range(NB + 1):
                    if s < NB:
                        pe.wait_ge(S["xn_ready"], NT + 4 + s + 1)
                        pe.wait_ge(S["x_ready"], NT)
                        if s >= 2:
                            pe.wait_ge(S["exp2_ready"], 2 * (s - 1))
                        for e in range(2):
                            for j in range(2):
                                last = T.matmul(ps[:, 2 + s % 2, e * D:(e + 1) * D], ctx_sb[:, 2 * s + j, e * P:(e + 1) * P], XN[:, 2 * s + j, :], start=(j == 0), stop=(j == 1))
                        last.then_inc(S["s2_psum"], 1)
                    if s >= 1:
                        i = s - 1
                        pe.wait_ge(S["attn2_ready"], 2 * (i + 1))
                        if i >= 2:
                            pe.wait_ge(S["x_ready"], NT + 2 * (i - 1))
                        for j in range(2):
                            for e in range(2):
                                last = T.matmul(ps[:, 4 + i % 2, j * D:(j + 1) * D], ctxT[:, e, i * SEQ + j * P:i * SEQ + (j + 1) * P], E2[:, i % 2, e, :], start=(e == 0), stop=(e == 1))
                        last.then_inc(S["out2_psum"], 1)
                pe.wait_ge(S["vmax_ready"], 1)
                for k in range(KD):
                    last = T.transpose(ps[:, 6, k * P:(k + 1) * P], vmax[:, k * P:(k + 1) * P], identf[:, :])
                last.then_inc(S["vmaxT_psum"], 1)
                pe.wait_ge(S["vscale_ready"], 4)
                for a in range(2):
                    for k in range(KD):
                        last = T.matmul(ps[:, 7, (a * KD + k) * P:(a * KD + k + 1) * P], svb[:, a * KD + k, :], identf[:, :], start=True, stop=True)
                last.then_inc(S["vrow_psum"], 1)
            if stages >= 3:
                pe.wait_ge(S["w_ternary"], 1)
                for s in range(NT + 2):
                    if s < NT:
                        pe.wait_ge(S["qx_ready"], s + 1)
                        if s >= 2:
                            pe.wait_ge(S["qxT_ready"], s - 1)
                        for k in range(KD):
                            last = T.transpose(ps[:, s % 2, k * 64:(k + 1) * 64].bitcast(BF16), QX[:, s, k * P:(k + 1) * P], identb[:, :])
                        last.then_inc(S["qxT_psum"], 1)
                        pe.wait_ge(S["qxT_ready"], s + 1)
                        if s >= 2:
                            pe.wait_ge(S["gelu_ready"], s - 1)
                        elif s == 0:
                            pe.wait_ge(S["x_ready"], 2 * NT)
                        for n in range(2):
                            for k in range(KD):
                                last = T.matmul(ps[:, 2 + 2 * (s % 2) + n, :], QXT[:, s % 2, k, :], w1t[:, k, n * 512:(n + 1) * 512], start=(k == 0), stop=(k == KD - 1))
                        last.then_inc(S["h3_psum"], 1)
                    if s >= 2:
                        u = s - 2
                        pe.wait_ge(S["qh_ready"], u + 1)
                        if u >= 1:
                            pe.wait_ge(S["qhT_ready"], u)
                        for k in range(KF):
                            last = T.transpose(ps[:, 6, k * 64:(k + 1) * 64].bitcast(BF16), QH[:, u % 2, k * P:(k + 1) * P], identb[:, :])
                        last.then_inc(S["qhT_psum"], 1)
                        pe.wait_ge(S["qhT_ready"], u + 1)
                        if u >= 1:
                            pe.wait_ge(S["x_ready"], 2 * NT + u)
                        for k in range(KF):
                            last = T.matmul(ps[:, 7, 0:D], QHT[:, u % 2, k, :], w2t[:, k, :], start=(k == 0), stop=(k == KF - 1))
                        last.then_inc(S["out3_psum"], 1)
            if stages >= 4:
                pe.wait_ge(S["low_loaded"], 16 * 9)
                for s in range(NT + 1):
                    if s < NT:
                        to_T(2, s, XN[:, s, :], S["xn_ready"], 3 * NT + s + 1)
                    if s >= 1:
                        project(2, s - 1, s - 1, 2 + (s - 1) % 2, wdown2, 2 * LOW, S["low_psum"], S["cn_ready"], 2 * (s - 2))
                for s in range(NT):
                    pe.wait_ge(S["cn_ready"], 2 * (s + 1))
                    if s >= 2:
                        pe.wait_ge(S["cnT_ready"], s - 1)
                    T.transpose(ps[:, s % 2, 0:P], CN[:, s, :], identf[:, :]).then_inc(S["cnT_psum"], 1)
                for j in range(8):
                    half, g = j // 4, j % 4
                    if j in (0, 4):
                        pe.wait_ge(S["cnT_ready"], 4 * (half + 1))
                    if j == 0:
                        pe.wait_ge(S["cn_ready"], 2 * NT)
                    for side, ready in ((0, "upq_ready"), (1, "upk_ready")):
                        if j >= 2:
                            pe.wait_ge(S[ready], j - 1)
                        rows = slice(side * LOW, (side + 1) * LOW)
                        T.matmul(ps[:, 2 + 2 * (j % 2) + side, :], wup[rows, g, :, :].rearrange("p r c -> p (r c)"), CNT[rows, half * 512:(half + 1) * 512],
                                 start=True, stop=True).then_inc(S["up_psum"], 1)
                for t in range(NT):
                    if t >= 2:
                        pe.wait_ge(S["v4_ready"], t - 1)
                    T.matmul(ps[:, 6 + t % 2, 0:D], CNT[LOW:P, t * P:(t + 1) * P], wuv[LOW:P, :], start=True, stop=True).then_inc(S["v4_psum"], 1)
                for s in range(U4 + 2):
                    if s < U4:
                        b, hp = s // 8, s % 8
                        if s == 0:
                            pe.wait_ge(S["upq_ready"], 8)
                            pe.wait_ge(S["upk_ready"], 8)
                            pe.wait_ge(S["v4_ready"], NT)
                        if s >= 2:
                            pe.wait_ge(S["sub4_ready"], 2 * (s - 1))
                        for j in range(2):
                            hh = 2 * hp + j
                            g, r = hh // 4, 32 * (hh % 4)
                            bank = 2 * (s % 2) + j
                            q = QT4[r:r + HD, g, b * SEQ:(b + 1) * SEQ]
                            k = KT4[r:r + HD, g, b * SEQ:(b + 1) * SEQ]
                            T.matmul(ps[:, bank, 0:P], q[:, 0:P], k[:, 0:P], start=True, stop=False)
                            T.matmul(ps[:, bank, 0:P], identb[:, :], causal[:, :], start=False, stop=True)
                            T.matmul(ps[:, bank, P:3 * P], q[:, P:2 * P], k[:, :], start=True, stop=False)
                            last = T.matmul(ps[:, bank, 2 * P:3 * P], identb[:, :], causal[:, :], start=False, stop=True)
                        last.then_inc(S["s4_psum"], 1)
                    if 1 <= s <= U4:
                        u = s - 1
                        pe.wait_ge(S["exp4_ready"], u + 1)
                        if u >= 1:
                            pe.wait_ge(S["p4T_ready"], u)
                        for j in range(2):
                            for m in range(3):
                                last = T.transpose(ps[:, 4 + j, m * P:(m + 1) * P], E4[:, u % 2, j, m * P:(m + 1) * P], identf[:, :])
                        last.then_inc(S["p4T_psum"], 1)
                    if s >= 2:
                        u = s - 2
                        b, hp = u // 8, u % 8
                        pe.wait_ge(S["p4T_ready"], u + 1)
                        if u >= 2:
                            pe.wait_ge(S["o4_ready"], u - 1)
                        for j in range(2):
                            hh = 2 * hp + j
                            o0 = ps[:, 6 + u % 2, (2 * j) * 17:(2 * j + 1) * 17]
                            o1 = ps[:, 6 + u % 2, (2 * j + 1) * 17:(2 * j + 2) * 17]
                            p = PT4[:, u % 2, j, :]
                            T.matmul(o0, p[:, 0:P], V4[:, 2 * b, hh, :], start=True, stop=True)
                            T.matmul(o1, p[:, P:2 * P], V4[:, 2 * b, hh, :], start=True, stop=False)
                            last = T.matmul(o1, p[:, 2 * P:3 * P], V4[:, 2 * b + 1, hh, :], start=False, stop=True)
                        last.then_inc(S["o4_psum"], 1)
                pe.wait_ge(S["w_loaded"], 16 * 7)
                for s in range(NT + 1):
                    if s < NT:
                        to_T(3, s, AT[:, s, :], S["o4_ready"], 8 * (s // 2 + 1))
                    if s >= 1:
                        project(3, s - 1, s - 1, 2 + (s - 1) % 2, woT, D, S["proj_psum"], S["x_ready"], 3 * NT + s - 2)
            if stages >= 5:
                for s in range(NT + 1):
                    if s < NT:
                        to_T(4, s, XN[:, s, :], S["xn_ready"], 4 * NT + s + 1)
                    if s >= 1:
                        project(4, s - 1, s - 1, 2 + (s - 1) % 2, wq5, D, S["q5_psum"], S["uq5_ready"], s - 2)
                pe.wait_ge(S["kq_step"], 8 * NT)
                for h in range(H):
                    if h >= 2:
                        pe.wait_ge(S["k5T_ready"], h - 1)
                    for t in range(NT):
                        last = T.transpose(ps[0:48, 4 + h % 2, t * 64:(t + 1) * 64].bitcast(BF16), kpart[:, t, h, :, :].rearrange("p a c -> p (a c)"), identb[:, :])
                    last.then_inc(S["k5T_psum"], 1)
                pe.wait_ge(S["q5i_ready"], 3)
                for h in range(H):
                    if h >= 2:
                        pe.wait_ge(S["q5T_ready"], h - 1)
                    for t in range(NT):
                        last = T.transpose(ps[0:48, 6 + h % 2, t * 64:(t + 1) * 64].bitcast(BF16), QI3[:, t, h, :, :].rearrange("p a c -> p (a c)"), identb[:, :])
                    last.then_inc(S["q5T_psum"], 1)
                pe.wait_ge(S["q5T_ready"], H)
                pe.wait_ge(S["k5T_ready"], H)
                pe.wait_ge(S["vint_ready"], 2 * NT)

                def heads(h, first):
                    for q in range(NT):
                        n = h * NT + q
                        if not (first and q < 2):
                            pe.wait_ge(S["exp5_ready"], n - 1)
                        for c in range(2):
                            last = T.matmul(ps[:, 2 * (q % 2) + c, :], QT5[:, h, q * P:(q + 1) * P], KT5[:, h, c * 512:(c + 1) * 512], start=True, stop=True)
                        last.then_inc(S["s5_psum"], 1)
                        if not (first and q < 1):
                            transposes(n - 1, (q - 1) % 2, first and q < 3)
                        if q >= 2:
                            values(n - 2, q - 2, h, first and q == 2)
                        elif not first:
                            values(n - 2, q + 6, h - 1, False)

                def transposes(n, b, fresh):
                    pe.wait_ge(S["pi5_ready"], n + 1)
                    if not fresh:
                        pe.wait_ge(S["p5T_ready"], n - 1)
                    for k in range(8):
                        last = T.transpose(ps[:, 4 + b, k * 64:(k + 1) * 64].bitcast(BF16), PI5[:, b, k * P:(k + 1) * P], identb[:, :])
                    last.then_inc(S["p5T_psum"], 1)

                def values(n, q, h, fresh):
                    pe.wait_ge(S["p5T_ready"], n + 1)
                    if q == 0 and not fresh:
                        pe.wait_ge(S["o5_ready"], h)
                    for k in range(8):
                        last = T.matmul(ps[:, 6, q * HD:(q + 1) * HD], PT5[:, q % 2, k, :], VI[:, k, bass.ds(h * HD, HD)], start=(k == 0), stop=(k == 7))
                    last.then_inc(S["p5V_done"], 1)
                    if q == NT - 1:
                        pass

                heads(0, True)
                with T.Fori(1, H) as h:
                    heads(h, False)
                transposes(H * NT - 1, 1, False)
                values(H * NT - 2, 6, H - 1, False)
                values(H * NT - 1, 7, H - 1, False)
                pe.wait_ge(S["p5V_done"], H * NT)
                pe.sem_inc(S["o5_psum"], H)
                for s in range(NT + 1):
                    if s < NT:
                        to_T(5, s, AT[:, s, :], S["out5_ready"], 1)
                    if s >= 1:
                        project(5, s - 1, s - 1, 2 + (s - 1) % 2, wp5, D, S["proj_psum"], S["x_ready"], 4 * NT + s - 2)
            if stages >= 6:
                for s in range(NT + 1):
                    if s < NT:
                        to_T(6, s, XN[:, s, :], S["xn_ready"], 5 * NT + s + 1)
                    if s >= 1:
                        if s == 1:
                            pe.wait_ge(S["x_ready"], 5 * NT)
                        t = s - 1
                        pe.wait_ge(S["tp_ready"], 6 * NT + s)
                        for k in range(KD):
                            last = T.matmul(ps[:, 2, t * NROUTE:(t + 1) * NROUTE], XT[:, k, t * P:(t + 1) * P], wclsT[:, k, :], start=(k == 0), stop=(k == KD - 1))
                last.then_inc(S["lg_psum"], 1)
                pe.wait_ge(S["cnt6_ready"], 1)
                T.matmul(ps[:, 3, 0:NT * NE], lower[:, :], mr6[:, :, :].rearrange("p t e -> p (t e)"), start=True, stop=False)
                T.matmul(ps[:, 3, 0:NT * NE], onesb[:, :], cum6[:, :, :].rearrange("p t e -> p (t e)"), start=False, stop=True).then_inc(S["pos6_psum"], 1)
                pe.wait_ge(S["idx_ready"], 1)
                for s in range(NE + 2):
                    if s < NE:
                        pe.wait_ge(xe_loaded[s % 4], 16 * (s // 4 + 1))
                        if s >= 2:
                            pe.wait_ge(S["xeT_ready"], s - 1)
                        for k in range(KD):
                            last = T.transpose(ps[:, s % 2, k * P:(k + 1) * P], XE[:, s % 4, k * P:(k + 1) * P], identf[:, :])
                        last.then_inc(S["xeT_psum"], 1)
                    if 1 <= s <= NE:
                        e = s - 1
                        pe.wait_ge(wg_loaded[e % 8], 32 * (e // 8 + 1))
                        pe.wait_ge(S["xeT_ready"], e + 1)
                        if e >= 2:
                            pe.wait_ge(S["he_ready"], e - 1)
                        for f in range(2):
                            for k in range(KD):
                                last = T.matmul(ps[:, 2 + e % 2, f * P:(f + 1) * P], WG[:, e % 8, k, f * P:(f + 1) * P], XET[:, e % 2, k, :], start=(k == 0), stop=(k == KD - 1))
                        last.then_inc(S["gu_psum"], 1)
                    if s >= 2:
                        e = s - 2
                        pe.wait_ge(S["he_ready"], e + 1)
                        if e >= 2:
                            pe.wait_ge(S["ye_ready"], e - 1)
                        T.matmul(ps[:, 4 + e % 2, 0:D], HE[:, e % 2, :], WD[:, e % 8, :], start=True, stop=True).then_inc(S["ye_psum"], 1)

        @block.vector
        def _(dve):
            v = nc.vector
            dve.wait_ge(S["const_ready"], 13)

            def norm(n, count0):
                order = PARITY_ORDER if n == 1 else IN_ORDER
                for s in range(NT):
                    if n == 0:
                        dve.wait_ge(S["x_loaded"], 16)
                    else:
                        dve.wait_ge(S["x_ready"], count0 + s + 1)
                    v.bn_stats(stats[:, order[s], :], X[:, order[s], :]).then_inc(S["stats_ready"], 1)
                for s in range(NT):
                    dve.wait_ge(S["stats_ready"], n * NT + s + 1)
                    v.bn_aggr(mv[:, order[s], :], stats[:, order[s], :]).then_inc(S["aggr_ready"], 1)
                for s in range(NT):
                    t = order[s]
                    dve.wait_ge(S["rstd_ready"], n * NT + s + 1)
                    v.tensor_scalar(XN[:, t, :], X[:, t, :], mv[:, t, 0:1], rstd[:, t:t + 1], ALU.subtract, ALU.mult).then_inc(S["xn_ready"], 1)

            def residual(s, t, bank, done, count):
                dve.wait_ge(done, count)
                v.tensor_tensor(X[:, t, :], X[:, t, :], ps[:, bank, 0:D], ALU.add).then_inc(S["x_ready"], 1)

            norm(0, 0)
            dve.wait_ge(S["w1_loaded"], 16)
            v.tensor_reduce(wsum[:, 0:1], w1stage.rearrange("p k c -> p (k c)"), AX.X, ALU.add, apply_absolute_value=True).then_inc(S["wabs_ready"], 1)
            dve.wait_ge(S["w2_loaded"], 16)
            v.tensor_reduce(wsum[:, 1:2], w2stage.rearrange("p k c -> p (k c)"), AX.X, ALU.add, apply_absolute_value=True).then_inc(S["wabs_ready"], 1)
            dve.wait_ge(S["qkv_ready"], NT)
            score_products(dve, v, 0, S["prod0_ready"])
            for j in range(2):
                for iq in range(4):
                    off = iq * (iq + 1) // 2
                    dve.wait_ge(S[f"prod{j}_ready"], off + iq + 1)
                    v.tensor_reduce(SC[:, j * 4 + iq, 0:iq + 1, :], prod[j][:, off:off + iq + 1, :].rearrange("p s (h d) -> p (s h) d", d=HD),
                                    AX.X, ALU.add).then_inc(S["step1"], 1)
            dve.wait_ge(S["step1"], 8)
            v.tensor_reduce(mx1[:, :, :], SC[:, :, :, :].rearrange("p a k h -> p a h k"), AX.X, ALU.max).then_inc(S["step1"], 1)
            dve.wait_ge(S["step1"], 9)
            v.tensor_tensor(SC[:, :, :, :], SC[:, :, :, :], mx1[:, :, :].unsqueeze(2).to_broadcast([P, 8, 4, H]), ALU.subtract).then_inc(S["step1"], 1)
            dve.wait_ge(S["wtot_psum"], 1)
            v.tensor_scalar(wmean[:, :], ps[:, 6, 0:2], 1.0 / (FF * D), EPS, ALU.mult, ALU.max).then_inc(S["wscale_ready"], 1)
            dve.wait_ge(S["wscale_ready"], 1)
            v.reciprocal(wrec[:, :], wmean[:, :]).then_inc(S["wscale_ready"], 1)
            v.tensor_scalar(w127[:, :], wmean[:, :], 1.0 / 127, None, ALU.mult).then_inc(S["wscale_ready"], 1)
            dve.wait_ge(S["exp1_ready"], 1)
            v.tensor_reduce(rs1[:, :, :], SC[:, :, :, :].rearrange("p a k h -> p a h k"), AX.X, ALU.add).then_inc(S["step1"], 1)
            dve.wait_ge(S["step1"], 11)
            v.reciprocal(rs1[:, :, :], rs1[:, :, :]).then_inc(S["step1"], 1)
            dve.wait_ge(S["step1"], 12)
            v.tensor_tensor(SC[:, :, :, :], SC[:, :, :, :], rs1[:, :, :].unsqueeze(2).to_broadcast([P, 8, 4, H]), ALU.mult).then_inc(S["step1"], 1)
            dve.wait_ge(S["step1"], 13)
            value_products(dve, v, 0, S["prod0_ready"])
            for j in range(2):
                for iq in range(4):
                    off = iq * (iq + 1) // 2
                    dve.wait_ge(S[f"prod{j}_ready"], 10 + off + iq + 1)
                    v.tensor_reduce(AT[:, 2 * iq + j, :], prod[j][:, off:off + iq + 1, :].rearrange("p s c -> p c s"),
                                    AX.X, ALU.add).then_inc(S["at_ready"], 1)
            for s in range(NT):
                residual(s, PARITY_ORDER[s], 2 + s % 2, S["proj_psum"], s + 1)
            if stages >= 2:
                norm(1, 0)
                for s in range(NB + 1):
                    if s < NB:
                        dve.wait_ge(S["s2_psum"], s + 1)
                        v.tensor_reduce(nm2[:, s % 2, :], ps[:, 2 + s % 2, :].rearrange("p (e c) -> p e c", e=2), AX.X, ALU.max, negate=True).then_inc(S["nm2_ready"], 1)
                        dve.wait_ge(S["nm2_ready"], s + 1)
                        v.tensor_scalar(b2[:, s % 2, :], nm2[:, s % 2, :], 1.0 / 16, None, ALU.mult).then_inc(S["bias2_ready"], 1)
                    if s >= 1:
                        i = s - 1
                        dve.wait_ge(S["exp2_ready"], 2 * (i + 1))
                        v.reciprocal(r2[:, i % 2, :], sum2[:, i % 2, :]).then_inc(S["r2_ready"], 1)
                        dve.wait_ge(S["r2_ready"], i + 1)
                        for e in range(2):
                            v.tensor_scalar(E2[:, i % 2, e, :], E2[:, i % 2, e, :], r2[:, i % 2, e:e + 1], None, ALU.mult).then_inc(S["attn2_ready"], 1)
                        dve.wait_ge(S["out2_psum"], i + 1)
                        for j in range(2):
                            v.tensor_tensor(X[:, 2 * i + j, :], X[:, 2 * i + j, :], ps[:, 4 + i % 2, j * D:(j + 1) * D], ALU.add).then_inc(S["x_ready"], 1)
                dve.wait_ge(S["kv_ready"], NT)
                v.tensor_reduce(kmax[:, :, :], KV[:, :, 0:D].rearrange("p t (h d) -> p t h d", h=H), AX.X, ALU.max, apply_absolute_value=True).then_inc(S["kscale_ready"], 1)
                dve.wait_ge(S["kscale_ready"], 1)
                v.tensor_scalar(sk[:, :, :], kmax[:, :, :], 1.0 / 127, 1e-8, ALU.mult, ALU.max).then_inc(S["kscale_ready"], 1)
                dve.wait_ge(S["kscale_ready"], 2)
                v.reciprocal(rk[:, :, :], sk[:, :, :]).then_inc(S["kscale_ready"], 1)
                v.tensor_reduce(vmax[:, :], KV[:, :, D:2 * D].rearrange("p t c -> p c t"), AX.X, ALU.max, apply_absolute_value=True).then_inc(S["vmax_ready"], 1)
                dve.wait_ge(S["vmaxT_psum"], 1)
                v.tensor_reduce(vm2[:, :], ps[:, 6, 0:D].rearrange("p (k c) -> p k c", k=KD), AX.X, ALU.max).then_inc(S["vscale_ready"], 1)
                dve.wait_ge(S["vscale_ready"], 1)
                v.tensor_scalar(svrv[:, 0, :], vm2[:, :], 1.0 / 127, 1e-8, ALU.mult, ALU.max).then_inc(S["vscale_ready"], 1)
                dve.wait_ge(S["vscale_ready"], 2)
                v.reciprocal(svrv[:, 1, :], svrv[:, 0, :]).then_inc(S["vscale_ready"], 1)
                dve.wait_ge(S["vscale_ready"], 3)
                v.tensor_copy(svb[:, :, :], svrv[:, :, :].rearrange("p a k -> p (a k)").unsqueeze(2).to_broadcast([P, 4, P])).then_inc(S["vscale_ready"], 1)
            if stages >= 3:
                norm(2, NT)
                dve.wait_ge(S["xn_ready"], 3 * NT)
                v.tensor_reduce(am3[:, :], XN[:, :, :], AX.X, ALU.max, apply_absolute_value=True).then_inc(S["dq3_step"], 1)
                dve.wait_ge(S["dq3_step"], 1)
                v.tensor_scalar(am3[:, :], am3[:, :], EPS, None, ALU.max).then_inc(S["dq3_step"], 1)
                dve.wait_ge(S["dq3_step"], 2)
                v.reciprocal(qs3[:, :], am3[:, :]).then_inc(S["dq3_step"], 1)
                v.tensor_scalar(dq3[:, :], am3[:, :], w127[:, 0:1], None, ALU.mult).then_inc(S["dq3_step"], 1)
                dve.wait_ge(S["dq3_step"], 3)
                v.tensor_scalar(qs3[:, :], qs3[:, :], 127.0, None, ALU.mult).then_inc(S["dq3_step"], 1)
                dve.wait_ge(S["dq3_step"], 5)
                for s in range(NT):
                    v.tensor_scalar(XN[:, s, :], XN[:, s, :], qs3[:, s:s + 1], ROUND, ALU.mult, ALU.add).then_inc(S["qx_step"], 1)
                for s in range(NT):
                    dve.wait_ge(S["qx_step"], s + 1)
                    v.tensor_scalar(QX[:, s, :], XN[:, s, :], -ROUND, None, ALU.add).then_inc(S["qx_ready"], 1)
                for s in range(NT + 1):
                    if s < NT:
                        dve.wait_ge(S["gelu_ready"], s + 1)
                        g3 = G3[:, s % 2, :]
                        v.tensor_reduce(am3b[:, s:s + 1], g3, AX.X, ALU.max, apply_absolute_value=True).then_inc(S["am3_step"], 1)
                        dve.wait_ge(S["am3_step"], 5 * s + 1)
                        v.tensor_scalar(am3b[:, s:s + 1], am3b[:, s:s + 1], EPS, None, ALU.max).then_inc(S["am3_step"], 1)
                        dve.wait_ge(S["am3_step"], 5 * s + 2)
                        v.reciprocal(qs3b[:, s:s + 1], am3b[:, s:s + 1]).then_inc(S["am3_step"], 1)
                        dve.wait_ge(S["am3_step"], 5 * s + 3)
                        v.tensor_scalar(qs3b[:, s:s + 1], qs3b[:, s:s + 1], 127.0, None, ALU.mult).then_inc(S["am3_step"], 1)
                        v.tensor_scalar(dq3b[:, s:s + 1], am3b[:, s:s + 1], w127[:, 1:2], None, ALU.mult).then_inc(S["am3_step"], 1)
                        dve.wait_ge(S["am3_step"], 5 * s + 4)
                        v.tensor_scalar(g3, g3, qs3b[:, s:s + 1], ROUND, ALU.mult, ALU.add).then_inc(S["qh_step"], 1)
                        dve.wait_ge(S["qh_step"], 2 * s + 1)
                        if s >= 2:
                            dve.wait_ge(S["qhT_psum"], s - 1)
                        v.tensor_scalar(QH[:, s % 2, :], g3, -ROUND, None, ALU.add).then_inc(S["qh_step"], 1)
                        dve.wait_ge(S["qh_step"], 2 * s + 2)
                        dve.sem_inc(S["qh_ready"], 1)
                    if s >= 1:
                        u = s - 1
                        dve.wait_ge(S["out3_psum"], u + 1)
                        v.scalar_tensor_tensor(X[:, u, :], ps[:, 7, 0:D], dq3b[:, u:u + 1], X[:, u, :], ALU.mult, ALU.add).then_inc(S["x_ready"], 1)
            if stages >= 4:
                norm(3, 2 * NT)
                for s in range(NT):
                    dve.wait_ge(S["low_psum"], s + 1)
                    for k in range(2):
                        v.bn_stats(st4[:, 2 * s + k, :], ps[:, 2 + s % 2, k * LOW:(k + 1) * LOW]).then_inc(S["lstats_ready"], 1)
                    for k in range(2):
                        dve.wait_ge(S["lstats_ready"], 2 * s + k + 1)
                        v.bn_aggr(mv4[:, 2 * s + k, :], st4[:, 2 * s + k, :]).then_inc(S["laggr_ready"], 1)
                    dve.wait_ge(S["lrstd_ready"], s + 1)
                    for k in range(2):
                        c = 2 * s + k
                        v.tensor_scalar(CN[:, s, k * LOW:(k + 1) * LOW], ps[:, 2 + s % 2, k * LOW:(k + 1) * LOW], mv4[:, c, 0:1], rs4[:, c:c + 1],
                                        ALU.subtract, ALU.mult).then_inc(S["cn_ready"], 1)
                for j in range(8):
                    dve.wait_ge(S["up_psum"], 2 * j + 2)
                    v.tensor_copy(KT4[:, j % 4, (j // 4) * 512:(j // 4 + 1) * 512], ps[:, 3 + 2 * (j % 2), :]).then_inc(S["upk_ready"], 1)
                v.memset(V4[:, :, :, HD:HD + 1], 1.0).then_inc(S["upk_ready"], 1)
                for s in range(U4 + 2):
                    if s < U4:
                        dve.wait_ge(S["s4_psum"], s + 1)
                        sc = ps[:, 2 * (s % 2):2 * (s % 2) + 2, :]
                        v.tensor_reduce(m4[:, s % 2, 0, :], sc[:, :, 0:P], AX.X, ALU.max).then_inc(S["max4_ready"], 1)
                        v.tensor_reduce(m4[:, s % 2, 1, :], sc[:, :, P:3 * P], AX.X, ALU.max).then_inc(S["max4_ready"], 1)
                        if s >= 2:
                            dve.wait_ge(S["p4T_psum"], s - 1)
                        for q, (lo, hi) in enumerate(((0, P), (P, 3 * P))):
                            dve.wait_ge(S["max4_ready"], 2 * s + q + 1)
                            v.tensor_tensor(E4[:, s % 2, :, lo:hi], sc[:, :, lo:hi], m4[:, s % 2, q, :].unsqueeze(2).to_broadcast([P, 2, hi - lo]),
                                            ALU.subtract).then_inc(S["sub4_ready"], 1)
                    if s >= 2:
                        u = s - 2
                        b, hp = u // 8, u % 8
                        dve.wait_ge(S["o4_psum"], u + 1)
                        o = ps[:, 6 + u % 2, 0:68].rearrange("p (a c) -> p a c", c=17)
                        v.reciprocal(r4[:, u % 2, :], o[:, :, 16]).then_inc(S["r4_ready"], 1)
                        dve.wait_ge(S["r4_ready"], u + 1)
                        v.tensor_tensor(AT[:, 2 * b:2 * b + 2, 2 * hp * HD:(2 * hp + 2) * HD].rearrange("p t (j c) -> p j t c", c=HD),
                                        o[:, :, 0:HD].rearrange("p (j t) c -> p j t c", t=2),
                                        r4[:, u % 2, :].rearrange("p (j t) -> p j t", t=2).unsqueeze(3).to_broadcast([P, 2, 2, HD]), ALU.mult).then_inc(S["o4_ready"], 1)
                for s in range(NT):
                    residual(s, s, 2 + s % 2, S["proj_psum"], NT + s + 1)
            if stages >= 5:
                norm(4, 3 * NT)
                for s in range(NT):
                    dve.wait_ge(S["q5_psum"], s + 1)
                    v.tensor_tensor(AT[:, s, :], ps[:, 2 + s % 2, 0:D], bqr[:, :], ALU.add).then_inc(S["uq5_ready"], 1)
                dve.wait_ge(S["uq5_ready"], NT)
                heads_view = AT[:, :, :].rearrange("p t (h d) -> p (t h) d", d=HD)
                v.tensor_reduce(sq5[:, :, :].rearrange("p t h -> p (t h)"), heads_view, AX.X, ALU.max, apply_absolute_value=True).then_inc(S["q5_step"], 1)
                dve.wait_ge(S["q5_step"], 1)
                v.tensor_scalar(sq5[:, :, :], sq5[:, :, :], 0.25 / 127, 1e-8, ALU.mult, ALU.max).then_inc(S["q5_step"], 1)
                dve.wait_ge(S["q5_step"], 2)
                v.reciprocal(rq5[:, :, :], sq5[:, :, :]).then_inc(S["q5_step"], 1)
                dve.wait_ge(S["q5_step"], 3)
                v.tensor_scalar(rq5[:, :, :], rq5[:, :, :], 0.25, None, ALU.mult).then_inc(S["q5_step"], 1)
                dve.wait_ge(S["q5_step"], 4)
                v.tensor_tensor(heads_view, heads_view, rq5[:, :, :].rearrange("p t h -> p (t h)").unsqueeze(2).to_broadcast([P, NT * H, HD]), ALU.mult).then_inc(S["q5_step"], 1)
                dve.wait_ge(S["q5_step"], 5)
                dve.wait_ge(S["k5T_psum"], H)
                for a in range(3):
                    v.tensor_scalar(QI3[:, :, :, a, :].rearrange("p t h d -> p (t h) d"), heads_view, ROUND, -ROUND, ALU.add, ALU.add).then_inc(S["q5i_ready"], 1)
                dve.wait_ge(S["pad5_ready"], 4)
                for h in range(H):
                    dve.wait_ge(S["q5T_psum"], h + 1)
                    v.tensor_copy(QT5[0:48, h, :], ps[0:48, 6 + h % 2, :].bitcast(BF16)).then_inc(S["q5T_ready"], 1)

                def softmax(h, first):
                    for q in range(NT):
                        n = h * NT + q
                        dve.wait_ge(S["s5_psum"], n + 1)
                        if not (first and q < 4):
                            dve.wait_ge(S["exp5_ready"], n - 3)
                        v.tensor_reduce(nm5[:, q % 4:q % 4 + 1], ps[:, 2 * (q % 2):2 * (q % 2) + 2, :].rearrange("p a c -> p (a c)"), AX.X, ALU.max, negate=True).then_inc(S["max5_ready"], 1)
                        dve.wait_ge(S["max5_ready"], n + 1)
                        v.tensor_scalar(b5[:, q % 4:q % 4 + 1], nm5[:, q % 4:q % 4 + 1], sq5[:, q, bass.ds(h, 1)], LN255, ALU.mult, ALU.add).then_inc(S["bias5_ready"], 1)
                        if not (first and q < 1):
                            convert(n - 1, (q - 1) % 2, first and q < 3)
                        if not (first and q < 2):
                            evacuate(n - 2, q % 2, first and q < 4)
                        if q == 2 and not first:
                            outputs(h - 1)

                def convert(n, b, fresh):
                    dve.wait_ge(S["exp5_ready"], n + 1)
                    if not fresh:
                        dve.wait_ge(S["p5T_psum"], n - 1)
                    v.tensor_copy(PI5[:, b, :], Y5[:, b, :]).then_inc(S["pi5_ready"], 1)

                def evacuate(n, b, fresh):
                    dve.wait_ge(S["p5T_psum"], n + 1)
                    if not fresh:
                        dve.wait_ge(S["p5V_done"], n - 1)
                    v.tensor_copy(PT5[:, b, :, :], ps[:, 4 + b, :].bitcast(BF16).rearrange("p (k c) -> p k c", k=8)).then_inc(S["p5T_ready"], 1)

                def outputs(h):
                    dve.wait_ge(S["p5V_done"], (h + 1) * NT)
                    v.reciprocal(r5[:, :], sum5[:, bass.ds(h * NT, NT)]).then_inc(S["r5_ready"], 1)
                    dve.wait_ge(S["r5_ready"], h + 1)
                    v.tensor_tensor(AT[:, :, bass.ds(h * HD, HD)], ps[:, 6, 0:P].rearrange("p (t c) -> p t c", t=NT),
                                    r5[:, :].unsqueeze(2).to_broadcast([P, NT, HD]), ALU.mult).then_inc(S["o5_ready"], 1)

                softmax(0, True)
                with v.Fori(1, H) as h:
                    softmax(h, False)
                convert(H * NT - 1, 1, False)
                evacuate(H * NT - 2, 0, False)
                evacuate(H * NT - 1, 1, False)
                outputs(H - 1)
                dve.wait_ge(S["o5_ready"], H)
                v.tensor_tensor(AT[:, :, :], AT[:, :, :], svrow[:, 0:2, :].rearrange("p k c -> p (k c)").unsqueeze(1).to_broadcast([P, NT, D]), ALU.mult).then_inc(S["out5_ready"], 1)
                for s in range(NT):
                    if s == 0:
                        dve.wait_ge(S["xbias_ready"], NT)
                    residual(s, s, 2 + s % 2, S["proj_psum"], 2 * NT + s + 1)
            if stages >= 6:
                norm(5, 4 * NT)
                c6 = [0]

                def step(inst):
                    inst.then_inc(S["step6"], 1)
                    c6[0] += 1
                    dve.wait_ge(S["step6"], c6[0])

                dve.wait_ge(S["lg_psum"], 1)
                lg = ps[:, 2, :].rearrange("p (t e) -> p t e", t=NT)
                per_tile = lambda a, n: a.unsqueeze(2).to_broadcast([P, NT, n])
                step(v.tensor_reduce(s6[:, 0, :], lg, AX.X, ALU.max))
                step(v.tensor_tensor(L6[:, :, :], lg, per_tile(s6[:, 0, :], NROUTE), ALU.subtract))
                dve.wait_ge(S["exp6_ready"], 1)
                step(v.tensor_reduce(s6[:, 1, :], L6[:, :, :], AX.X, ALU.add))
                step(v.reciprocal(s6[:, 1, :], s6[:, 1, :]))
                step(v.tensor_tensor(L6[:, :, :], L6[:, :, :], per_tile(s6[:, 1, :], NROUTE), ALU.mult))
                step(v.tensor_tensor(BI6[:, :, :], L6[:, :, :], rbias[:, :].unsqueeze(1).to_broadcast([P, NT, NROUTE]), ALU.add))
                for t in range(NT):
                    step(v.max(top6[:, t, :], BI6[:, t, :]))
                for t in range(NT):
                    step(v.match_replace(RP6[:, t, :], top6[:, t, :], BI6[:, t, :], NEG))
                step(v.tensor_tensor(MK6[:, :, :], BI6[:, :, :], RP6[:, :, :], ALU.not_equal))
                step(v.tensor_copy(mr6[:, :, :], MK6[:, :, 0:NE]))
                step(v.memset(cum6[:, 0, :], 0.0))
                for t in range(1, NT):
                    step(v.tensor_tensor(cum6[:, t, :], cum6[:, t - 1, :], mr6[:, t - 1, :], ALU.add))
                dve.sem_inc(S["cnt6_ready"], 1)
                step(v.tensor_tensor(L6[:, :, :], L6[:, :, :], MK6[:, :, :], ALU.mult))
                step(v.tensor_reduce(s6[:, 2, :], L6[:, :, :], AX.X, ALU.add))
                step(v.tensor_scalar(s6[:, 2, :], s6[:, 2, :], 1e-20, None, ALU.add))
                step(v.reciprocal(s6[:, 2, :], s6[:, 2, :]))
                step(v.tensor_scalar(s6[:, 2, :], s6[:, 2, :], 1.5, None, ALU.mult))
                step(v.tensor_tensor(L6[:, :, :], L6[:, :, :], per_tile(s6[:, 2, :], NROUTE), ALU.mult))
                step(v.tensor_reduce(s6[:, 3, :], L6[:, :, NE:NROUTE], AX.X, ALU.add))
                step(v.tensor_scalar(s6[:, 3, :], s6[:, 3, :], 1.0, None, ALU.add))
                step(v.tensor_tensor(L6[:, :, 0:NE], L6[:, :, 0:NE], per_tile(s6[:, 3, :], NE), ALU.mult))
                dve.wait_ge(S["pos6_psum"], 1)
                pos = ps[:, 3, 0:NT * NE].rearrange("p (t e) -> p t e", t=NT)
                step(v.scalar_tensor_tensor(va6[:, :, :], pos, float(CAP), mr6[:, :, :], ALU.is_lt, ALU.mult))
                step(v.tensor_tensor(key6[:, :, :], base6[:, :].unsqueeze(1).to_broadcast([P, NT, NE]), pos, ALU.subtract))
                step(v.tensor_tensor(key6[:, :, :], key6[:, :, :], va6[:, :, :], ALU.mult))
                for t in range(NT):
                    step(v.max(keys6[:, t, :], key6[:, t, :]))
                step(v.tensor_scalar(idxf[:, :, :], keys6[:, :, :], -1.0, 2.0 * SLOTS, ALU.mult, ALU.add))
                flat = idxf[:, :, :].rearrange("p t k -> p (t k)")
                step(v.tensor_copy(idx_put[:, :], flat))
                step(v.tensor_scalar(idx_get[:, :], flat, float(SLOTS), None, ALU.min))
                dve.sem_inc(S["idx_ready"], 1)
                for t in range(NT):
                    step(v.tensor_tensor(eq6[:, t, :, :], key6[:, t, :].unsqueeze(1).to_broadcast([P, 8, NE]), keys6[:, t, :].unsqueeze(2).to_broadcast([P, 8, NE]), ALU.is_equal))
                    step(v.tensor_tensor(eq6[:, t, :, :], eq6[:, t, :, :], L6[:, t, 0:NE].unsqueeze(1).to_broadcast([P, 8, NE]), ALU.mult))
                step(v.tensor_reduce(wk6[:, :, :], eq6, AX.X, ALU.add))
                for s in range(NE + 1):
                    if s < NE:
                        dve.wait_ge(S["silu_ready"], s + 1)
                        if s >= 2:
                            dve.wait_ge(S["ye_psum"], s - 1)
                        v.tensor_tensor(HE[:, s % 2, :], SG[:, s % 2, :], ps[:, 2 + s % 2, CAP:2 * CAP], ALU.mult).then_inc(S["he_ready"], 1)
                    if s >= 1:
                        e = s - 1
                        dve.wait_ge(S["ye_psum"], e + 1)
                        if e >= 4:
                            dve.wait_ge(ye_stored[e % 4], 16 * (e // 4))
                        v.tensor_copy(YE[:, e % 4, :], ps[:, 4 + e % 2, 0:D]).then_inc(S["ye_ready"], 1)
                for j in range(NT * TOPK):
                    t = j // TOPK
                    dve.wait_ge(yg_loaded[j % YGN], 16 * (j // YGN + 1))
                    dve.wait_ge(S["x_ready"], 8 * 5 + j)
                    v.scalar_tensor_tensor(X[:, t, :], YG[:, j % YGN, :], wk6[:, t, j % TOPK:j % TOPK + 1], X[:, t, :], ALU.mult, ALU.add).then_inc(S["x_ready"], 1)


_ARGS = [("x", None), ("ctx_2048", None), ("ctx_2048", (2, 0, 1)), ("L0_attn_weight_qkv", (1, 0)), ("L0_attn_weight_proj", (1, 0)),
         ("L0_ffn_w1", (1, 0)), ("L0_ffn_w2", (1, 0)), ("L1_attn_W_dq", None), ("L1_attn_W_uq", None), ("L1_attn_q_ln_g", None),
         ("L1_attn_q_ln_b", None), ("L1_attn_W_dkv", None), ("L1_attn_W_ukv", None), ("L1_attn_kv_ln_g", None), ("L1_attn_kv_ln_b", None),
         ("L1_attn_W_o", (1, 0)), ("L1_xattn_Wq", None), ("L1_xattn_bq", None), ("L1_xattn_Wkv", None), ("L1_xattn_bkv", None),
         ("L1_xattn_Wp", None), ("L1_xattn_bp", None), ("L1_ffn_w_cls", (1, 0)), ("L1_ffn_bias", None), ("L1_ffn_w_gate_up", None),
         ("L1_ffn_w_down", None)]
STAGES = 6


def kernel(**inputs):
    import numpy as np
    import concourse.bacc as bacc
    from concourse.bass_utils import run_bass_kernel_spmd

    nc = bacc.Bacc("TRN2", target_bir_lowering=False, num_devices=1)
    arrays, args = {}, []
    for i, (name, order) in enumerate(_ARGS):
        a = np.asarray(inputs[name])
        if order is not None:
            a = a.transpose(order)
        if len(order or ()) == 3:
            a = a.reshape(a.shape[0], -1)
        a = np.ascontiguousarray(a)
        arrays[f"in_{i}"] = a
        args.append(nc.dram_tensor(f"in_{i}", a.shape, mybir.dt.from_np(a.dtype), kind="ExternalInput").ap())
    out = nc.dram_tensor("out_0", (NB, SEQ, D), F32, kind="ExternalOutput").ap()
    decoder_kernel(nc, *args, out, stages=STAGES)
    r = run_bass_kernel_spmd(nc, [arrays], core_ids=[0])
    return r.results[0]["out_0"]
```

```python
import concourse.bass as bass
from concourse import mybir
from contextlib import ExitStack

F32 = mybir.dt.float32
BF16 = mybir.dt.bfloat16
I16 = mybir.dt.int16
U32 = mybir.dt.uint32
ALU = mybir.AluOpType
ACT = mybir.ActivationFunctionType
AX = mybir.AxisListType

P = 128
NB, SEQ, D = 4, 256, 256
NT = NB * SEQ // P
KD = D // P
H, HD = 16, 16
FF = 1024
KF = FF // P
LOW = 64
NE, NROUTE, TOPK, CAP = 32, 64, 8, 128
SLOTS = NE * CAP
ROUND = 12582912.0
NEG = -1.0e30
YGN = 8
LN255 = 5.541263545158426
EPS = 1e-5
PARITY_ORDER = [0, 2, 4, 6, 1, 3, 5, 7]
IN_ORDER = list(range(NT))


def decoder_kernel(nc, x_in, ctx_in, ctxT_in, wqkvT_in, wprojT_in, w1T_in, w2T_in, wdq_in, wuq_in, qg_in, qb_in,
                   wdkv_in, wukv_in, kvg_in, kvb_in, woT_in, wq_in, bq_in, wkv_in, bkv_in, wp_in, bp_in,
                   wclsT_in, rbias_in, wgu_in, wdown_in, out, stages=6):
    es = ExitStack()
    with es:
        def sb(name, shape, dt=F32):
            return es.enter_context(nc.sbuf_tensor(name, shape, dt))

        def sem(name):
            return es.enter_context(nc.semaphore(name))

        slot_rows = nc.dram_tensor("slot_rows", [SLOTS, D], F32, kind="Internal").ap()
        y_rows = nc.dram_tensor("y_rows", [SLOTS + P, D], F32, kind="Internal").ap()

        ps = es.enter_context(nc.psum_tensor("ps", [P, 8, 512], F32))

        X = sb("X", [P, NT, D])
        XN = sb("XN", [P, NT, D])
        XT = sb("XT", [P, KD, NT * P])
        AT = sb("AT", [P, NT, D])
        stats = sb("stats", [P, NT, 6])
        mv = sb("mv", [P, NT, 2])
        veps = sb("veps", [P, NT])
        rstd = sb("rstd", [P, NT])
        neghalf = sb("neghalf", [P, 16])
        roundc = sb("roundc", [P, 2])
        identf = sb("identf", [P, P])
        identb = sb("identb", [P, P], BF16)
        causal = sb("causal", [P, P], BF16)
        onesf = sb("onesf", [P, P])
        zeros = sb("zeros", [P, 4 * D])

        ctx_sb = sb("ctx_sb", [P, NT, D])
        ctxT = sb("ctxT", [P, KD, NT * P])
        wqkvT = sb("wqkvT", [P, KD, 384])
        wprojT = sb("wprojT", [P, KD, D])
        wdown2 = sb("wdown2", [P, KD, 2 * LOW])
        wupq = sb("wupq", [P, 4, 4, 32])
        wupk = sb("wupk", [P, 4, 4, 32])
        wuv = sb("wuv", [P, D])
        lng = sb("lng", [P, 1])
        lnb = sb("lnb", [P, 1])
        woT = sb("woT", [P, KD, D])
        wq5 = sb("wq5", [P, KD, D])
        wkv5 = sb("wkv5", [P, KD, 2 * D])
        wp5 = sb("wp5", [P, KD, D])
        wclsT = sb("wclsT", [P, KD, NROUTE])
        bqr = sb("bqr", [P, D])
        bkvr = sb("bkvr", [P, 2 * D])
        bpr = sb("bpr", [P, D])
        rbias = sb("rbias", [P, NROUTE])

        A = sb("A", [P, 16384])
        qkv = A[:, 0:3072].rearrange("p (t c) -> p t c", t=NT)
        prod = [A[:, 3072 + 2560 * j:3072 + 2560 * (j + 1)].rearrange("p (s c) -> p s c", s=10) for j in range(2)]
        w1stage = A[:, 8192:10240].rearrange("p (k c) -> p k c", k=KD)
        w2stage = A[:, 10240:12288].rearrange("p (k c) -> p k c", k=KF)
        QT4 = A[:, 0:4096].rearrange("p (g c) -> p g c", g=4)
        KB4 = A[:, 4096:12288].rearrange("p (b g r c) -> p b g r c", b=2, g=4, r=4)
        V4 = A[:, 12288:14464].rearrange("p (t h c) -> p t h c", t=NT, h=H)
        E4 = A[:, 14464:16000].rearrange("p (b j c) -> p b j c", b=2, j=2)
        PT4 = XT[:, :, :].rearrange("p k c -> p (k c)")[:, 0:1536].rearrange("p (b j c) -> p b j c", b=2, j=2)
        CN = A[:, 14464:15488].rearrange("p (t c) -> p t c", t=NT)
        CNT = XN[:, 0:4, :].rearrange("p t c -> p (t c)")
        QT5 = A[:, 0:8192].bitcast(BF16).rearrange("p (h c) -> p h c", h=H)
        KT5 = A[:, 8192:16384].bitcast(BF16).rearrange("p (h c) -> p h c", h=H)
        WG = A[:, 0:4096].rearrange("p (s k c) -> p s k c", s=8, k=KD)
        WD = A[:, 4096:6144].rearrange("p (s c) -> p s c", s=8)
        XE = A[:, 6144:7168].rearrange("p (s c) -> p s c", s=4)
        XET = A[:, 7168:7680].rearrange("p (s k c) -> p s k c", s=2, k=KD)
        SG = A[:, 7680:7936].rearrange("p (s c) -> p s c", s=2)
        HE = A[:, 7936:8192].rearrange("p (s c) -> p s c", s=2)
        YE = A[:, 8192:9216].rearrange("p (s c) -> p s c", s=4)
        YG = A[:, 9216:9216 + YGN * D].rearrange("p (s c) -> p s c", s=YGN)

        w1t = sb("w1t", [P, KD, FF], BF16)
        w2t = sb("w2t", [P, KF, D], BF16)

        SC = sb("SC", [P, 8, 4, H])
        mx1 = sb("mx1", [P, 8, H])
        rs1 = sb("rs1", [P, 8, H])

        E2 = A[:, 4352:5376].rearrange("p (i e c) -> p i e c", i=2, e=2)
        nm2 = sb("nm2", [P, 2, 2])
        b2 = sb("b2", [P, 2, 2])
        sum2 = sb("sum2", [P, 2, 2])
        r2 = sb("r2", [P, 2, 2])

        wsum = sb("wsum", [P, 2])
        wmean = sb("wmean", [P, 2])
        wrec = sb("wrec", [P, 2])
        w127 = sb("w127", [P, 2])
        am3 = sb("am3", [P, NT])
        qs3 = sb("qs3", [P, NT])
        dq3 = sb("dq3", [P, NT])
        QX = sb("QX", [P, NT, D], BF16)
        QXT = A[:, 4096:4352].bitcast(BF16).rearrange("p (s k c) -> p s k c", s=2, k=KD)
        G3 = A[:, 0:2048].rearrange("p (s c) -> p s c", s=2)
        am3b = sb("am3b", [P, NT])
        qs3b = sb("qs3b", [P, NT])
        dq3b = sb("dq3b", [P, NT])
        QH = A[:, 2048:3072].bitcast(BF16).rearrange("p (s c) -> p s c", s=2)
        QHT = A[:, 3072:4096].bitcast(BF16).rearrange("p (s k c) -> p s k c", s=2, k=KF)

        st4 = sb("st4", [P, 2 * NT, 6])
        mv4 = sb("mv4", [P, 2 * NT, 2])
        ve4 = sb("ve4", [P, 2 * NT])
        rs4 = sb("rs4", [P, 2 * NT])
        m4 = sb("m4", [P, 2, 2, 2])
        r4 = sb("r4", [P, 2, 4])

        KV = sb("KV", [P, NT, 2 * D])
        kmax = sb("kmax", [P, NT, H])
        sk = sb("sk", [P, NT, H])
        rk = sb("rk", [P, NT, H])
        kpart = sb("kpart", [P, NT, H, 3, HD], BF16)
        ktmp = sb("ktmp", [P, 2, D])
        vmax = sb("vmax", [P, D])
        vm2 = sb("vm2", [P, KD])
        svrv = sb("svrv", [P, 2, KD])
        svb = sb("svb", [P, 4, P])
        svrow = sb("svrow", [P, 4, P])
        VI = sb("VI", [P, NT, D], BF16)
        sq5 = sb("sq5", [P, NT, H])
        rq5 = sb("rq5", [P, NT, H])
        QI = QX
        QI3 = kpart
        kv_flat = KV[:, :, :].rearrange("p t c -> p (t c)")
        Y5 = kv_flat[:, 0:1024].bitcast(I16).rearrange("p (b c) -> p b c", b=2)
        PI5 = kv_flat[:, 1024:3072].bitcast(BF16).rearrange("p (b c) -> p b c", b=4)
        PT5 = kv_flat[:, 3072:4096].bitcast(BF16).rearrange("p (b k c) -> p b k c", b=2, k=8)
        nm5 = sb("nm5", [P, 4])
        b5 = sb("b5", [P, 4])
        sum5 = sb("sum5", [P, H * NT])
        r5 = sb("r5", [P, NT])

        L6, BI6, RP6, MK6 = (ctx_sb[:, 2 * i:2 * i + 2, :].rearrange("p a (t e) -> p (a t) e", e=NROUTE) for i in range(4))
        s6 = sb("s6", [P, 6, NT])
        top6 = sb("top6", [P, NT, 8])
        mr6 = sb("mr6", [P, NT, NE], BF16)
        cum6 = sb("cum6", [P, NT, NE], BF16)
        lower = sb("lower", [P, P], BF16)
        onesb = sb("onesb", [P, P], BF16)
        base6 = sb("base6", [P, NE])
        va6 = sb("va6", [P, NT, NE])
        key6 = sb("key6", [P, NT, NE])
        keys6 = sb("keys6", [P, NT, 8])
        idxf = sb("idxf", [P, NT, 8])
        idx_put = sb("idx_put", [P, NT * 8], U32)
        idx_get = sb("idx_get", [P, NT * 8], U32)
        eq6 = AT[:, :, :].rearrange("p t (k e) -> p t k e", e=NE)
        wk6 = sb("wk6", [P, NT, 8])

        names = """x_loaded w0_loaded ctx_loaded w_loaded w1_loaded w2_loaded low_loaded zero_rows
            const_ready zeros_ready pads_ready rstd_e rstd_ready stats_ready aggr_ready xn_ready x_ready tp_psum tp_ready
            qkv_psum qkv_ready prod0_ready prod1_ready step1 exp1_ready at_ready proj_psum
            kv_psum kv_copied kv_ready kscale_ready kq_step vmax_ready vmaxT_psum vscale_ready vrow_psum vrow_ready vint_ready
            wabs_ready wtot_psum wscale_ready wq_step w_ternary
            s2_psum nm2_ready bias2_ready exp2_ready r2_ready attn2_ready out2_psum
            dq3_step qx_step qx_ready qxT_psum qxT_ready h3_psum gelu_ready am3_step qh_step qh_ready qhT_psum qhT_ready out3_psum
            low_psum lstats_ready laggr_ready lveps lrstd_ready cn_ready cnT_psum cnT_ready upq_psum upqa_ready upqd_ready kb_zero kup_psum kupa_ready kupd_ready v4_psum v4_ready
            s4_psum max4_ready sub4_ready exp4_ready p4T_psum p4T_ready o4_psum r4_ready o4_ready
            q5_psum uq5_ready q5_step q5i_ready q5T_psum q5T_ready k5T_psum k5T_ready pad5_ready xbias_ready
            s5_psum max5_ready bias5_ready exp5_ready pi5_ready p5T_psum p5Te_ready p5To_ready p5V_done o5_psum r5_ready o5_ready out5_ready
            lg_psum step6 exp6_ready cnt6_ready pos6_psum idx_ready rows_put
            xeT_psum xeT_ready gu_psum silu_ready he_ready ye_psum ye_ready out_stored""".split()
        S = {n: sem(n) for n in names}
        xe_loaded = [sem(f"xe_loaded{i}") for i in range(4)]
        wg_loaded = [sem(f"wg_loaded{i}") for i in range(8)]
        ye_stored = [sem(f"ye_stored{i}") for i in range(4)]
        yg_loaded = [sem(f"yg_loaded{i}") for i in range(YGN)]

        block = es.enter_context(nc.Block())

        def row(ap):
            return ap.partition_broadcast(P)

        U4 = NB * H // 2
        SUB_READY, P_READY = 10, 13

        STEPS, LAG5 = 2 * NT, 5

        def wait_pos(eng, semaphore, count):
            if not isinstance(count, int) or count > 0:
                eng.wait_ge(semaphore, count)

        def qkv_heads(t, lo, n):
            return qkv[:, t, :].rearrange("p (g c) -> p g c", g=4)[:, :, lo:lo + n]

        def score_products(eng, e, j, done):
            for iq in range(4):
                for ik in range(iq + 1):
                    q = qkv_heads(2 * iq + j, 0, 64).rearrange("p g (r d) -> p g r d", d=HD)
                    k = qkv_heads(2 * ik + j, 64, HD).unsqueeze(2).to_broadcast([P, 4, 4, HD])
                    o = prod[j][:, iq * (iq + 1) // 2 + ik, :].rearrange("p (g r d) -> p g r d", g=4, d=HD)
                    e.tensor_tensor(o, q, k, ALU.mult).then_inc(done, 1)

        def value_products(eng, e, j, done):
            for iq in range(4):
                for ik in range(iq + 1):
                    w = SC[:, j * 4 + iq, ik, :].rearrange("p (g r) -> p g r", g=4).unsqueeze(3).to_broadcast([P, 4, 4, HD])
                    vv = qkv_heads(2 * ik + j, 80, HD).unsqueeze(2).to_broadcast([P, 4, 4, HD])
                    o = prod[j][:, iq * (iq + 1) // 2 + ik, :].rearrange("p (g r d) -> p g r d", g=4, d=HD)
                    e.tensor_tensor(o, vv, w, ALU.mult).then_inc(done, 1)

        @block.sync
        def _(sp):
            sp.dma_start(X[:, :, :], x_in.rearrange("b (j p) d -> p (b j) d", p=P)).then_inc(S["x_loaded"], 16)
            sp.dma_start(wqkvT[:, :, :], wqkvT_in.rearrange("(k p) c -> p k c", p=P)).then_inc(S["w0_loaded"], 16)
            sp.dma_start(wprojT[:, :, :], wprojT_in.rearrange("(k p) c -> p k c", p=P)).then_inc(S["w0_loaded"], 16)
            sp.dma_start(ctxT[:, :, :], ctxT_in.rearrange("(k p) c -> p k c", p=P)).then_inc(S["ctx_loaded"], 16)
            sp.dma_start(wkv5[:, :, :], wkv_in.rearrange("(k p) c -> p k c", p=P)).then_inc(S["ctx_loaded"], 16)
            sp.dma_start(bkvr[:, :], row(bkv_in)).then_inc(S["ctx_loaded"], 16)
            sp.dma_start(ctx_sb[:, :, :], ctx_in.rearrange("b (j p) d -> p (b j) d", p=P)).then_inc(S["ctx_loaded"], 16)
            sp.dma_start(w1stage, w1T_in.rearrange("(k p) c -> p k c", p=P)).then_inc(S["w1_loaded"], 16)
            sp.dma_start(w2stage, w2T_in.rearrange("(k p) c -> p k c", p=P)).then_inc(S["w2_loaded"], 16)
            sp.dma_start(wdown2[:, :, 0:LOW], wdq_in.rearrange("(k p) c -> p k c", p=P)).then_inc(S["low_loaded"], 16)
            sp.dma_start(wdown2[:, :, LOW:2 * LOW], wdkv_in.rearrange("(k p) c -> p k c", p=P)).then_inc(S["low_loaded"], 16)
            sp.wait_ge(S["pads_ready"], 3)
            sp.dma_start(wupq[0:LOW, :, :, 0:HD].rearrange("p g r c -> p (g r) c"), wuq_in.rearrange("l (h c) -> l h c", c=HD)).then_inc(S["low_loaded"], 16)
            sp.dma_start(wupk[LOW:P, :, :, 0:HD].rearrange("p g r c -> p (g r) c"), wukv_in[:, 0:D].rearrange("l (h c) -> l h c", c=HD)).then_inc(S["low_loaded"], 16)
            sp.dma_start(wuv[LOW:P, :], wukv_in[:, D:2 * D]).then_inc(S["low_loaded"], 16)
            for dst, src in ((lng[0:LOW, :], qg_in), (lng[LOW:P, :], kvg_in), (lnb[0:LOW, :], qb_in), (lnb[LOW:P, :], kvb_in)):
                sp.dma_start(dst, src.rearrange("(p a) -> p a", a=1)).then_inc(S["low_loaded"], 16)
            for dst, src in ((woT, woT_in), (wq5, wq_in), (wp5, wp_in), (wclsT, wclsT_in)):
                sp.dma_start(dst[:, :, :], src.rearrange("(k p) c -> p k c", p=P)).then_inc(S["w_loaded"], 16)
            for dst, src in ((bqr, bq_in), (bpr, bp_in), (rbias, rbias_in)):
                sp.dma_start(dst[:, :], row(src)).then_inc(S["w_loaded"], 16)
            sp.wait_ge(S["zeros_ready"], 1)
            if stages >= 6:
                for c in range(SLOTS // (4 * P)):
                    sp.dma_start(slot_rows[c * 4 * P:(c + 1) * 4 * P, :].rearrange("(p a) d -> p (a d)", a=4), zeros[:, :]).then_inc(S["zero_rows"], 16)
                sp.dma_start(y_rows[SLOTS:SLOTS + P, :], zeros[:, 0:D]).then_inc(S["zero_rows"], 16)

                def load_weights(e):
                    sp.dma_start(WG[:, e % 8, :, :], wgu_in[e, :, :].rearrange("(k p) c -> p k c", p=P)).then_inc(wg_loaded[e % 8], 16)
                    sp.dma_start(WD[:, e % 8, :], wdown_in[e, :, :]).then_inc(wg_loaded[e % 8], 16)

                def load_rows(e):
                    sp.dma_start(XE[:, e % 4, :], slot_rows[e * CAP:(e + 1) * CAP, :]).then_inc(xe_loaded[e % 4], 16)

                sp.wait_ge(S["o5_psum"], H)
                for e in range(8):
                    load_weights(e)
                sp.wait_ge(S["rows_put"], 16 * NT * TOPK)
                for e in range(4):
                    load_rows(e)
                for e in range(NE):
                    if e + 4 < NE:
                        sp.wait_ge(S["xeT_psum"], e + 1)
                        load_rows(e + 4)
                    sp.wait_ge(S["ye_ready"], e + 1)
                    sp.dma_start(y_rows[e * CAP:(e + 1) * CAP, :], YE[:, e % 4, :]).then_inc(ye_stored[e % 4], 16)
                    if e + 8 < NE:
                        load_weights(e + 8)
            out_v = out.rearrange("b (j p) d -> p (b j) d", p=P)
            if stages < 6:
                sp.wait_ge(S["x_ready"], 8 * stages)
                sp.dma_start(out_v, X[:, :, :]).then_inc(S["out_stored"], 16)
                sp.wait_ge(S["out_stored"], 16)
            else:
                for t in range(NT):
                    sp.wait_ge(S["x_ready"], 8 * 5 + TOPK * (t + 1))
                    sp.dma_start(out_v[:, t, :], X[:, t, :]).then_inc(S["out_stored"], 16)
                sp.wait_ge(S["out_stored"], 16 * NT)

        @block.gpsimd
        def _(pool):
            g = nc.gpsimd
            g.memset(identf[:, :], 0.0).then_inc(S["const_ready"], 1)
            g.memset(identb[:, :], 0.0).then_inc(S["const_ready"], 1)
            g.memset(neghalf[:, :], -0.5).then_inc(S["const_ready"], 1)
            g.memset(onesf[:, :], 1.0).then_inc(S["const_ready"], 1)
            g.memset(causal[:, :], 0.0).then_inc(S["const_ready"], 1)
            g.memset(lower[:, :], 1.0).then_inc(S["const_ready"], 1)
            g.memset(onesb[:, :], 1.0).then_inc(S["const_ready"], 1)
            pool.wait_ge(S["const_ready"], 7)
            for m in (identf, identb):
                g.affine_select(out=m[:, :], in_=m[:, :], compare_op=ALU.not_equal, fill=1.0, base=0,
                                pattern=[[-1, P]], channel_multiplier=1).then_inc(S["const_ready"], 1)
            g.affine_select(out=causal[:, :], in_=causal[:, :], compare_op=ALU.is_ge, fill=NEG, base=0,
                            pattern=[[-1, P]], channel_multiplier=1).then_inc(S["const_ready"], 1)
            g.affine_select(out=lower[:, :], in_=lower[:, :], compare_op=ALU.is_gt, fill=0.0, base=0,
                            pattern=[[1, P]], channel_multiplier=-1).then_inc(S["const_ready"], 1)
            g.iota(base6[:, :], pattern=[[-CAP, NE]], base=2 * SLOTS, channel_multiplier=0,
                   allow_small_or_imprecise_dtypes=True).then_inc(S["const_ready"], 1)
            g.memset(roundc[:, 0:1], ROUND).then_inc(S["const_ready"], 1)
            g.memset(roundc[:, 1:2], -ROUND).then_inc(S["const_ready"], 1)
            g.memset(SC[:, :, :, :], NEG).then_inc(S["const_ready"], 1)
            for pad in (wupq[:, :, :, :], wupk[:, :, :, :], wuv[:, :]):
                g.memset(pad, 0.0).then_inc(S["pads_ready"], 1)
            g.memset(zeros[:, :], 0.0).then_inc(S["zeros_ready"], 1)

            def norm_rstd(n):
                for s in range(2):
                    tiles = slice(s, NT, 2) if n == 1 else slice(4 * s, 4 * s + 4)
                    pool.wait_ge(S["aggr_ready"], n * NT + 4 * (s + 1))
                    g.tensor_scalar(veps[:, tiles], mv[:, tiles, 1], EPS, None, ALU.add).then_inc(S["rstd_e"], 1)
                    pool.wait_ge(S["rstd_e"], 2 * n + s + 1)
                    g.tensor_tensor(rstd[:, tiles], veps[:, tiles], neghalf[:, 0:4], ALU.pow).then_inc(S["rstd_ready"], 1)

            norm_rstd(0)
            pool.wait_ge(S["qkv_ready"], NT)
            score_products(pool, g, 1, S["prod1_ready"])
            pool.wait_ge(S["step1"], P_READY)
            value_products(pool, g, 1, S["prod1_ready"])
            if stages >= 2:
                norm_rstd(1)
            for t in range(NT):
                pool.wait_ge(S["kv_copied"], t + 1)
                g.tensor_tensor(KV[:, t, :], KV[:, t, :], bkvr[:, :], ALU.add).then_inc(S["kv_ready"], 1)
            if stages >= 3:
                norm_rstd(2)
            if stages >= 2:
                pool.wait_ge(S["vrow_ready"], 1)
            rv = svrow[:, 2:4, :].rearrange("p k c -> p (k c)")
            for t in range(NT if stages >= 2 else 0):
                g.tensor_tensor(KV[:, t, D:2 * D], KV[:, t, D:2 * D], rv, ALU.mult).then_inc(S["vint_ready"], 1)
                pool.wait_ge(S["vint_ready"], 2 * t + 1)
                g.tensor_scalar(VI[:, t, :], KV[:, t, D:2 * D], ROUND, -ROUND, ALU.add, ALU.add).then_inc(S["vint_ready"], 1)
            if stages >= 4:
                norm_rstd(3)
            if stages >= 4:
                pool.wait_ge(S["out3_psum"], NT)
                pool.wait_ge(S["w_ternary"], 2)
                for b in range(2):
                    g.memset(KB4[:, b, :, :, :], 0.0).then_inc(S["kb_zero"], 1)
            for s in range(NT if stages >= 4 else 0):
                pool.wait_ge(S["laggr_ready"], 2 * (s + 1))
                g.tensor_scalar(ve4[:, 2 * s:2 * s + 2], mv4[:, 2 * s:2 * s + 2, 1], EPS, None, ALU.add).then_inc(S["lveps"], 1)
                pool.wait_ge(S["lveps"], s + 1)
                g.tensor_tensor(rs4[:, 2 * s:2 * s + 2], ve4[:, 2 * s:2 * s + 2], neghalf[:, 0:2], ALU.pow).then_inc(S["lrstd_ready"], 1)
            for t in range(NT if stages >= 2 else 0):
                c = 8 * t
                kt = KV[:, t, 0:D].rearrange("p (h d) -> p h d", h=H)
                a = ktmp[:, 0, :].rearrange("p (h d) -> p h d", h=H)
                b = ktmp[:, 1, :].rearrange("p (h d) -> p h d", h=H)
                if t == 0:
                    pool.wait_ge(S["kscale_ready"], 3)
                if t > 0:
                    pool.wait_ge(S["kq_step"], c)
                g.tensor_tensor(a, kt, rk[:, t, :].unsqueeze(2).to_broadcast([P, H, HD]), ALU.mult).then_inc(S["kq_step"], 1)
                pool.wait_ge(S["kq_step"], c + 1)
                g.tensor_scalar(b, a, ROUND, -ROUND, ALU.add, ALU.add).then_inc(S["kq_step"], 1)
                pool.wait_ge(S["kq_step"], c + 2)
                g.tensor_tensor(a, b, sk[:, t, :].unsqueeze(2).to_broadcast([P, H, HD]), ALU.mult).then_inc(S["kq_step"], 1)
                pool.wait_ge(S["kq_step"], c + 3)
                g.tensor_copy(kpart[:, t, :, 0, :], a).then_inc(S["kq_step"], 1)
                pool.wait_ge(S["kq_step"], c + 4)
                g.tensor_tensor(b, a, kpart[:, t, :, 0, :], ALU.subtract).then_inc(S["kq_step"], 1)
                pool.wait_ge(S["kq_step"], c + 5)
                g.tensor_copy(kpart[:, t, :, 1, :], b).then_inc(S["kq_step"], 1)
                pool.wait_ge(S["kq_step"], c + 6)
                g.tensor_tensor(a, b, kpart[:, t, :, 1, :], ALU.subtract).then_inc(S["kq_step"], 1)
                pool.wait_ge(S["kq_step"], c + 7)
                g.tensor_copy(kpart[:, t, :, 2, :], a).then_inc(S["kq_step"], 1)
            if stages >= 5:
                norm_rstd(4)
            for t in range(NT if stages >= 5 else 0):
                pool.wait_ge(S["xn_ready"], 4 * NT + t + 1)
                g.tensor_tensor(X[:, t, :], X[:, t, :], bpr[:, :], ALU.add).then_inc(S["xbias_ready"], 1)
            if stages >= 5:
                pool.wait_ge(S["proj_psum"], 2 * NT)
                g.memset(A[:, 0:8192], 0.0).then_inc(S["pad5_ready"], 2)
                g.memset(A[:, 8192:16384], 0.0).then_inc(S["pad5_ready"], 2)
            if stages >= 6:
                norm_rstd(5)
                pool.wait_ge(S["idx_ready"], 1)
                pool.wait_ge(S["zero_rows"], 16 * (SLOTS // (4 * P) + 1))
                for j in range(NT * TOPK):
                    g.indirect_dma_start(out=slot_rows, out_offset=bass.IndirectOffsetOnAxis(ap=idx_put[:, j:j + 1], axis=0),
                                         in_=XN[:, j // TOPK, :], in_offset=None, bounds_check=SLOTS - 1,
                                         oob_is_err=False).then_inc(S["rows_put"], 16)
                for i in range(4):
                    pool.wait_ge(ye_stored[i], 16 * (NE // 4))
                for j in range(NT * TOPK):
                    if j >= YGN:
                        pool.wait_ge(S["x_ready"], 8 * 5 + j - YGN + 1)
                    g.indirect_dma_start(out=YG[:, j % YGN, :], out_offset=None, in_=y_rows[:, :],
                                         in_offset=bass.IndirectOffsetOnAxis(ap=idx_get[:, j:j + 1], axis=0),
                                         bounds_check=SLOTS + P - 1, oob_is_err=False).then_inc(yg_loaded[j % YGN], 16)

        @block.scalar
        def _(act):
            a = nc.scalar

            def copy_T(m, s, t):
                act.wait_ge(S["tp_psum"], m * NT + s + 1)
                a.activation(XT[:, :, t * P:(t + 1) * P], ps[:, s % 2, 0:D].rearrange("p (k c) -> p k c", k=KD), ACT.Copy).then_inc(S["tp_ready"], 1)

            for s in range(NT + 1):
                if s < NT:
                    copy_T(0, s, s)
                if s >= 1:
                    act.wait_ge(S["qkv_psum"], s)
                    a.activation(qkv[:, s - 1, :], ps[:, 2 + (s - 1) % 2, 0:384], ACT.Copy).then_inc(S["qkv_ready"], 1)
            for t in range(NT):
                act.wait_ge(S["kv_psum"], t + 1)
                a.activation(KV[:, t, :], ps[:, 4 + t % 2, :], ACT.Copy).then_inc(S["kv_copied"], 1)
            act.wait_ge(S["step1"], SUB_READY)
            a.activation(SC[:, :, :, :], SC[:, :, :, :], ACT.Exp, scale=0.25).then_inc(S["exp1_ready"], 1)
            act.wait_ge(S["wscale_ready"], 2)
            w_flat = [w1stage.rearrange("p k c -> p (k c)"), w2stage.rearrange("p k c -> p (k c)")]
            for w in range(2):
                a.activation(w_flat[w], w_flat[w], ACT.Identity, scale=wrec[:, w:w + 1], bias=roundc[:, 0:1]).then_inc(S["wq_step"], 1)
            for s in range(4):
                copy_T(1, s, PARITY_ORDER[s])
            for w in range(2):
                act.wait_ge(S["wq_step"], w + 1)
                a.activation(w_flat[w], w_flat[w], ACT.Identity, bias=roundc[:, 1:2]).then_inc(S["wq_step"], 1)
            for s in range(4, NT):
                copy_T(1, s, PARITY_ORDER[s])
            if stages >= 2:
                for i in range(NB):
                    act.wait_ge(S["bias2_ready"], i + 1)
                    if i >= 2:
                        act.wait_ge(S["out2_psum"], i - 1)
                    for e in range(2):
                        a.activation(E2[:, i % 2, e, :], ps[:, 2 + i % 2, e * D:(e + 1) * D], ACT.Exp, scale=1.0 / 16, bias=b2[:, i % 2, e:e + 1],
                                     accum_out=sum2[:, i % 2, e:e + 1]).then_inc(S["exp2_ready"], 1)
                act.wait_ge(S["vrow_psum"], 1)
                a.activation(svrow[:, :, :], ps[:, 7, :].rearrange("p (a c) -> p a c", a=4), ACT.Copy).then_inc(S["vrow_ready"], 1)
            if stages >= 3:
                for s in range(NT + 2):
                    if s < NT:
                        act.wait_ge(S["qxT_psum"], s + 1)
                        a.activation(QXT[:, s % 2, :, :], ps[:, s % 2, 0:P].bitcast(BF16).rearrange("p (k c) -> p k c", k=KD), ACT.Copy).then_inc(S["qxT_ready"], 1)
                    if 1 <= s <= NT:
                        u = s - 1
                        act.wait_ge(S["h3_psum"], u + 1)
                        if u >= 2:
                            act.wait_ge(S["qh_step"], 2 * (u - 1))
                        a.activation(G3[:, u % 2, :], ps[:, 2 + 2 * (u % 2):4 + 2 * (u % 2), :], ACT.Gelu_apprx_tanh,
                                     scale=dq3[:, u:u + 1]).then_inc(S["gelu_ready"], 1)
                    if s >= 2:
                        u = s - 2
                        act.wait_ge(S["qhT_psum"], u + 1)
                        a.activation(QHT[:, u % 2, :, :], ps[:, 6, :].bitcast(BF16).rearrange("p (k c) -> p k c", k=KF), ACT.Copy).then_inc(S["qhT_ready"], 1)
            if stages >= 4:
                for s in range(NT):
                    copy_T(2, s, s)
                for s in range(NT):
                    act.wait_ge(S["cnT_psum"], s + 1)
                    a.activation(CNT[:, s * P:(s + 1) * P], ps[:, s % 2, 0:P], ACT.Identity, scale=lng[:, 0:1], bias=lnb[:, 0:1]).then_inc(S["cnT_ready"], 1)
                for j in range(0, 8, 2):
                    act.wait_ge(S["upq_psum"], j + 1)
                    a.activation(QT4[:, j % 4, (j // 4) * 512:(j // 4 + 1) * 512], ps[:, 2 + j % 4, :], ACT.Copy).then_inc(S["upqa_ready"], 1)

                def keys_a(n):
                    act.wait_ge(S["kup_psum"], n + 1)
                    b, half = n // 2, n % 2
                    if n == 0:
                        act.wait_ge(S["kb_zero"], 2)
                    for r in range(2):
                        a.activation(KB4[32 * r:32 * r + 32, b % 2, 2 * half:2 * half + 2, r, :], ps[32 * r:32 * r + 32, 7, :].rearrange("p (g c) -> p g c", g=2),
                                     ACT.Copy).then_inc(S["kupa_ready"], 1)

                for t in range(NT):
                    act.wait_ge(S["v4_psum"], t + 1)
                    a.activation(V4[:, t, :, 0:HD], ps[:, 2 + t % 2, 0:D].rearrange("p (h c) -> p h c", h=H), ACT.Copy).then_inc(S["v4_ready"], 1)
                keys_a(0)
                keys_a(1)
                for s in range(U4 + 1):
                    if s % 8 in (3, 6) and s < 24:
                        keys_a(2 * (s // 8 + 1) + (s % 8) // 6)
                    if s < U4:
                        act.wait_ge(S["sub4_ready"], 2 * (s + 1))
                        a.activation(E4[:, s % 2, :, :], E4[:, s % 2, :, :], ACT.Exp, scale=0.25).then_inc(S["exp4_ready"], 1)
                    if s >= 1:
                        u = s - 1
                        act.wait_ge(S["p4T_psum"], u + 1)
                        if u >= 2:
                            act.wait_ge(S["o4_psum"], u - 1)
                        a.activation(PT4[:, u % 2, :, :], ps[:, 4:6, 0:384], ACT.Copy).then_inc(S["p4T_ready"], 1)
                for s in range(NT):
                    copy_T(3, s, s)
            if stages >= 5:
                for s in range(NT):
                    copy_T(4, s, s)
                act.wait_ge(S["pad5_ready"], 4)
                for h in range(H):
                    act.wait_ge(S["k5T_psum"], h + 1)
                    a.activation(KT5[0:48, h, :], ps[0:48, 4 + h % 2, :].bitcast(BF16), ACT.Copy).then_inc(S["k5T_ready"], 1)

                def exps(g, first, last=False):
                    for i in range(STEPS if not last else LAG5):
                        h, q = 2 * g + i // NT, i % NT
                        n = h * NT + q
                        if i % 2 == 0 and not (first and i < 4) and not (last and i >= 4):
                            m = n - 4
                            act.wait_ge(S["p5T_psum"], m + 1)
                            wait_pos(act, S["p5V_done"], m - 1)
                            a.activation(PT5[:, 0, :, :], ps[:, 4, :].bitcast(BF16).rearrange("p (k c) -> p k c", k=8), ACT.Copy).then_inc(S["p5Te_ready"], 1)
                        if not last:
                            act.wait_ge(S["bias5_ready"], n + 1)
                            wait_pos(act, S["pi5_ready"], n - 1)
                            a.activation(Y5[:, q % 2, :], ps[:, 2 * (q % 2):2 * (q % 2) + 2, :], ACT.Exp, scale=sq5[:, q, bass.ds(h, 1)],
                                         bias=b5[:, q % 4:q % 4 + 1], accum_out=sum5[:, bass.ds(n, 1)]).then_inc(S["exp5_ready"], 1)

                exps(0, True)
                with a.Fori(1, H // 2) as g:
                    exps(g, False)
                exps(H // 2, False, True)
                for s in range(NT):
                    copy_T(5, s, s)
            if stages >= 6:
                for s in range(NT):
                    copy_T(6, s, s)
                act.wait_ge(S["step6"], 2)
                a.activation(L6[:, :, :], L6[:, :, :], ACT.Exp).then_inc(S["exp6_ready"], 1)
                for s in range(NE + 1):
                    if s < NE:
                        act.wait_ge(S["xeT_psum"], s + 1)
                        if s >= 2:
                            act.wait_ge(S["gu_psum"], s - 1)
                        a.activation(XET[:, s % 2, :, :], ps[:, s % 2, 0:D].rearrange("p (k c) -> p k c", k=KD), ACT.Copy).then_inc(S["xeT_ready"], 1)
                    if s >= 1:
                        e = s - 1
                        act.wait_ge(S["gu_psum"], e + 1)
                        if e >= 2:
                            act.wait_ge(S["he_ready"], e - 1)
                        a.activation(SG[:, e % 2, :], ps[:, 2 + e % 2, 0:CAP], ACT.Silu).then_inc(S["silu_ready"], 1)

        @block.tensor
        def _(pe):
            T = nc.tensor
            pe.wait_ge(S["const_ready"], 15)

            def to_T(m, s, src, ready, count):
                c = m * NT + s + 1
                pe.wait_ge(ready, count)
                if c > 2:
                    pe.wait_ge(S["tp_ready"], c - 2)
                for k in range(KD):
                    last = T.transpose(ps[:, s % 2, k * P:(k + 1) * P], src[:, k * P:(k + 1) * P], identf[:, :])
                last.then_inc(S["tp_psum"], 1)

            def project(m, s, t, bank, w, n, done, free, free_count):
                pe.wait_ge(S["tp_ready"], m * NT + s + 1)
                if free is not None and free_count > 0:
                    pe.wait_ge(free, free_count)
                for k in range(KD):
                    last = T.matmul(ps[:, bank, 0:n], XT[:, k, t * P:(t + 1) * P], w[:, k, 0:n], start=(k == 0), stop=(k == KD - 1))
                last.then_inc(done, 1)

            for s in range(NT + 1):
                if s < NT:
                    to_T(0, s, XN[:, s, :], S["xn_ready"], s + 1)
                if s >= 1:
                    if s == 1:
                        pe.wait_ge(S["w0_loaded"], 32)
                    project(0, s - 1, s - 1, 2 + (s - 1) % 2, wqkvT, 384, S["qkv_psum"], S["qkv_ready"], s - 2)
            pe.wait_ge(S["ctx_loaded"], 64)
            for t in range(NT):
                if t >= 2:
                    pe.wait_ge(S["kv_copied"], t - 1)
                for k in range(KD):
                    last = T.matmul(ps[:, 4 + t % 2, :], ctxT[:, k, t * P:(t + 1) * P], wkv5[:, k, :], start=(k == 0), stop=(k == KD - 1))
                last.then_inc(S["kv_psum"], 1)
            pe.wait_ge(S["wabs_ready"], 2)
            T.matmul(ps[:, 6, 0:2], onesf[:, :], wsum[:, :], start=True, stop=True).then_inc(S["wtot_psum"], 1)
            for s in range(NT + 1):
                if s < NT:
                    to_T(1, s, AT[:, PARITY_ORDER[s], :], S["at_ready"], s + 1)
                if s >= 1:
                    project(1, s - 1, PARITY_ORDER[s - 1], 2 + (s - 1) % 2, wprojT, D, S["proj_psum"], S["x_ready"], s - 2)
            if stages >= 2:
                for s in range(NB + 1):
                    if s < NB:
                        pe.wait_ge(S["xn_ready"], NT + 4 + s + 1)
                        pe.wait_ge(S["x_ready"], NT)
                        if s >= 2:
                            pe.wait_ge(S["exp2_ready"], 2 * (s - 1))
                        for e in range(2):
                            for j in range(2):
                                last = T.matmul(ps[:, 2 + s % 2, e * D:(e + 1) * D], ctx_sb[:, 2 * s + j, e * P:(e + 1) * P], XN[:, 2 * s + j, :], start=(j == 0), stop=(j == 1))
                        last.then_inc(S["s2_psum"], 1)
                    if s >= 1:
                        i = s - 1
                        pe.wait_ge(S["attn2_ready"], 2 * (i + 1))
                        if i >= 2:
                            pe.wait_ge(S["x_ready"], NT + 2 * (i - 1))
                        for j in range(2):
                            for e in range(2):
                                last = T.matmul(ps[:, 4 + i % 2, j * D:(j + 1) * D], ctxT[:, e, i * SEQ + j * P:i * SEQ + (j + 1) * P], E2[:, i % 2, e, :], start=(e == 0), stop=(e == 1))
                        last.then_inc(S["out2_psum"], 1)
                pe.wait_ge(S["vmax_ready"], 1)
                for k in range(KD):
                    last = T.transpose(ps[:, 6, k * P:(k + 1) * P], vmax[:, k * P:(k + 1) * P], identf[:, :])
                last.then_inc(S["vmaxT_psum"], 1)
                pe.wait_ge(S["vscale_ready"], 4)
                for a in range(2):
                    for k in range(KD):
                        last = T.matmul(ps[:, 7, (a * KD + k) * P:(a * KD + k + 1) * P], svb[:, a * KD + k, :], identf[:, :], start=True, stop=True)
                last.then_inc(S["vrow_psum"], 1)
            if stages >= 3:
                pe.wait_ge(S["w_ternary"], 2)
                for s in range(NT + 2):
                    if s < NT:
                        pe.wait_ge(S["qx_ready"], s + 1)
                        if s >= 2:
                            pe.wait_ge(S["qxT_ready"], s - 1)
                        for k in range(KD):
                            last = T.transpose(ps[:, s % 2, k * 64:(k + 1) * 64].bitcast(BF16), QX[:, s, k * P:(k + 1) * P], identb[:, :])
                        last.then_inc(S["qxT_psum"], 1)
                        pe.wait_ge(S["qxT_ready"], s + 1)
                        if s >= 2:
                            pe.wait_ge(S["gelu_ready"], s - 1)
                        elif s == 0:
                            pe.wait_ge(S["x_ready"], 2 * NT)
                        for n in range(2):
                            for k in range(KD):
                                last = T.matmul(ps[:, 2 + 2 * (s % 2) + n, :], QXT[:, s % 2, k, :], w1t[:, k, n * 512:(n + 1) * 512], start=(k == 0), stop=(k == KD - 1))
                        last.then_inc(S["h3_psum"], 1)
                    if s >= 2:
                        u = s - 2
                        pe.wait_ge(S["qh_ready"], u + 1)
                        if u >= 1:
                            pe.wait_ge(S["qhT_ready"], u)
                        for k in range(KF):
                            last = T.transpose(ps[:, 6, k * 64:(k + 1) * 64].bitcast(BF16), QH[:, u % 2, k * P:(k + 1) * P], identb[:, :])
                        last.then_inc(S["qhT_psum"], 1)
                        pe.wait_ge(S["qhT_ready"], u + 1)
                        if u >= 1:
                            pe.wait_ge(S["x_ready"], 2 * NT + u)
                        for k in range(KF):
                            last = T.matmul(ps[:, 7, 0:D], QHT[:, u % 2, k, :], w2t[:, k, :], start=(k == 0), stop=(k == KF - 1))
                        last.then_inc(S["out3_psum"], 1)
            if stages >= 4:
                pe.wait_ge(S["low_loaded"], 16 * 9)
                for s in range(NT + 1):
                    if s < NT:
                        to_T(2, s, XN[:, s, :], S["xn_ready"], 3 * NT + s + 1)
                    if s >= 1:
                        project(2, s - 1, s - 1, 2 + (s - 1) % 2, wdown2, 2 * LOW, S["low_psum"], S["cn_ready"], 2 * (s - 2))
                for s in range(NT):
                    pe.wait_ge(S["cn_ready"], 2 * (s + 1))
                    if s >= 2:
                        pe.wait_ge(S["cnT_ready"], s - 1)
                    T.transpose(ps[:, s % 2, 0:P], CN[:, s, :], identf[:, :]).then_inc(S["cnT_psum"], 1)
                for j in range(8):
                    half, g = j // 4, j % 4
                    if j in (0, 4):
                        pe.wait_ge(S["cnT_ready"], 4 * (half + 1))
                    if j == 0:
                        pe.wait_ge(S["cn_ready"], 2 * NT)
                    if j >= 4:
                        pe.wait_ge(S[("upqa_ready", "upqd_ready")[j % 2]], j // 2 - 1)
                    T.matmul(ps[:, 2 + j % 4, :], wupq[:, g, :, :].rearrange("p r c -> p (r c)"), CNT[:, half * 512:(half + 1) * 512],
                             start=True, stop=True).then_inc(S["upq_psum"], 1)
                for t in range(NT):
                    if t < 2:
                        pe.wait_ge(S[("upqa_ready", "upqd_ready")[t]], 3)
                    if t >= 2:
                        pe.wait_ge(S["v4_ready"], t - 1)
                    T.matmul(ps[:, 2 + t % 2, 0:D], CNT[:, t * P:(t + 1) * P], wuv[:, :], start=True, stop=True).then_inc(S["v4_psum"], 1)

                def keys_up(n):
                    b, half = n // 2, n % 2
                    if n >= 1:
                        pe.wait_ge(S["kupa_ready"], 2 * n)
                        pe.wait_ge(S["kupd_ready"], 2 * n)
                    for g in range(2):
                        done = T.matmul(ps[:, 7, g * SEQ:(g + 1) * SEQ], wupk[:, 2 * half + g, :, :].rearrange("p r c -> p (r c)"), CNT[:, b * SEQ:(b + 1) * SEQ],
                                        start=True, stop=True)
                    done.then_inc(S["kup_psum"], 1)

                keys_up(0)
                keys_up(1)
                for s in range(U4 + 2):
                    if s < U4:
                        b, hp = s // 8, s % 8
                        if s == 0:
                            pe.wait_ge(S["upqa_ready"], 4)
                            pe.wait_ge(S["upqd_ready"], 5)
                            pe.wait_ge(S["v4_ready"], NT)
                        if hp == 0:
                            pe.wait_ge(S["kupa_ready"], 4 * (b + 1))
                            pe.wait_ge(S["kupd_ready"], 4 * (b + 1))
                        if hp in (2, 5) and b < NB - 1:
                            if hp == 2 and b >= 1:
                                pe.wait_ge(S["s4_psum"], 8 * b)
                            keys_up(2 * (b + 1) + hp // 5)
                        if s >= 2:
                            pe.wait_ge(S["sub4_ready"], 2 * (s - 1))
                        for j in range(2):
                            hh = 2 * hp + j
                            bank = 2 * (s % 2) + j
                            q = QT4[:, hh // 4, b * SEQ:(b + 1) * SEQ]
                            k = KB4[:, b % 2, hh // 4, hh % 4, :]
                            T.matmul(ps[:, bank, 0:P], q[:, 0:P], k[:, 0:P], start=True, stop=False)
                            T.matmul(ps[:, bank, 0:P], identb[:, :], causal[:, :], start=False, stop=True)
                            T.matmul(ps[:, bank, P:3 * P], q[:, P:2 * P], k[:, :], start=True, stop=False)
                            last = T.matmul(ps[:, bank, 2 * P:3 * P], identb[:, :], causal[:, :], start=False, stop=True)
                        last.then_inc(S["s4_psum"], 1)
                    if 1 <= s <= U4:
                        u = s - 1
                        pe.wait_ge(S["exp4_ready"], u + 1)
                        if u >= 1:
                            pe.wait_ge(S["p4T_ready"], u)
                        for j in range(2):
                            for m in range(3):
                                last = T.transpose(ps[:, 4 + j, m * P:(m + 1) * P], E4[:, u % 2, j, m * P:(m + 1) * P], identf[:, :])
                        last.then_inc(S["p4T_psum"], 1)
                    if s >= 2:
                        u = s - 2
                        b, hp = u // 8, u % 8
                        pe.wait_ge(S["p4T_ready"], u + 1)
                        if u >= 1:
                            pe.wait_ge(S["o4_ready"], u)
                        for j in range(2):
                            hh = 2 * hp + j
                            o0 = ps[:, 6, (2 * j) * 17:(2 * j + 1) * 17]
                            o1 = ps[:, 6, (2 * j + 1) * 17:(2 * j + 2) * 17]
                            p = PT4[:, u % 2, j, :]
                            T.matmul(o0, p[:, 0:P], V4[:, 2 * b, hh, :], start=True, stop=True)
                            T.matmul(o1, p[:, P:2 * P], V4[:, 2 * b, hh, :], start=True, stop=False)
                            last = T.matmul(o1, p[:, 2 * P:3 * P], V4[:, 2 * b + 1, hh, :], start=False, stop=True)
                        last.then_inc(S["o4_psum"], 1)
                pe.wait_ge(S["w_loaded"], 16 * 7)
                for s in range(NT + 1):
                    if s < NT:
                        to_T(3, s, AT[:, s, :], S["o4_ready"], 8 * (s // 2 + 1))
                    if s >= 1:
                        project(3, s - 1, s - 1, 2 + (s - 1) % 2, woT, D, S["proj_psum"], S["x_ready"], 3 * NT + s - 2)
            if stages >= 5:
                for s in range(NT + 1):
                    if s < NT:
                        to_T(4, s, XN[:, s, :], S["xn_ready"], 4 * NT + s + 1)
                    if s >= 1:
                        project(4, s - 1, s - 1, 2 + (s - 1) % 2, wq5, D, S["q5_psum"], S["uq5_ready"], s - 2)
                pe.wait_ge(S["kq_step"], 8 * NT)
                for h in range(H):
                    if h >= 2:
                        pe.wait_ge(S["k5T_ready"], h - 1)
                    for t in range(NT):
                        last = T.transpose(ps[0:48, 4 + h % 2, t * 64:(t + 1) * 64].bitcast(BF16), kpart[:, t, h, :, :].rearrange("p a c -> p (a c)"), identb[:, :])
                    last.then_inc(S["k5T_psum"], 1)
                pe.wait_ge(S["q5i_ready"], 3)
                for h in range(H):
                    if h >= 2:
                        pe.wait_ge(S["q5T_ready"], h - 1)
                    for t in range(NT):
                        last = T.transpose(ps[0:48, 6 + h % 2, t * 64:(t + 1) * 64].bitcast(BF16), QI3[:, t, h, :, :].rearrange("p a c -> p (a c)"), identb[:, :])
                    last.then_inc(S["q5T_psum"], 1)
                pe.wait_ge(S["q5T_ready"], H)
                pe.wait_ge(S["k5T_ready"], H)
                pe.wait_ge(S["vint_ready"], 2 * NT)

                def heads(g, first, last=False):
                    for i in range(STEPS if not last else LAG5):
                        h, q = 2 * g + i // NT, i % NT
                        n = h * NT + q
                        if not last:
                            wait_pos(pe, S["exp5_ready"], n - 1)
                            for c in range(2):
                                done = T.matmul(ps[:, 2 * (q % 2) + c, :], QT5[:, h, q * P:(q + 1) * P], KT5[:, h, c * 512:(c + 1) * 512], start=True, stop=True)
                            done.then_inc(S["s5_psum"], 1)
                        ready = "p5Te_ready" if i % 2 == 1 else "p5To_ready"
                        if not (first and i < 3) and not (last and i >= 3):
                            transposes(n - 3, (i + 1) % 2, (i + 1) % 4, ready, NT * g + (i - 3) // 2)
                        if not (first and i < 5):
                            j = i - 5
                            values(n - 5, j % NT, 2 * g + j // NT, (j // NT) % 2, ready, NT * g + (i - 3) // 2)

                def transposes(n, b, buf, ready, count):
                    pe.wait_ge(S["pi5_ready"], n + 1)
                    wait_pos(pe, S[ready], count)
                    for k in range(8):
                        done = T.transpose(ps[:, 4 + b, k * 64:(k + 1) * 64].bitcast(BF16), PI5[:, buf, k * P:(k + 1) * P], identb[:, :])
                    done.then_inc(S["p5T_psum"], 1)

                def values(n, q, h, bank, ready, count):
                    pe.wait_ge(S[ready], count)
                    if q == 0:
                        wait_pos(pe, S["o5_ready"], h - 1)
                    for k in range(8):
                        done = T.matmul(ps[:, 6 + bank, q * HD:(q + 1) * HD], PT5[:, q % 2, k, :], VI[:, k, bass.ds(h * HD, HD)], start=(k == 0), stop=(k == 7))
                    done.then_inc(S["p5V_done"], 1)

                heads(0, True)
                with T.Fori(1, H // 2) as g:
                    heads(g, False)
                heads(H // 2, False, True)
                pe.wait_ge(S["p5V_done"], H * NT)
                pe.sem_inc(S["o5_psum"], H)
                for s in range(NT + 1):
                    if s < NT:
                        to_T(5, s, AT[:, s, :], S["out5_ready"], 1)
                    if s >= 1:
                        project(5, s - 1, s - 1, 2 + (s - 1) % 2, wp5, D, S["proj_psum"], S["x_ready"], 4 * NT + s - 2)
            if stages >= 6:
                for s in range(NT + 1):
                    if s < NT:
                        to_T(6, s, XN[:, s, :], S["xn_ready"], 5 * NT + s + 1)
                    if s >= 1:
                        if s == 1:
                            pe.wait_ge(S["x_ready"], 5 * NT)
                        t = s - 1
                        pe.wait_ge(S["tp_ready"], 6 * NT + s)
                        for k in range(KD):
                            last = T.matmul(ps[:, 2, t * NROUTE:(t + 1) * NROUTE], XT[:, k, t * P:(t + 1) * P], wclsT[:, k, :], start=(k == 0), stop=(k == KD - 1))
                last.then_inc(S["lg_psum"], 1)
                pe.wait_ge(S["cnt6_ready"], 1)
                T.matmul(ps[:, 3, 0:NT * NE], lower[:, :], mr6[:, :, :].rearrange("p t e -> p (t e)"), start=True, stop=False)
                T.matmul(ps[:, 3, 0:NT * NE], onesb[:, :], cum6[:, :, :].rearrange("p t e -> p (t e)"), start=False, stop=True).then_inc(S["pos6_psum"], 1)
                pe.wait_ge(S["idx_ready"], 1)
                for s in range(NE + 2):
                    if s < NE:
                        pe.wait_ge(xe_loaded[s % 4], 16 * (s // 4 + 1))
                        if s >= 2:
                            pe.wait_ge(S["xeT_ready"], s - 1)
                        for k in range(KD):
                            last = T.transpose(ps[:, s % 2, k * P:(k + 1) * P], XE[:, s % 4, k * P:(k + 1) * P], identf[:, :])
                        last.then_inc(S["xeT_psum"], 1)
                    if 1 <= s <= NE:
                        e = s - 1
                        pe.wait_ge(wg_loaded[e % 8], 32 * (e // 8 + 1))
                        pe.wait_ge(S["xeT_ready"], e + 1)
                        if e >= 2:
                            pe.wait_ge(S["he_ready"], e - 1)
                        for f in range(2):
                            for k in range(KD):
                                last = T.matmul(ps[:, 2 + e % 2, f * P:(f + 1) * P], WG[:, e % 8, k, f * P:(f + 1) * P], XET[:, e % 2, k, :], start=(k == 0), stop=(k == KD - 1))
                        last.then_inc(S["gu_psum"], 1)
                    if s >= 2:
                        e = s - 2
                        pe.wait_ge(S["he_ready"], e + 1)
                        if e >= 2:
                            pe.wait_ge(S["ye_ready"], e - 1)
                        T.matmul(ps[:, 4 + e % 2, 0:D], HE[:, e % 2, :], WD[:, e % 8, :], start=True, stop=True).then_inc(S["ye_psum"], 1)

        @block.vector
        def _(dve):
            v = nc.vector
            dve.wait_ge(S["const_ready"], 15)

            def norm(n, count0):
                order = PARITY_ORDER if n == 1 else IN_ORDER
                for s in range(NT):
                    if n == 0:
                        dve.wait_ge(S["x_loaded"], 16)
                    else:
                        dve.wait_ge(S["x_ready"], count0 + s + 1)
                    v.bn_stats(stats[:, order[s], :], X[:, order[s], :]).then_inc(S["stats_ready"], 1)
                for s in range(NT):
                    dve.wait_ge(S["stats_ready"], n * NT + s + 1)
                    v.bn_aggr(mv[:, order[s], :], stats[:, order[s], :]).then_inc(S["aggr_ready"], 1)
                for s in range(NT):
                    t = order[s]
                    dve.wait_ge(S["rstd_ready"], 2 * n + s // 4 + 1)
                    v.tensor_scalar(XN[:, t, :], X[:, t, :], mv[:, t, 0:1], rstd[:, t:t + 1], ALU.subtract, ALU.mult).then_inc(S["xn_ready"], 1)

            def residual(s, t, bank, done, count):
                dve.wait_ge(done, count)
                v.tensor_tensor(X[:, t, :], X[:, t, :], ps[:, bank, 0:D], ALU.add).then_inc(S["x_ready"], 1)

            norm(0, 0)
            dve.wait_ge(S["w1_loaded"], 16)
            v.tensor_reduce(wsum[:, 0:1], w1stage.rearrange("p k c -> p (k c)"), AX.X, ALU.add, apply_absolute_value=True).then_inc(S["wabs_ready"], 1)
            dve.wait_ge(S["w2_loaded"], 16)
            v.tensor_reduce(wsum[:, 1:2], w2stage.rearrange("p k c -> p (k c)"), AX.X, ALU.add, apply_absolute_value=True).then_inc(S["wabs_ready"], 1)
            dve.wait_ge(S["qkv_ready"], NT)
            score_products(dve, v, 0, S["prod0_ready"])
            for j in range(2):
                for iq in range(4):
                    off = iq * (iq + 1) // 2
                    dve.wait_ge(S[f"prod{j}_ready"], off + iq + 1)
                    v.tensor_reduce(SC[:, j * 4 + iq, 0:iq + 1, :], prod[j][:, off:off + iq + 1, :].rearrange("p s (h d) -> p (s h) d", d=HD),
                                    AX.X, ALU.add).then_inc(S["step1"], 1)
            dve.wait_ge(S["step1"], 8)
            v.tensor_reduce(mx1[:, :, :], SC[:, :, :, :].rearrange("p a k h -> p a h k"), AX.X, ALU.max).then_inc(S["step1"], 1)
            dve.wait_ge(S["step1"], 9)
            v.tensor_tensor(SC[:, :, :, :], SC[:, :, :, :], mx1[:, :, :].unsqueeze(2).to_broadcast([P, 8, 4, H]), ALU.subtract).then_inc(S["step1"], 1)
            dve.wait_ge(S["wtot_psum"], 1)
            v.tensor_scalar(wmean[:, :], ps[:, 6, 0:2], 1.0 / (FF * D), EPS, ALU.mult, ALU.max).then_inc(S["wscale_ready"], 1)
            dve.wait_ge(S["wscale_ready"], 1)
            v.reciprocal(wrec[:, :], wmean[:, :]).then_inc(S["wscale_ready"], 1)
            v.tensor_scalar(w127[:, :], wmean[:, :], 1.0 / 127, None, ALU.mult).then_inc(S["wscale_ready"], 1)
            dve.wait_ge(S["exp1_ready"], 1)
            v.tensor_reduce(rs1[:, :, :], SC[:, :, :, :].rearrange("p a k h -> p a h k"), AX.X, ALU.add).then_inc(S["step1"], 1)
            dve.wait_ge(S["step1"], 11)
            v.reciprocal(rs1[:, :, :], rs1[:, :, :]).then_inc(S["step1"], 1)
            dve.wait_ge(S["step1"], 12)
            v.tensor_tensor(SC[:, :, :, :], SC[:, :, :, :], rs1[:, :, :].unsqueeze(2).to_broadcast([P, 8, 4, H]), ALU.mult).then_inc(S["step1"], 1)
            dve.wait_ge(S["step1"], 13)
            value_products(dve, v, 0, S["prod0_ready"])
            for j in range(2):
                for iq in range(4):
                    off = iq * (iq + 1) // 2
                    dve.wait_ge(S[f"prod{j}_ready"], 10 + off + iq + 1)
                    v.tensor_reduce(AT[:, 2 * iq + j, :], prod[j][:, off:off + iq + 1, :].rearrange("p s c -> p c s"),
                                    AX.X, ALU.add).then_inc(S["at_ready"], 1)
            for s in range(NT):
                residual(s, PARITY_ORDER[s], 2 + s % 2, S["proj_psum"], s + 1)
            if stages >= 2:
                norm(1, 0)
                for s in range(NB + 1):
                    if s < NB:
                        dve.wait_ge(S["s2_psum"], s + 1)
                        v.tensor_reduce(nm2[:, s % 2, :], ps[:, 2 + s % 2, :].rearrange("p (e c) -> p e c", e=2), AX.X, ALU.max, negate=True).then_inc(S["nm2_ready"], 1)
                        dve.wait_ge(S["nm2_ready"], s + 1)
                        v.tensor_scalar(b2[:, s % 2, :], nm2[:, s % 2, :], 1.0 / 16, None, ALU.mult).then_inc(S["bias2_ready"], 1)
                    if s >= 1:
                        i = s - 1
                        dve.wait_ge(S["exp2_ready"], 2 * (i + 1))
                        v.reciprocal(r2[:, i % 2, :], sum2[:, i % 2, :]).then_inc(S["r2_ready"], 1)
                        dve.wait_ge(S["r2_ready"], i + 1)
                        for e in range(2):
                            v.tensor_scalar(E2[:, i % 2, e, :], E2[:, i % 2, e, :], r2[:, i % 2, e:e + 1], None, ALU.mult).then_inc(S["attn2_ready"], 1)
                        dve.wait_ge(S["out2_psum"], i + 1)
                        for j in range(2):
                            v.tensor_tensor(X[:, 2 * i + j, :], X[:, 2 * i + j, :], ps[:, 4 + i % 2, j * D:(j + 1) * D], ALU.add).then_inc(S["x_ready"], 1)
                dve.wait_ge(S["kv_ready"], NT)
                v.tensor_reduce(kmax[:, :, :], KV[:, :, 0:D].rearrange("p t (h d) -> p t h d", h=H), AX.X, ALU.max, apply_absolute_value=True).then_inc(S["kscale_ready"], 1)
                dve.wait_ge(S["kscale_ready"], 1)
                v.tensor_scalar(sk[:, :, :], kmax[:, :, :], 1.0 / 127, 1e-8, ALU.mult, ALU.max).then_inc(S["kscale_ready"], 1)
                dve.wait_ge(S["kscale_ready"], 2)
                v.reciprocal(rk[:, :, :], sk[:, :, :]).then_inc(S["kscale_ready"], 1)
                v.tensor_reduce(vmax[:, :], KV[:, :, D:2 * D].rearrange("p t c -> p c t"), AX.X, ALU.max, apply_absolute_value=True).then_inc(S["vmax_ready"], 1)
                dve.wait_ge(S["vmaxT_psum"], 1)
                v.tensor_reduce(vm2[:, :], ps[:, 6, 0:D].rearrange("p (k c) -> p k c", k=KD), AX.X, ALU.max).then_inc(S["vscale_ready"], 1)
                dve.wait_ge(S["vscale_ready"], 1)
                v.tensor_scalar(svrv[:, 0, :], vm2[:, :], 1.0 / 127, 1e-8, ALU.mult, ALU.max).then_inc(S["vscale_ready"], 1)
                dve.wait_ge(S["vscale_ready"], 2)
                v.reciprocal(svrv[:, 1, :], svrv[:, 0, :]).then_inc(S["vscale_ready"], 1)
                dve.wait_ge(S["vscale_ready"], 3)
                v.tensor_copy(svb[:, :, :], svrv[:, :, :].rearrange("p a k -> p (a k)").unsqueeze(2).to_broadcast([P, 4, P])).then_inc(S["vscale_ready"], 1)
            if stages >= 3:
                for w, (stage, dst) in enumerate(((w1stage, w1t), (w2stage, w2t))):
                    dve.wait_ge(S["wq_step"], w + 3)
                    v.tensor_scalar(dst[:, :, :], stage, 1.0, -1.0, ALU.min, ALU.max).then_inc(S["w_ternary"], 1)
                norm(2, NT)
                dve.wait_ge(S["xn_ready"], 3 * NT)
                v.tensor_reduce(am3[:, :], XN[:, :, :], AX.X, ALU.max, apply_absolute_value=True).then_inc(S["dq3_step"], 1)
                dve.wait_ge(S["dq3_step"], 1)
                v.tensor_scalar(am3[:, :], am3[:, :], EPS, None, ALU.max).then_inc(S["dq3_step"], 1)
                dve.wait_ge(S["dq3_step"], 2)
                v.reciprocal(qs3[:, :], am3[:, :]).then_inc(S["dq3_step"], 1)
                v.tensor_scalar(dq3[:, :], am3[:, :], w127[:, 0:1], None, ALU.mult).then_inc(S["dq3_step"], 1)
                dve.wait_ge(S["dq3_step"], 3)
                v.tensor_scalar(qs3[:, :], qs3[:, :], 127.0, None, ALU.mult).then_inc(S["dq3_step"], 1)
                dve.wait_ge(S["dq3_step"], 5)
                for s in range(NT):
                    v.tensor_scalar(XN[:, s, :], XN[:, s, :], qs3[:, s:s + 1], ROUND, ALU.mult, ALU.add).then_inc(S["qx_step"], 1)
                for s in range(NT):
                    dve.wait_ge(S["qx_step"], s + 1)
                    v.tensor_scalar(QX[:, s, :], XN[:, s, :], -ROUND, None, ALU.add).then_inc(S["qx_ready"], 1)
                for s in range(NT + 1):
                    if s < NT:
                        dve.wait_ge(S["gelu_ready"], s + 1)
                        g3 = G3[:, s % 2, :]
                        v.tensor_reduce(am3b[:, s:s + 1], g3, AX.X, ALU.max, apply_absolute_value=True).then_inc(S["am3_step"], 1)
                        dve.wait_ge(S["am3_step"], 5 * s + 1)
                        v.tensor_scalar(am3b[:, s:s + 1], am3b[:, s:s + 1], EPS, None, ALU.max).then_inc(S["am3_step"], 1)
                        dve.wait_ge(S["am3_step"], 5 * s + 2)
                        v.reciprocal(qs3b[:, s:s + 1], am3b[:, s:s + 1]).then_inc(S["am3_step"], 1)
                        dve.wait_ge(S["am3_step"], 5 * s + 3)
                        v.tensor_scalar(qs3b[:, s:s + 1], qs3b[:, s:s + 1], 127.0, None, ALU.mult).then_inc(S["am3_step"], 1)
                        v.tensor_scalar(dq3b[:, s:s + 1], am3b[:, s:s + 1], w127[:, 1:2], None, ALU.mult).then_inc(S["am3_step"], 1)
                        dve.wait_ge(S["am3_step"], 5 * s + 4)
                        v.tensor_scalar(g3, g3, qs3b[:, s:s + 1], ROUND, ALU.mult, ALU.add).then_inc(S["qh_step"], 1)
                        dve.wait_ge(S["qh_step"], 2 * s + 1)
                        if s >= 2:
                            dve.wait_ge(S["qhT_psum"], s - 1)
                        v.tensor_scalar(QH[:, s % 2, :], g3, -ROUND, None, ALU.add).then_inc(S["qh_step"], 1)
                        dve.wait_ge(S["qh_step"], 2 * s + 2)
                        dve.sem_inc(S["qh_ready"], 1)
                    if s >= 1:
                        u = s - 1
                        dve.wait_ge(S["out3_psum"], u + 1)
                        v.scalar_tensor_tensor(X[:, u, :], ps[:, 7, 0:D], dq3b[:, u:u + 1], X[:, u, :], ALU.mult, ALU.add).then_inc(S["x_ready"], 1)
            if stages >= 4:
                norm(3, 2 * NT)
                for s in range(NT):
                    dve.wait_ge(S["low_psum"], s + 1)
                    for k in range(2):
                        v.bn_stats(st4[:, 2 * s + k, :], ps[:, 2 + s % 2, k * LOW:(k + 1) * LOW]).then_inc(S["lstats_ready"], 1)
                    for k in range(2):
                        dve.wait_ge(S["lstats_ready"], 2 * s + k + 1)
                        v.bn_aggr(mv4[:, 2 * s + k, :], st4[:, 2 * s + k, :]).then_inc(S["laggr_ready"], 1)
                    dve.wait_ge(S["lrstd_ready"], s + 1)
                    for k in range(2):
                        c = 2 * s + k
                        v.tensor_scalar(CN[:, s, k * LOW:(k + 1) * LOW], ps[:, 2 + s % 2, k * LOW:(k + 1) * LOW], mv4[:, c, 0:1], rs4[:, c:c + 1],
                                        ALU.subtract, ALU.mult).then_inc(S["cn_ready"], 1)
                for j in range(1, 8, 2):
                    dve.wait_ge(S["upq_psum"], j + 1)
                    v.tensor_copy(QT4[:, j % 4, (j // 4) * 512:(j // 4 + 1) * 512], ps[:, 2 + j % 4, :]).then_inc(S["upqd_ready"], 1)
                v.memset(V4[:, :, :, HD:HD + 1], 1.0).then_inc(S["upqd_ready"], 1)

                def keys_d(n):
                    dve.wait_ge(S["kup_psum"], n + 1)
                    b, half = n // 2, n % 2
                    for r in range(2, 4):
                        v.tensor_copy(KB4[32 * r:32 * r + 32, b % 2, 2 * half:2 * half + 2, r, :],
                                      ps[32 * r:32 * r + 32, 7, :].rearrange("p (g c) -> p g c", g=2)).then_inc(S["kupd_ready"], 1)

                dve.wait_ge(S["kb_zero"], 2)
                keys_d(0)
                keys_d(1)
                for s in range(U4 + 2):
                    if s % 8 in (3, 6) and s < 24:
                        keys_d(2 * (s // 8 + 1) + (s % 8) // 6)
                    if s < U4:
                        dve.wait_ge(S["s4_psum"], s + 1)
                        sc = ps[:, 2 * (s % 2):2 * (s % 2) + 2, :]
                        v.tensor_reduce(m4[:, s % 2, 0, :], sc[:, :, 0:P], AX.X, ALU.max).then_inc(S["max4_ready"], 1)
                        v.tensor_reduce(m4[:, s % 2, 1, :], sc[:, :, P:3 * P], AX.X, ALU.max).then_inc(S["max4_ready"], 1)
                        if s >= 2:
                            dve.wait_ge(S["p4T_psum"], s - 1)
                        for q, (lo, hi) in enumerate(((0, P), (P, 3 * P))):
                            dve.wait_ge(S["max4_ready"], 2 * s + q + 1)
                            v.tensor_tensor(E4[:, s % 2, :, lo:hi], sc[:, :, lo:hi], m4[:, s % 2, q, :].unsqueeze(2).to_broadcast([P, 2, hi - lo]),
                                            ALU.subtract).then_inc(S["sub4_ready"], 1)
                    if s >= 2:
                        u = s - 2
                        b, hp = u // 8, u % 8
                        dve.wait_ge(S["o4_psum"], u + 1)
                        o = ps[:, 6, 0:68].rearrange("p (a c) -> p a c", c=17)
                        v.reciprocal(r4[:, u % 2, :], o[:, :, 16]).then_inc(S["r4_ready"], 1)
                        dve.wait_ge(S["r4_ready"], u + 1)
                        v.tensor_tensor(AT[:, 2 * b:2 * b + 2, 2 * hp * HD:(2 * hp + 2) * HD].rearrange("p t (j c) -> p j t c", c=HD),
                                        o[:, :, 0:HD].rearrange("p (j t) c -> p j t c", t=2),
                                        r4[:, u % 2, :].rearrange("p (j t) -> p j t", t=2).unsqueeze(3).to_broadcast([P, 2, 2, HD]), ALU.mult).then_inc(S["o4_ready"], 1)
                for s in range(NT):
                    residual(s, s, 2 + s % 2, S["proj_psum"], NT + s + 1)
            if stages >= 5:
                norm(4, 3 * NT)
                for s in range(NT):
                    dve.wait_ge(S["q5_psum"], s + 1)
                    v.tensor_tensor(AT[:, s, :], ps[:, 2 + s % 2, 0:D], bqr[:, :], ALU.add).then_inc(S["uq5_ready"], 1)
                dve.wait_ge(S["uq5_ready"], NT)
                heads_view = AT[:, :, :].rearrange("p t (h d) -> p (t h) d", d=HD)
                v.tensor_reduce(sq5[:, :, :].rearrange("p t h -> p (t h)"), heads_view, AX.X, ALU.max, apply_absolute_value=True).then_inc(S["q5_step"], 1)
                dve.wait_ge(S["q5_step"], 1)
                v.tensor_scalar(sq5[:, :, :], sq5[:, :, :], 0.25 / 127, 1e-8, ALU.mult, ALU.max).then_inc(S["q5_step"], 1)
                dve.wait_ge(S["q5_step"], 2)
                v.reciprocal(rq5[:, :, :], sq5[:, :, :]).then_inc(S["q5_step"], 1)
                dve.wait_ge(S["q5_step"], 3)
                v.tensor_scalar(rq5[:, :, :], rq5[:, :, :], 0.25, None, ALU.mult).then_inc(S["q5_step"], 1)
                dve.wait_ge(S["q5_step"], 4)
                v.tensor_tensor(heads_view, heads_view, rq5[:, :, :].rearrange("p t h -> p (t h)").unsqueeze(2).to_broadcast([P, NT * H, HD]), ALU.mult).then_inc(S["q5_step"], 1)
                dve.wait_ge(S["q5_step"], 5)
                dve.wait_ge(S["k5T_psum"], H)
                for a in range(3):
                    v.tensor_scalar(QI3[:, :, :, a, :].rearrange("p t h d -> p (t h) d"), heads_view, ROUND, -ROUND, ALU.add, ALU.add).then_inc(S["q5i_ready"], 1)
                dve.wait_ge(S["pad5_ready"], 4)
                for h in range(H):
                    dve.wait_ge(S["q5T_psum"], h + 1)
                    v.tensor_copy(QT5[0:48, h, :], ps[0:48, 6 + h % 2, :].bitcast(BF16)).then_inc(S["q5T_ready"], 1)

                def softmax(g, first, last=False):
                    for i in range(STEPS if not last else LAG5):
                        h, q = 2 * g + i // NT, i % NT
                        n = h * NT + q
                        if not last:
                            dve.wait_ge(S["s5_psum"], n + 1)
                            wait_pos(dve, S["exp5_ready"], n - 3)
                            v.tensor_reduce(nm5[:, q % 4:q % 4 + 1], ps[:, 2 * (q % 2):2 * (q % 2) + 2, :].rearrange("p a c -> p (a c)"), AX.X, ALU.max, negate=True).then_inc(S["max5_ready"], 1)
                        if i % 2 == 1 and not (first and i < 4) and not (last and i >= 4):
                            m = n - 4
                            dve.wait_ge(S["p5T_psum"], m + 1)
                            wait_pos(dve, S["p5V_done"], m - 1)
                            v.tensor_copy(PT5[:, 1, :, :], ps[:, 5, :].bitcast(BF16).rearrange("p (k c) -> p k c", k=8)).then_inc(S["p5To_ready"], 1)
                        if not last:
                            dve.wait_ge(S["max5_ready"], n + 1)
                            v.tensor_scalar(b5[:, q % 4:q % 4 + 1], nm5[:, q % 4:q % 4 + 1], sq5[:, q, bass.ds(h, 1)], LN255, ALU.mult, ALU.add).then_inc(S["bias5_ready"], 1)
                        if not (first and i < 1) and not (last and i >= 1):
                            dve.wait_ge(S["exp5_ready"], n)
                            wait_pos(dve, S["p5T_psum"], n - 4)
                            v.tensor_copy(PI5[:, (i - 1) % 4, :], Y5[:, (i - 1) % 2, :]).then_inc(S["pi5_ready"], 1)
                        if i % NT == 6 and not (first and i < NT) and not last:
                            outputs(2 * g + i // NT - 1, (i // NT - 1) % 2)

                def outputs(h, bank):
                    dve.wait_ge(S["p5V_done"], (h + 1) * NT)
                    v.reciprocal(r5[:, :], sum5[:, bass.ds(h * NT, NT)]).then_inc(S["r5_ready"], 1)
                    dve.wait_ge(S["r5_ready"], h + 1)
                    v.tensor_tensor(AT[:, :, bass.ds(h * HD, HD)], ps[:, 6 + bank, 0:P].rearrange("p (t c) -> p t c", t=NT),
                                    r5[:, :].unsqueeze(2).to_broadcast([P, NT, HD]), ALU.mult).then_inc(S["o5_ready"], 1)

                softmax(0, True)
                with v.Fori(1, H // 2) as g:
                    softmax(g, False)
                softmax(H // 2, False, True)
                outputs(H - 1, 1)
                dve.wait_ge(S["o5_ready"], H)
                v.tensor_tensor(AT[:, :, :], AT[:, :, :], svrow[:, 0:2, :].rearrange("p k c -> p (k c)").unsqueeze(1).to_broadcast([P, NT, D]), ALU.mult).then_inc(S["out5_ready"], 1)
                for s in range(NT):
                    if s == 0:
                        dve.wait_ge(S["xbias_ready"], NT)
                    residual(s, s, 2 + s % 2, S["proj_psum"], 2 * NT + s + 1)
            if stages >= 6:
                norm(5, 4 * NT)
                c6 = [0]

                def step(inst):
                    inst.then_inc(S["step6"], 1)
                    c6[0] += 1
                    dve.wait_ge(S["step6"], c6[0])

                dve.wait_ge(S["lg_psum"], 1)
                lg = ps[:, 2, :].rearrange("p (t e) -> p t e", t=NT)
                per_tile = lambda a, n: a.unsqueeze(2).to_broadcast([P, NT, n])
                step(v.tensor_reduce(s6[:, 0, :], lg, AX.X, ALU.max))
                step(v.tensor_tensor(L6[:, :, :], lg, per_tile(s6[:, 0, :], NROUTE), ALU.subtract))
                dve.wait_ge(S["exp6_ready"], 1)
                step(v.tensor_reduce(s6[:, 1, :], L6[:, :, :], AX.X, ALU.add))
                step(v.reciprocal(s6[:, 1, :], s6[:, 1, :]))
                step(v.tensor_tensor(L6[:, :, :], L6[:, :, :], per_tile(s6[:, 1, :], NROUTE), ALU.mult))
                step(v.tensor_tensor(BI6[:, :, :], L6[:, :, :], rbias[:, :].unsqueeze(1).to_broadcast([P, NT, NROUTE]), ALU.add))
                for t in range(NT):
                    step(v.max(top6[:, t, :], BI6[:, t, :]))
                for t in range(NT):
                    step(v.match_replace(RP6[:, t, :], top6[:, t, :], BI6[:, t, :], NEG))
                step(v.tensor_tensor(MK6[:, :, :], BI6[:, :, :], RP6[:, :, :], ALU.not_equal))
                step(v.tensor_copy(mr6[:, :, :], MK6[:, :, 0:NE]))
                step(v.memset(cum6[:, 0, :], 0.0))
                for t in range(1, NT):
                    step(v.tensor_tensor(cum6[:, t, :], cum6[:, t - 1, :], mr6[:, t - 1, :], ALU.add))
                dve.sem_inc(S["cnt6_ready"], 1)
                step(v.tensor_tensor(L6[:, :, :], L6[:, :, :], MK6[:, :, :], ALU.mult))
                step(v.tensor_reduce(s6[:, 2, :], L6[:, :, :], AX.X, ALU.add))
                step(v.tensor_scalar(s6[:, 2, :], s6[:, 2, :], 1e-20, None, ALU.add))
                step(v.reciprocal(s6[:, 2, :], s6[:, 2, :]))
                step(v.tensor_scalar(s6[:, 2, :], s6[:, 2, :], 1.5, None, ALU.mult))
                step(v.tensor_tensor(L6[:, :, :], L6[:, :, :], per_tile(s6[:, 2, :], NROUTE), ALU.mult))
                step(v.tensor_reduce(s6[:, 3, :], L6[:, :, NE:NROUTE], AX.X, ALU.add))
                step(v.tensor_scalar(s6[:, 3, :], s6[:, 3, :], 1.0, None, ALU.add))
                step(v.tensor_tensor(L6[:, :, 0:NE], L6[:, :, 0:NE], per_tile(s6[:, 3, :], NE), ALU.mult))
                dve.wait_ge(S["pos6_psum"], 1)
                pos = ps[:, 3, 0:NT * NE].rearrange("p (t e) -> p t e", t=NT)
                step(v.scalar_tensor_tensor(va6[:, :, :], pos, float(CAP), mr6[:, :, :], ALU.is_lt, ALU.mult))
                step(v.tensor_tensor(key6[:, :, :], base6[:, :].unsqueeze(1).to_broadcast([P, NT, NE]), pos, ALU.subtract))
                step(v.tensor_tensor(key6[:, :, :], key6[:, :, :], va6[:, :, :], ALU.mult))
                for t in range(NT):
                    step(v.max(keys6[:, t, :], key6[:, t, :]))
                step(v.tensor_scalar(idxf[:, :, :], keys6[:, :, :], -1.0, 2.0 * SLOTS, ALU.mult, ALU.add))
                flat = idxf[:, :, :].rearrange("p t k -> p (t k)")
                step(v.tensor_copy(idx_put[:, :], flat))
                step(v.tensor_scalar(idx_get[:, :], flat, float(SLOTS), None, ALU.min))
                dve.sem_inc(S["idx_ready"], 1)
                for t in range(NT):
                    step(v.tensor_tensor(eq6[:, t, :, :], key6[:, t, :].unsqueeze(1).to_broadcast([P, 8, NE]), keys6[:, t, :].unsqueeze(2).to_broadcast([P, 8, NE]), ALU.is_equal))
                    step(v.tensor_tensor(eq6[:, t, :, :], eq6[:, t, :, :], L6[:, t, 0:NE].unsqueeze(1).to_broadcast([P, 8, NE]), ALU.mult))
                step(v.tensor_reduce(wk6[:, :, :], eq6, AX.X, ALU.add))
                for s in range(NE + 1):
                    if s < NE:
                        dve.wait_ge(S["silu_ready"], s + 1)
                        if s >= 2:
                            dve.wait_ge(S["ye_psum"], s - 1)
                        v.tensor_tensor(HE[:, s % 2, :], SG[:, s % 2, :], ps[:, 2 + s % 2, CAP:2 * CAP], ALU.mult).then_inc(S["he_ready"], 1)
                    if s >= 1:
                        e = s - 1
                        dve.wait_ge(S["ye_psum"], e + 1)
                        if e >= 4:
                            dve.wait_ge(ye_stored[e % 4], 16 * (e // 4))
                        v.tensor_copy(YE[:, e % 4, :], ps[:, 4 + e % 2, 0:D]).then_inc(S["ye_ready"], 1)
                for j in range(NT * TOPK):
                    t = j // TOPK
                    dve.wait_ge(yg_loaded[j % YGN], 16 * (j // YGN + 1))
                    dve.wait_ge(S["x_ready"], 8 * 5 + j)
                    v.scalar_tensor_tensor(X[:, t, :], YG[:, j % YGN, :], wk6[:, t, j % TOPK:j % TOPK + 1], X[:, t, :], ALU.mult, ALU.add).then_inc(S["x_ready"], 1)


_ARGS = [("x", None), ("ctx_2048", None), ("ctx_2048", (2, 0, 1)), ("L0_attn_weight_qkv", (1, 0)), ("L0_attn_weight_proj", (1, 0)),
         ("L0_ffn_w1", (1, 0)), ("L0_ffn_w2", (1, 0)), ("L1_attn_W_dq", None), ("L1_attn_W_uq", None), ("L1_attn_q_ln_g", None),
         ("L1_attn_q_ln_b", None), ("L1_attn_W_dkv", None), ("L1_attn_W_ukv", None), ("L1_attn_kv_ln_g", None), ("L1_attn_kv_ln_b", None),
         ("L1_attn_W_o", (1, 0)), ("L1_xattn_Wq", None), ("L1_xattn_bq", None), ("L1_xattn_Wkv", None), ("L1_xattn_bkv", None),
         ("L1_xattn_Wp", None), ("L1_xattn_bp", None), ("L1_ffn_w_cls", (1, 0)), ("L1_ffn_bias", None), ("L1_ffn_w_gate_up", None),
         ("L1_ffn_w_down", None)]
STAGES = 6


def kernel(**inputs):
    import numpy as np
    import concourse.bacc as bacc
    from concourse.bass_utils import run_bass_kernel_spmd

    nc = bacc.Bacc("TRN2", target_bir_lowering=False, num_devices=1)
    arrays, args = {}, []
    for i, (name, order) in enumerate(_ARGS):
        a = np.asarray(inputs[name])
        if order is not None:
            a = a.transpose(order)
        if len(order or ()) == 3:
            a = a.reshape(a.shape[0], -1)
        a = np.ascontiguousarray(a)
        arrays[f"in_{i}"] = a
        args.append(nc.dram_tensor(f"in_{i}", a.shape, mybir.dt.from_np(a.dtype), kind="ExternalInput").ap())
    out = nc.dram_tensor("out_0", (NB, SEQ, D), F32, kind="ExternalOutput").ap()
    decoder_kernel(nc, *args, out, stages=STAGES)
    r = run_bass_kernel_spmd(nc, [arrays], core_ids=[0])
    return r.results[0]["out_0"]
```

```python
import concourse.bass as bass
from concourse import mybir
from contextlib import ExitStack

F32 = mybir.dt.float32
BF16 = mybir.dt.bfloat16
I16 = mybir.dt.int16
U32 = mybir.dt.uint32
ALU = mybir.AluOpType
ACT = mybir.ActivationFunctionType
AX = mybir.AxisListType

P = 128
NB, SEQ, D = 4, 256, 256
NT = NB * SEQ // P
KD = D // P
H, HD = 16, 16
FF = 1024
KF = FF // P
LOW = 64
NE, NROUTE, TOPK, CAP = 32, 64, 8, 128
DUMP = NB * SEQ
ROWS = DUMP + CAP
WS, EG = 16, 4
LEAD, ROWLEAD = 10, 5
ROUND = 12582912.0
NEG = -1.0e30
LN255 = 5.541263545158426
EPS = 1e-5
PARITY_ORDER = [0, 2, 4, 6, 1, 3, 5, 7]
IN_ORDER = list(range(NT))


def decoder_kernel(nc, x_in, ctx_in, ctxT_in, wqkvT_in, wprojT_in, w1T_in, w2T_in, wdq_in, wuq_in, qg_in, qb_in,
                   wdkv_in, wukv_in, kvg_in, kvb_in, woT_in, wq_in, bq_in, wkv_in, bkv_in, wp_in, bp_in,
                   wclsT_in, rbias_in, wgu_in, wdown_in, out):
    es = ExitStack()
    with es:
        def sb(name, shape, dt=F32):
            return es.enter_context(nc.sbuf_tensor(name, shape, dt))

        def sem(name):
            return es.enter_context(nc.semaphore(name))

        x_rows = nc.dram_tensor("x_rows", [ROWS, D], F32, kind="Internal").ap()
        sums = [nc.dram_tensor(f"sums{i}", [ROWS, D], F32, kind="Internal").ap() for i in range(2)]

        ps = es.enter_context(nc.psum_tensor("ps", [P, 8, 512], F32))

        X = sb("X", [P, NT, D])
        XN = sb("XN", [P, NT, D])
        XT = sb("XT", [P, KD, NT * P])
        AT = sb("AT", [P, NT, D])
        stats = sb("stats", [P, NT, 6])
        mv = sb("mv", [P, NT, 2])
        veps = sb("veps", [P, NT])
        rstd = sb("rstd", [P, NT])
        neghalf = sb("neghalf", [P, 16])
        roundc = sb("roundc", [P, 2])
        identf = sb("identf", [P, P])
        identb = sb("identb", [P, P], BF16)
        causal = sb("causal", [P, P], BF16)
        onesf = sb("onesf", [P, P])
        zeros = sb("zeros", [P, 4 * D])
        table = sb("table", [P, 3])

        ctx_sb = sb("ctx_sb", [P, NT, D])
        ctxT = sb("ctxT", [P, KD, NT * P])
        wqkvT = sb("wqkvT", [P, KD, 384])
        wprojT = sb("wprojT", [P, KD, D])
        wdown2 = sb("wdown2", [P, KD, 2 * LOW])
        wupq = sb("wupq", [P, 4, 4, 32])
        wupk = sb("wupk", [P, 4, 4, 32])
        wuv = sb("wuv", [P, D])
        lng = sb("lng", [P, 1])
        lnb = sb("lnb", [P, 1])
        woT = sb("woT", [P, KD, D])
        wq5 = sb("wq5", [P, KD, D])
        wkv5 = sb("wkv5", [P, KD, 2 * D])
        wp5 = sb("wp5", [P, KD, D])
        wclsT = sb("wclsT", [P, KD, NROUTE])
        bqr = sb("bqr", [P, D])
        bkvr = sb("bkvr", [P, 2 * D])
        bpr = sb("bpr", [P, D])
        rbias = sb("rbias", [P, NROUTE])

        A = sb("A", [P, 16384])
        qkv = A[:, 0:3072].rearrange("p (t c) -> p t c", t=NT)
        prod = [A[:, 3072 + 2560 * j:3072 + 2560 * (j + 1)].rearrange("p (s c) -> p s c", s=10) for j in range(2)]
        w1stage = A[:, 8192:10240].rearrange("p (k c) -> p k c", k=KD)
        w2stage = A[:, 10240:12288].rearrange("p (k c) -> p k c", k=KF)
        QT4 = A[:, 0:4096].rearrange("p (g c) -> p g c", g=4)
        KB4 = A[:, 4096:12288].rearrange("p (b g r c) -> p b g r c", b=2, g=4, r=4)
        V4 = A[:, 12288:14464].rearrange("p (t h c) -> p t h c", t=NT, h=H)
        E4 = A[:, 14464:16000].rearrange("p (b j c) -> p b j c", b=2, j=2)
        PT4 = XT[:, :, :].rearrange("p k c -> p (k c)")[:, 0:1536].rearrange("p (b j c) -> p b j c", b=2, j=2)
        CN = A[:, 14464:15488].rearrange("p (t c) -> p t c", t=NT)
        CNT = XN[:, 0:4, :].rearrange("p t c -> p (t c)")
        QT5 = A[:, 0:8192].bitcast(BF16).rearrange("p (h c) -> p h c", h=H)
        KT5 = A[:, 8192:16384].bitcast(BF16).rearrange("p (h c) -> p h c", h=H)
        WG = A[:, 0:512 * WS].rearrange("p (s k c) -> p s k c", s=WS, k=KD)
        WD = A[:, 8192:8192 + 256 * WS].rearrange("p (s c) -> p s c", s=WS)
        XE = A[:, 12288:14336].rearrange("p (s c) -> p s c", s=8)
        XET = A[:, 14336:14848].rearrange("p (s k c) -> p s k c", s=2, k=KD)
        SG = A[:, 14848:15104].rearrange("p (s c) -> p s c", s=2)
        HE = A[:, 15104:15360].rearrange("p (s c) -> p s c", s=2)
        YE = A[:, 15360:16384].rearrange("p (s c) -> p s c", s=4)
        SUM = A[:, 0:2 * NT * D].rearrange("p (a t c) -> p a t c", a=2, t=NT)

        w1t = sb("w1t", [P, KD, FF], BF16)
        w2t = sb("w2t", [P, KF, D], BF16)

        SC = sb("SC", [P, 8, 4, H])
        mx1 = sb("mx1", [P, 8, H])
        rs1 = sb("rs1", [P, 8, H])

        E2 = A[:, 4352:5376].rearrange("p (i e c) -> p i e c", i=2, e=2)
        nm2 = sb("nm2", [P, 2, 2])
        b2 = sb("b2", [P, 2, 2])
        sum2 = sb("sum2", [P, 2, 2])
        r2 = sb("r2", [P, 2, 2])

        wsum = sb("wsum", [P, 2])
        wmean = sb("wmean", [P, 2])
        wrec = sb("wrec", [P, 2])
        w127 = sb("w127", [P, 2])
        am3 = sb("am3", [P, NT])
        qs3 = sb("qs3", [P, NT])
        dq3 = sb("dq3", [P, NT])
        QX = sb("QX", [P, NT, D], BF16)
        QXT = A[:, 4096:4352].bitcast(BF16).rearrange("p (s k c) -> p s k c", s=2, k=KD)
        G3 = A[:, 0:2048].rearrange("p (s c) -> p s c", s=2)
        am3b = sb("am3b", [P, NT])
        qs3b = sb("qs3b", [P, NT])
        dq3b = sb("dq3b", [P, NT])
        QH = A[:, 2048:3072].bitcast(BF16).rearrange("p (s c) -> p s c", s=2)
        QHT = A[:, 3072:4096].bitcast(BF16).rearrange("p (s k c) -> p s k c", s=2, k=KF)

        st4 = sb("st4", [P, 2 * NT, 6])
        mv4 = sb("mv4", [P, 2 * NT, 2])
        ve4 = sb("ve4", [P, 2 * NT])
        rs4 = sb("rs4", [P, 2 * NT])
        m4 = sb("m4", [P, 2, 2, 2])
        r4 = sb("r4", [P, 2, 4])

        KV = sb("KV", [P, NT, 2 * D])
        kmax = sb("kmax", [P, NT, H])
        sk = sb("sk", [P, NT, H])
        rk = sb("rk", [P, NT, H])
        kpart_flat = sb("kpart", [P, NT * H * 3 * HD + P - 3 * HD], BF16)
        kpart = kpart_flat[:, 0:NT * H * 3 * HD].rearrange("p (t h a d) -> p t h a d", t=NT, h=H, a=3)
        ktmp = sb("ktmp", [P, 2, D])
        vmax = sb("vmax", [P, D])
        vm2 = sb("vm2", [P, KD])
        svrv = sb("svrv", [P, 2, KD])
        svb = sb("svb", [P, 4, P])
        svrow = sb("svrow", [P, 4, P])
        VI = sb("VI", [P, NT, D], BF16)
        sq5 = sb("sq5", [P, NT, H])
        rq5 = sb("rq5", [P, NT, H])
        QI3 = kpart
        kv_flat = KV[:, :, :].rearrange("p t c -> p (t c)")
        Y5 = kv_flat[:, 0:1024].bitcast(I16).rearrange("p (b c) -> p b c", b=2)
        PI5 = kv_flat[:, 1024:3072].bitcast(BF16).rearrange("p (b c) -> p b c", b=4)
        PT5 = kv_flat[:, 3072:4096].bitcast(BF16).rearrange("p (b k c) -> p b k c", b=2, k=8)
        sp5 = sb("sp5", [P, NT, 2])
        nm5 = sb("nm5", [P, 4])
        b5 = sb("b5", [P, 4])
        sum5 = sb("sum5", [P, H * NT])
        r5 = sb("r5", [P, NT])

        L6, BI6, RP6, MK6 = (ctx_sb[:, 2 * i:2 * i + 2, :].rearrange("p a (t e) -> p (a t) e", e=NROUTE) for i in range(4))
        s6 = sb("s6", [P, 6, NT])
        top6 = sb("top6", [P, NT, 8])
        mr6 = sb("mr6", [P, NT, NE], BF16)
        lower = sb("lower", [P, P], BF16)
        onesb = sb("onesb", [P, P], BF16)
        iota6 = sb("iota6", [P, CAP], BF16)
        SEL = kv_flat.bitcast(BF16).rearrange("p (s t c) -> p s t c", s=8, t=NT)
        LR = AT[:, 0:4, :].rearrange("p t c -> p (t c)").bitcast(BF16).rearrange("p (t e c) -> p t e c", t=NT, e=NE)
        pos6 = sb("pos6", [P, NT, NE], BF16)
        wr6 = sb("wr6", [P, NT, NE])
        dump6 = sb("dump6", [P, 2])
        empty6 = sb("empty6", [P, 2, EG])
        list6 = sb("list6", [P, 2, EG])
        slot_token = sb("slot_token", [P, NE], U32)
        slot_weight = sb("slot_weight", [P, NE])

        names = """x_loaded w0_loaded ctx_loaded w_loaded w1_loaded w2_loaded low_loaded rows_ready
            const_ready zeros_ready pads_ready rstd_e rstd_ready stats_ready aggr_ready xn_ready x_ready tp_psum tp_ready
            qkv_psum qkv_ready prod0_ready prod1_ready step1 exp1_ready at_ready proj_psum
            kv_psum kv_copied kv_ready kscale_ready kq_step vmax_ready vmaxT_psum vscale_ready vrow_psum vrow_ready vint_ready
            wabs_ready wtot_psum wscale_ready wq_step w_ternary
            s2_psum nm2_ready bias2_ready exp2_ready r2_ready attn2_ready out2_psum
            dq3_step qx_step qx_ready qxT_psum qxT_ready h3_psum gelu_ready am3_step qh_step qh_ready qhT_psum qhT_ready out3_psum
            low_psum lstats_ready laggr_ready lveps lrstd_ready cn_ready cnT_psum cnT_ready upq_psum upqa_ready upqd_ready kb_zero kup_psum kupa_ready kupd_ready v4_psum v4_ready
            s4_psum max4_ready sub4_ready exp4_ready p4T_psum p4T_ready o4_psum r4_ready o4_ready
            q5_psum uq5_ready q5_step q5i_ready q5T_psum dve5T_ready k5T_psum act5T_ready pad5_ready xbias_ready
            s5_psum max5_ready scale5_ready bias5_begun bias5_ready exp5_ready pi5_ready p5T_psum p5Te_ready p5To_ready p5V_done r5_ready o5_ready
            lg_psum step6 exp6_ready router_ready pos6_psum lr_const sel_ready wpart_ready list_psum wlist_psum list_step weight_ready list_ready
            xeT_psum xeT_ready gu_psum silu_ready he_ready ye_psum ye_ready sums_added out_stored""".split()
        S = {n: sem(n) for n in names}
        xe_loaded = [sem(f"xe_loaded{i}") for i in range(8)]
        wg_loaded = [sem(f"wg_loaded{i}") for i in range(8)]
        sums_loaded = [sem(f"sums_loaded{i}") for i in range(NT // 2)]
        ye_added = [sem(f"ye_added{i}") for i in range(2)]

        block = es.enter_context(nc.Block())

        def row(ap):
            return ap.partition_broadcast(P)

        U4 = NB * H // 2
        SUB_READY, P_READY = 10, 13

        STEPS, LAG5 = 2 * NT, 5

        def q_bank(h):
            return 4 + (h + 2) % 4

        def selects(s):
            if s in (0, 1):
                return range(2 * EG + 2 * s, 2 * EG + 2 * s + 2)
            return range(s + LEAD, s + LEAD + 1) if 2 <= s < NE - LEAD else range(0)

        def wait_pos(eng, semaphore, count):
            if not isinstance(count, int) or count > 0:
                eng.wait_ge(semaphore, count)

        def qkv_heads(t, lo, n):
            return qkv[:, t, :].rearrange("p (g c) -> p g c", g=4)[:, :, lo:lo + n]

        def score_products(eng, e, j, done, queries=range(4)):
            for iq in queries:
                eng.wait_ge(S["qkv_ready"], 2 * iq + j + 1)
                for ik in range(iq + 1):
                    q = qkv_heads(2 * iq + j, 0, 64).rearrange("p g (r d) -> p g r d", d=HD)
                    k = qkv_heads(2 * ik + j, 64, HD).unsqueeze(2).to_broadcast([P, 4, 4, HD])
                    o = prod[j][:, iq * (iq + 1) // 2 + ik, :].rearrange("p (g r d) -> p g r d", g=4, d=HD)
                    e.tensor_tensor(o, q, k, ALU.mult).then_inc(done, 1)

        def value_products(eng, e, j, done):
            for iq in range(4):
                for ik in range(iq + 1):
                    w = SC[:, j * 4 + iq, ik, :].rearrange("p (g r) -> p g r", g=4).unsqueeze(3).to_broadcast([P, 4, 4, HD])
                    vv = qkv_heads(2 * ik + j, 80, HD).unsqueeze(2).to_broadcast([P, 4, 4, HD])
                    o = prod[j][:, iq * (iq + 1) // 2 + ik, :].rearrange("p (g r d) -> p g r d", g=4, d=HD)
                    e.tensor_tensor(o, vv, w, ALU.mult).then_inc(done, 1)

        @block.sync
        def _(sp):
            sp.dma_start(X[:, :, :], x_in.rearrange("b (j p) d -> p (b j) d", p=P)).then_inc(S["x_loaded"], 16)
            sp.dma_start(wqkvT[:, :, :], wqkvT_in.rearrange("(k p) c -> p k c", p=P)).then_inc(S["w0_loaded"], 16)
            sp.dma_start(wprojT[:, :, :], wprojT_in.rearrange("(k p) c -> p k c", p=P)).then_inc(S["w0_loaded"], 16)
            sp.dma_start(ctxT[:, :, :], ctxT_in.rearrange("(k p) c -> p k c", p=P)).then_inc(S["ctx_loaded"], 16)
            sp.dma_start(wkv5[:, :, :], wkv_in.rearrange("(k p) c -> p k c", p=P)).then_inc(S["ctx_loaded"], 16)
            sp.dma_start(bkvr[:, :], row(bkv_in)).then_inc(S["ctx_loaded"], 16)
            sp.dma_start(ctx_sb[:, :, :], ctx_in.rearrange("b (j p) d -> p (b j) d", p=P)).then_inc(S["ctx_loaded"], 16)
            sp.dma_start(w1stage, w1T_in.rearrange("(k p) c -> p k c", p=P)).then_inc(S["w1_loaded"], 16)
            sp.dma_start(w2stage, w2T_in.rearrange("(k p) c -> p k c", p=P)).then_inc(S["w2_loaded"], 16)
            sp.dma_start(wdown2[:, :, 0:LOW], wdq_in.rearrange("(k p) c -> p k c", p=P)).then_inc(S["low_loaded"], 16)
            sp.dma_start(wdown2[:, :, LOW:2 * LOW], wdkv_in.rearrange("(k p) c -> p k c", p=P)).then_inc(S["low_loaded"], 16)
            sp.wait_ge(S["pads_ready"], 3)
            sp.dma_start(wupq[0:LOW, :, :, 0:HD].rearrange("p g r c -> p (g r) c"), wuq_in.rearrange("l (h c) -> l h c", c=HD)).then_inc(S["low_loaded"], 16)
            sp.dma_start(wupk[LOW:P, :, :, 0:HD].rearrange("p g r c -> p (g r) c"), wukv_in[:, 0:D].rearrange("l (h c) -> l h c", c=HD)).then_inc(S["low_loaded"], 16)
            sp.dma_start(wuv[LOW:P, :], wukv_in[:, D:2 * D]).then_inc(S["low_loaded"], 16)
            for dst, src in ((lng[0:LOW, :], qg_in), (lng[LOW:P, :], kvg_in), (lnb[0:LOW, :], qb_in), (lnb[LOW:P, :], kvb_in)):
                sp.dma_start(dst, src.rearrange("(p a) -> p a", a=1)).then_inc(S["low_loaded"], 16)
            for dst, src in ((woT, woT_in), (wq5, wq_in), (wp5, wp_in), (wclsT, wclsT_in)):
                sp.dma_start(dst[:, :, :], src.rearrange("(k p) c -> p k c", p=P)).then_inc(S["w_loaded"], 16)
            for dst, src in ((bqr, bq_in), (bpr, bp_in), (rbias, rbias_in)):
                sp.dma_start(dst[:, :], row(src)).then_inc(S["w_loaded"], 16)
            sp.wait_ge(S["zeros_ready"], 1)
            for acc in sums:
                for c in range(DUMP // (4 * P)):
                    sp.dma_start(acc[c * 4 * P:(c + 1) * 4 * P, :].rearrange("(p a) d -> p (a d)", a=4), zeros[:, :]).then_inc(S["rows_ready"], 16)
                sp.dma_start(acc[DUMP:ROWS, :], zeros[:, 0:D]).then_inc(S["rows_ready"], 16)
            sp.dma_start(x_rows[DUMP:ROWS, :], zeros[:, 0:D]).then_inc(S["rows_ready"], 16)

            def load_weights(e):
                sp.dma_start(WG[:, e % WS, :, :], wgu_in[e, :, :].rearrange("(k p) c -> p k c", p=P)).then_inc(wg_loaded[e % 8], 16)
                sp.dma_start(WD[:, e % WS, :], wdown_in[e, :, :]).then_inc(wg_loaded[e % 8], 16)

            sp.wait_ge(S["p5V_done"], H * NT)
            for e in range(8):
                load_weights(e)
            for c in range(2):
                sp.wait_ge(S["xn_ready"], 5 * NT + 4 * (c + 1))
                sp.dma_start(x_rows[c * 4 * P:(c + 1) * 4 * P, :].rearrange("(t p) d -> p t d", p=P), XN[:, 4 * c:4 * c + 4, :]).then_inc(S["rows_ready"], 16)
            for e in range(8, NE):
                sp.wait_ge(wg_loaded[e % 8], 32 * (e // 8))
                if e >= WS:
                    sp.wait_ge(S["ye_psum"], e - WS + 1)
                load_weights(e)
            out_v = out.rearrange("b (j p) d -> p (b j) d", p=P)
            for i in range(2):
                sp.wait_ge(ye_added[i], 16 * (NE // 2))
            for c in range(NT // 2):
                for i in range(2):
                    sp.dma_start(SUM[:, i, 2 * c:2 * c + 2, :], sums[i][c * 2 * P:(c + 1) * 2 * P, :].rearrange("(t p) d -> p t d", p=P)).then_inc(sums_loaded[c], 16)
            for c in range(NT // 2):
                sp.wait_ge(S["x_ready"], 8 * 5 + 2 * (c + 1))
                sp.dma_start(out_v[:, 2 * c:2 * c + 2, :], X[:, 2 * c:2 * c + 2, :]).then_inc(S["out_stored"], 16)
            sp.wait_ge(S["out_stored"], 16 * (NT // 2))

        @block.gpsimd
        def _(pool):
            g = nc.gpsimd
            g.memset(identf[:, :], 0.0).then_inc(S["const_ready"], 1)
            g.memset(identb[:, :], 0.0).then_inc(S["const_ready"], 1)
            g.memset(neghalf[:, :], -0.5).then_inc(S["const_ready"], 1)
            g.memset(onesf[:, :], 1.0).then_inc(S["const_ready"], 1)
            g.memset(causal[:, :], 0.0).then_inc(S["const_ready"], 1)
            g.memset(lower[:, :], 1.0).then_inc(S["const_ready"], 1)
            g.memset(onesb[:, :], 1.0).then_inc(S["const_ready"], 1)
            pool.wait_ge(S["const_ready"], 7)
            for m in (identf, identb):
                g.affine_select(out=m[:, :], in_=m[:, :], compare_op=ALU.not_equal, fill=1.0, base=0,
                                pattern=[[-1, P]], channel_multiplier=1).then_inc(S["const_ready"], 1)
            g.affine_select(out=causal[:, :], in_=causal[:, :], compare_op=ALU.is_ge, fill=NEG, base=0,
                            pattern=[[-1, P]], channel_multiplier=1).then_inc(S["const_ready"], 1)
            g.affine_select(out=lower[:, :], in_=lower[:, :], compare_op=ALU.is_gt, fill=0.0, base=0,
                            pattern=[[1, P]], channel_multiplier=-1).then_inc(S["const_ready"], 1)
            g.iota(iota6[:, :], pattern=[[1, CAP]], base=-256, channel_multiplier=0,
                   allow_small_or_imprecise_dtypes=True).then_inc(S["const_ready"], 1)
            g.iota(dump6[:, 0:1], pattern=[[0, 1]], base=DUMP, channel_multiplier=1,
                   allow_small_or_imprecise_dtypes=True).then_inc(S["const_ready"], 1)
            g.iota(dump6[:, 1:2], pattern=[[0, 1]], base=-DUMP, channel_multiplier=-1,
                   allow_small_or_imprecise_dtypes=True).then_inc(S["const_ready"], 1)
            g.memset(roundc[:, 0:1], ROUND).then_inc(S["const_ready"], 1)
            g.memset(roundc[:, 1:2], -ROUND).then_inc(S["const_ready"], 1)
            g.memset(SC[:, :, :, :], NEG).then_inc(S["const_ready"], 1)
            for pad in (wupq[:, :, :, :], wupk[:, :, :, :], wuv[:, :]):
                g.memset(pad, 0.0).then_inc(S["pads_ready"], 1)
            g.memset(zeros[:, :], 0.0).then_inc(S["zeros_ready"], 1)
            g.memset(kpart_flat[:, NT * H * 3 * HD:], 0.0).then_inc(S["zeros_ready"], 1)

            def norm_rstd(n):
                for s in range(2):
                    tiles = slice(s, NT, 2) if n == 1 else slice(4 * s, 4 * s + 4)
                    pool.wait_ge(S["aggr_ready"], n * NT + 4 * (s + 1))
                    g.tensor_scalar(veps[:, tiles], mv[:, tiles, 1], EPS, None, ALU.add).then_inc(S["rstd_e"], 1)
                    pool.wait_ge(S["rstd_e"], 2 * n + s + 1)
                    g.tensor_tensor(rstd[:, tiles], veps[:, tiles], neghalf[:, 0:4], ALU.pow).then_inc(S["rstd_ready"], 1)

            norm_rstd(0)
            score_products(pool, g, 1, S["prod1_ready"])
            pool.wait_ge(S["step1"], P_READY)
            value_products(pool, g, 1, S["prod1_ready"])
            norm_rstd(1)
            for t in range(NT):
                pool.wait_ge(S["kv_copied"], t + 1)
                g.tensor_tensor(KV[:, t, :], KV[:, t, :], bkvr[:, :], ALU.add).then_inc(S["kv_ready"], 1)
            norm_rstd(2)
            norm_rstd(3)
            for s in range(NT):
                pool.wait_ge(S["laggr_ready"], 2 * (s + 1))
                g.tensor_scalar(ve4[:, 2 * s:2 * s + 2], mv4[:, 2 * s:2 * s + 2, 1], EPS, None, ALU.add).then_inc(S["lveps"], 1)
                pool.wait_ge(S["lveps"], s + 1)
                g.tensor_tensor(rs4[:, 2 * s:2 * s + 2], ve4[:, 2 * s:2 * s + 2], neghalf[:, 0:2], ALU.pow).then_inc(S["lrstd_ready"], 1)
            pool.wait_ge(S["out3_psum"], NT)
            pool.wait_ge(S["w_ternary"], 2)
            for b in range(2):
                g.memset(KB4[:, b, :, :, :], 0.0).then_inc(S["kb_zero"], 1)
            pool.wait_ge(S["vrow_ready"], 1)
            rv = svrow[:, 2:4, :].rearrange("p k c -> p (k c)")
            for t in range(NT):
                g.tensor_tensor(KV[:, t, D:2 * D], KV[:, t, D:2 * D], rv, ALU.mult).then_inc(S["vint_ready"], 1)
                pool.wait_ge(S["vint_ready"], 2 * t + 1)
                g.tensor_scalar(VI[:, t, :], KV[:, t, D:2 * D], ROUND, -ROUND, ALU.add, ALU.add).then_inc(S["vint_ready"], 1)
            for t in range(NT):
                c = 8 * t
                kt = KV[:, t, 0:D].rearrange("p (h d) -> p h d", h=H)
                a = ktmp[:, 0, :].rearrange("p (h d) -> p h d", h=H)
                b = ktmp[:, 1, :].rearrange("p (h d) -> p h d", h=H)
                if t == 0:
                    pool.wait_ge(S["kscale_ready"], 3)
                if t > 0:
                    pool.wait_ge(S["kq_step"], c)
                g.tensor_tensor(a, kt, rk[:, t, :].unsqueeze(2).to_broadcast([P, H, HD]), ALU.mult).then_inc(S["kq_step"], 1)
                pool.wait_ge(S["kq_step"], c + 1)
                g.tensor_scalar(b, a, ROUND, -ROUND, ALU.add, ALU.add).then_inc(S["kq_step"], 1)
                pool.wait_ge(S["kq_step"], c + 2)
                g.tensor_tensor(a, b, sk[:, t, :].unsqueeze(2).to_broadcast([P, H, HD]), ALU.mult).then_inc(S["kq_step"], 1)
                pool.wait_ge(S["kq_step"], c + 3)
                g.tensor_copy(kpart[:, t, :, 0, :], a).then_inc(S["kq_step"], 1)
                pool.wait_ge(S["kq_step"], c + 4)
                g.tensor_tensor(b, a, kpart[:, t, :, 0, :], ALU.subtract).then_inc(S["kq_step"], 1)
                pool.wait_ge(S["kq_step"], c + 5)
                g.tensor_copy(kpart[:, t, :, 1, :], b).then_inc(S["kq_step"], 1)
                pool.wait_ge(S["kq_step"], c + 6)
                g.tensor_tensor(a, b, kpart[:, t, :, 1, :], ALU.subtract).then_inc(S["kq_step"], 1)
                pool.wait_ge(S["kq_step"], c + 7)
                g.tensor_copy(kpart[:, t, :, 2, :], a).then_inc(S["kq_step"], 1)
            norm_rstd(4)
            for t in range(NT):
                pool.wait_ge(S["xn_ready"], 4 * NT + t + 1)
                g.tensor_tensor(X[:, t, :], X[:, t, :], bpr[:, :], ALU.add).then_inc(S["xbias_ready"], 1)
            pool.wait_ge(S["proj_psum"], 2 * NT)
            g.memset(A[:, 0:8192], 0.0).then_inc(S["pad5_ready"], 1)
            def biases(g, first):
                for i in range(STEPS):
                    h, q = 2 * g + i // NT, i % NT
                    n = h * NT + q
                    if i == 0:
                        pool.wait_ge(S["scale5_ready"], g + 1)
                    pool.wait_ge(S["max5_ready"], n + 1)
                    wait_pos(pool, S["exp5_ready"], n - 3)
                    pool.sem_inc(S["bias5_begun"], 1)
                    nc.gpsimd.tensor_scalar(b5[:, q % 4:q % 4 + 1], nm5[:, q % 4:q % 4 + 1], sp5[:, q, i // NT:i // NT + 1], LN255, ALU.mult, ALU.add).then_inc(S["bias5_ready"], 1)

            biases(0, True)
            with g.Fori(1, H // 2) as pair:
                biases(pair, False)
            norm_rstd(5)
            pool.wait_ge(S["tp_psum"], 6 * NT)
            g.iota(LR[:, :, :, 0], pattern=[[0, NT], [0, NE]], base=0, channel_multiplier=1,
                   allow_small_or_imprecise_dtypes=True).then_inc(S["lr_const"], 1)
            g.iota(LR[:, :, :, 1], pattern=[[P, NT], [0, NE]], base=0, channel_multiplier=0,
                   allow_small_or_imprecise_dtypes=True).then_inc(S["lr_const"], 1)
            g.memset(LR[:, :, :, 2], 0.0).then_inc(S["lr_const"], 1)
            g.memset(LR[:, :, :, 3], 1.0).then_inc(S["lr_const"], 1)
            g.memset(LR[:, :, :, 7], 0.0).then_inc(S["lr_const"], 1)

            def gather(e):
                pool.wait_ge(S["list_ready"], e // EG + 1)
                if e >= 8:
                    pool.wait_ge(S["xeT_psum"], e - 7)
                g.indirect_dma_start(out=XE[:, e % 8, :], out_offset=None, in_=x_rows,
                                     in_offset=bass.IndirectOffsetOnAxis(ap=slot_token[:, e:e + 1], axis=0),
                                     bounds_check=ROWS - 1, oob_is_err=True).then_inc(xe_loaded[e % 8], 16)

            pool.wait_ge(S["rows_ready"], 16 * 9)
            for e in range(EG):
                gather(e)
            w = L6[:, :, 0:NE]
            pool.wait_ge(S["wpart_ready"], 1)
            g.tensor_tensor(wr6[:, :, :], w, LR[:, :, :, 4], ALU.subtract).then_inc(S["wpart_ready"], 1)
            pool.wait_ge(S["wpart_ready"], 3)
            g.tensor_tensor(LR[:, :, :, 6], wr6[:, :, :], LR[:, :, :, 5], ALU.subtract).then_inc(S["wpart_ready"], 1)
            for e in range(EG, ROWLEAD):
                gather(e)
            for s in range(NE):
                if s + ROWLEAD < NE:
                    gather(s + ROWLEAD)
                pool.wait_ge(S["ye_ready"], s + 1)
                if s >= 2:
                    pool.wait_ge(ye_added[s % 2], 16 * (s // 2))
                g.indirect_dma_start(out=sums[s % 2], out_offset=bass.IndirectOffsetOnAxis(ap=slot_token[:, s:s + 1], axis=0),
                                     in_=YE[:, s % 4, :], in_offset=None, bounds_check=ROWS - 1,
                                     oob_is_err=True, compute_op=ALU.add).then_inc(ye_added[s % 2], 16)

        @block.scalar
        def _(act):
            a = nc.scalar

            def copy_T(m, s, t):
                act.wait_ge(S["tp_psum"], m * NT + s + 1)
                a.activation(XT[:, :, t * P:(t + 1) * P], ps[:, s % 2, 0:D].rearrange("p (k c) -> p k c", k=KD), ACT.Copy).then_inc(S["tp_ready"], 1)

            for s in range(NT + 1):
                if s < NT:
                    copy_T(0, s, s)
                if s >= 1:
                    act.wait_ge(S["qkv_psum"], s)
                    a.activation(qkv[:, s - 1, :], ps[:, 2 + (s - 1) % 2, 0:384], ACT.Copy).then_inc(S["qkv_ready"], 1)
            for t in range(NT):
                act.wait_ge(S["kv_psum"], t + 1)
                a.activation(KV[:, t, :], ps[:, 4 + t % 2, :], ACT.Copy).then_inc(S["kv_copied"], 1)
                if t == NT // 2:
                    act.wait_ge(S["step1"], SUB_READY)
                    a.activation(SC[:, :, :, :], SC[:, :, :, :], ACT.Exp, scale=0.25).then_inc(S["exp1_ready"], 1)
            act.wait_ge(S["wscale_ready"], 2)
            w_flat = [w1stage.rearrange("p k c -> p (k c)"), w2stage.rearrange("p k c -> p (k c)")]
            for w in range(2):
                a.activation(w_flat[w], w_flat[w], ACT.Identity, scale=wrec[:, w:w + 1], bias=roundc[:, 0:1]).then_inc(S["wq_step"], 1)
            for s in range(NT):
                copy_T(1, s, PARITY_ORDER[s])
            for w in range(2):
                act.wait_ge(S["wq_step"], w + 1)
                a.activation(w_flat[w], w_flat[w], ACT.Identity, bias=roundc[:, 1:2]).then_inc(S["wq_step"], 1)
            for i in range(NB):
                act.wait_ge(S["bias2_ready"], i + 1)
                if i >= 2:
                    act.wait_ge(S["out2_psum"], i - 1)
                for e in range(2):
                    a.activation(E2[:, i % 2, e, :], ps[:, 2 + i % 2, e * D:(e + 1) * D], ACT.Exp, scale=1.0 / 16, bias=b2[:, i % 2, e:e + 1],
                                 accum_out=sum2[:, i % 2, e:e + 1]).then_inc(S["exp2_ready"], 1)
            a.activation(table[:, 0:1], neghalf[:, 0:1], ACT.Gelu_apprx_tanh)
            for s in range(NT + 2):
                if s < NT:
                    act.wait_ge(S["qxT_psum"], s + 1)
                    a.activation(QXT[:, s % 2, :, :], ps[:, s % 2, 0:P].bitcast(BF16).rearrange("p (k c) -> p k c", k=KD), ACT.Copy).then_inc(S["qxT_ready"], 1)
                if 1 <= s <= NT:
                    u = s - 1
                    act.wait_ge(S["h3_psum"], u + 1)
                    if u >= 2:
                        act.wait_ge(S["qh_step"], 2 * (u - 1))
                    a.activation(G3[:, u % 2, :], ps[:, 2 + 2 * (u % 2):4 + 2 * (u % 2), :], ACT.Gelu_apprx_tanh,
                                 scale=dq3[:, u:u + 1]).then_inc(S["gelu_ready"], 1)
                if s >= 2:
                    u = s - 2
                    act.wait_ge(S["qhT_psum"], u + 1)
                    a.activation(QHT[:, u % 2, :, :], ps[:, 6, :].bitcast(BF16).rearrange("p (k c) -> p k c", k=KF), ACT.Copy).then_inc(S["qhT_ready"], 1)
            a.activation(table[:, 1:2], neghalf[:, 0:1], ACT.Exp)
            for s in range(NT):
                copy_T(2, s, s)
            for s in range(NT):
                act.wait_ge(S["cnT_psum"], s + 1)
                a.activation(CNT[:, s * P:(s + 1) * P], ps[:, s % 2, 0:P], ACT.Identity, scale=lng[:, 0:1], bias=lnb[:, 0:1]).then_inc(S["cnT_ready"], 1)
            for j in range(0, 8, 2):
                act.wait_ge(S["upq_psum"], j + 1)
                a.activation(QT4[:, j % 4, (j // 4) * 512:(j // 4 + 1) * 512], ps[:, 2 + j % 4, :], ACT.Copy).then_inc(S["upqa_ready"], 1)

            def keys_a(n):
                act.wait_ge(S["kup_psum"], n + 1)
                b, half = n // 2, n % 2
                if n == 0:
                    act.wait_ge(S["kb_zero"], 2)
                for r in range(2):
                    a.activation(KB4[32 * r:32 * r + 32, b % 2, 2 * half:2 * half + 2, r, :], ps[32 * r:32 * r + 32, 7, :].rearrange("p (g c) -> p g c", g=2),
                                 ACT.Copy).then_inc(S["kupa_ready"], 1)

            for t in range(NT):
                act.wait_ge(S["v4_psum"], t + 1)
                a.activation(V4[:, t, :, 0:HD], ps[:, 2 + t % 2, 0:D].rearrange("p (h c) -> p h c", h=H), ACT.Copy).then_inc(S["v4_ready"], 1)
            keys_a(0)
            act.wait_ge(S["vrow_psum"], 1)
            a.activation(svrow[:, :, :], ps[:, 5, :].rearrange("p (a c) -> p a c", a=4), ACT.Copy).then_inc(S["vrow_ready"], 1)
            keys_a(1)
            for s in range(U4 + 1):
                if s % 8 in (3, 6) and s < 24:
                    keys_a(2 * (s // 8 + 1) + (s % 8) // 6)
                if s < U4:
                    act.wait_ge(S["sub4_ready"], 2 * (s + 1))
                    a.activation(E4[:, s % 2, :, :], E4[:, s % 2, :, :], ACT.Exp, scale=0.25).then_inc(S["exp4_ready"], 1)
                if s >= 1:
                    u = s - 1
                    act.wait_ge(S["p4T_psum"], u + 1)
                    if u >= 2:
                        act.wait_ge(S["o4_psum"], u - 1)
                    a.activation(PT4[:, u % 2, :, :], ps[:, 4:6, 0:384], ACT.Copy).then_inc(S["p4T_ready"], 1)
            for s in range(NT):
                copy_T(3, s, s)
            def keys_out(lo, hi):
                for h in range(lo, hi):
                    act.wait_ge(S["k5T_psum"], h + 1)
                    a.activation(KT5[:, h, :], ps[:, 4 + h % 2, :].bitcast(BF16), ACT.Copy).then_inc(S["act5T_ready"], 1)

            keys_out(0, 7)
            for s in range(NT):
                copy_T(4, s, s)
            keys_out(7, H)
            act.wait_ge(S["pad5_ready"], 1)
            for h in range(0, H, 2):
                act.wait_ge(S["q5T_psum"], h + 1)
                a.activation(QT5[0:48, h, :], ps[0:48, q_bank(h), :].bitcast(BF16), ACT.Copy).then_inc(S["act5T_ready"], 1)

            def exps(g, first, last=False):
                for i in range(STEPS if not last else LAG5):
                    h, q = 2 * g + i // NT, i % NT
                    n = h * NT + q
                    if i % 2 == 0 and not (first and i < 4) and not (last and i >= 4):
                        m = n - 4
                        act.wait_ge(S["p5T_psum"], m + 1)
                        wait_pos(act, S["p5V_done"], m - 1)
                        a.activation(PT5[:, 0, :, :], ps[:, 4, :].bitcast(BF16).rearrange("p (k c) -> p k c", k=8), ACT.Copy).then_inc(S["p5Te_ready"], 1)
                    if not last:
                        act.wait_ge(S["bias5_ready"], n + 1)
                        wait_pos(act, S["pi5_ready"], n - 1)
                        a.activation(Y5[:, q % 2, :], ps[:, 2 * (q % 2):2 * (q % 2) + 2, :], ACT.Exp, scale=sq5[:, q, bass.ds(h, 1)],
                                     bias=b5[:, q % 4:q % 4 + 1], accum_out=sum5[:, bass.ds(n, 1)]).then_inc(S["exp5_ready"], 1)

            exps(0, True)
            with a.Fori(1, H // 2) as g:
                exps(g, False)
            exps(H // 2, False, True)
            for s in range(NT):
                copy_T(5, s, s)
            for s in range(NT):
                copy_T(6, s, s)
            act.wait_ge(S["step6"], 2)
            a.activation(L6[:, :, :], L6[:, :, :], ACT.Exp).then_inc(S["exp6_ready"], 1)
            a.activation(table[:, 2:3], neghalf[:, 0:1], ACT.Silu)
            act.wait_ge(S["router_ready"], 2)
            a.activation(LR[:, :, :, 4], L6[:, :, 0:NE], ACT.Copy).then_inc(S["wpart_ready"], 1)
            act.wait_ge(S["wpart_ready"], 2)
            a.activation(LR[:, :, :, 5], wr6[:, :, :], ACT.Copy).then_inc(S["wpart_ready"], 1)
            for s in range(NE + 2):
                if s < NE:
                    act.wait_ge(S["xeT_psum"], s + 1)
                    if s >= 2:
                        act.wait_ge(S["gu_psum"], s - 1)
                    a.activation(XET[:, s % 2, :, :], ps[:, s % 2, 0:D].rearrange("p (k c) -> p k c", k=KD), ACT.Copy).then_inc(S["xeT_ready"], 1)
                if 1 <= s <= NE:
                    e = s - 1
                    act.wait_ge(S["gu_psum"], e + 1)
                    if e >= 2:
                        act.wait_ge(S["he_ready"], e - 1)
                    a.activation(SG[:, e % 2, :], ps[:, 2 + e % 2, 0:CAP], ACT.Silu).then_inc(S["silu_ready"], 1)
                if s >= 2:
                    e = s - 2
                    act.wait_ge(S["ye_psum"], e + 1)
                    act.wait_ge(S["weight_ready"], e // EG + 1)
                    if e >= 4:
                        act.wait_ge(ye_added[e % 2], 16 * (e // 2 - 1))
                    a.activation(YE[:, e % 4, :], ps[:, 4 + e % 2, 0:D], ACT.Copy, scale=slot_weight[:, e:e + 1]).then_inc(S["ye_ready"], 1)

        @block.tensor
        def _(pe):
            T = nc.tensor
            pe.wait_ge(S["const_ready"], 17)

            def to_T(m, s, src, ready, count):
                c = m * NT + s + 1
                pe.wait_ge(ready, count)
                if c > 2:
                    pe.wait_ge(S["tp_ready"], c - 2)
                for k in range(KD):
                    last = T.transpose(ps[:, s % 2, k * P:(k + 1) * P], src[:, k * P:(k + 1) * P], identf[:, :])
                last.then_inc(S["tp_psum"], 1)

            def project(m, s, t, bank, w, n, done, free, free_count):
                pe.wait_ge(S["tp_ready"], m * NT + s + 1)
                if free is not None and free_count > 0:
                    pe.wait_ge(free, free_count)
                for k in range(KD):
                    last = T.matmul(ps[:, bank, 0:n], XT[:, k, t * P:(t + 1) * P], w[:, k, 0:n], start=(k == 0), stop=(k == KD - 1))
                last.then_inc(done, 1)

            for s in range(NT + 1):
                if s < NT:
                    to_T(0, s, XN[:, s, :], S["xn_ready"], s + 1)
                if s >= 1:
                    if s == 1:
                        pe.wait_ge(S["w0_loaded"], 32)
                    project(0, s - 1, s - 1, 2 + (s - 1) % 2, wqkvT, 384, S["qkv_psum"], S["qkv_ready"], s - 2)
            pe.wait_ge(S["ctx_loaded"], 64)
            for t in range(NT):
                if t == 3:
                    pe.wait_ge(S["wabs_ready"], 2)
                    T.matmul(ps[:, 6, 0:2], onesf[:, :], wsum[:, :], start=True, stop=True).then_inc(S["wtot_psum"], 1)
                if t >= 2:
                    pe.wait_ge(S["kv_copied"], t - 1)
                for k in range(KD):
                    last = T.matmul(ps[:, 4 + t % 2, :], ctxT[:, k, t * P:(t + 1) * P], wkv5[:, k, :], start=(k == 0), stop=(k == KD - 1))
                last.then_inc(S["kv_psum"], 1)
            for s in range(NT + 1):
                if s < NT:
                    to_T(1, s, AT[:, PARITY_ORDER[s], :], S["at_ready"], s + 1)
                if s >= 1:
                    project(1, s - 1, PARITY_ORDER[s - 1], 2 + (s - 1) % 2, wprojT, D, S["proj_psum"], S["x_ready"], s - 2)
            for s in range(NB + 2):
                if s < NB:
                    pe.wait_ge(S["xn_ready"], NT + 4 + s + 1)
                    pe.wait_ge(S["x_ready"], NT)
                    if s >= 2:
                        pe.wait_ge(S["exp2_ready"], 2 * (s - 1))
                    for e in range(2):
                        for j in range(2):
                            last = T.matmul(ps[:, 2 + s % 2, e * D:(e + 1) * D], ctx_sb[:, 2 * s + j, e * P:(e + 1) * P], XN[:, 2 * s + j, :], start=(j == 0), stop=(j == 1))
                    last.then_inc(S["s2_psum"], 1)
                if s >= 2:
                    i = s - 2
                    pe.wait_ge(S["attn2_ready"], 2 * (i + 1))
                    if i >= 2:
                        pe.wait_ge(S["x_ready"], NT + 2 * (i - 1))
                    for j in range(2):
                        for e in range(2):
                            last = T.matmul(ps[:, 4 + i % 2, j * D:(j + 1) * D], ctxT[:, e, i * SEQ + j * P:i * SEQ + (j + 1) * P], E2[:, i % 2, e, :], start=(e == 0), stop=(e == 1))
                    last.then_inc(S["out2_psum"], 1)
            pe.wait_ge(S["w_ternary"], 2)
            for s in range(NT + 2):
                if s < NT:
                    pe.wait_ge(S["qx_ready"], s + 1)
                    if s >= 2:
                        pe.wait_ge(S["qxT_ready"], s - 1)
                    for k in range(KD):
                        last = T.transpose(ps[:, s % 2, k * 64:(k + 1) * 64].bitcast(BF16), QX[:, s, k * P:(k + 1) * P], identb[:, :])
                    last.then_inc(S["qxT_psum"], 1)
                    pe.wait_ge(S["qxT_ready"], s + 1)
                    if s >= 2:
                        pe.wait_ge(S["gelu_ready"], s - 1)
                    elif s == 0:
                        pe.wait_ge(S["x_ready"], 2 * NT)
                    for n in range(2):
                        for k in range(KD):
                            last = T.matmul(ps[:, 2 + 2 * (s % 2) + n, :], QXT[:, s % 2, k, :], w1t[:, k, n * 512:(n + 1) * 512], start=(k == 0), stop=(k == KD - 1))
                    last.then_inc(S["h3_psum"], 1)
                if s >= 2:
                    u = s - 2
                    pe.wait_ge(S["qh_ready"], u + 1)
                    if u >= 1:
                        pe.wait_ge(S["qhT_ready"], u)
                    for k in range(KF):
                        last = T.transpose(ps[:, 6, k * 64:(k + 1) * 64].bitcast(BF16), QH[:, u % 2, k * P:(k + 1) * P], identb[:, :])
                    last.then_inc(S["qhT_psum"], 1)
                    pe.wait_ge(S["qhT_ready"], u + 1)
                    if u >= 1:
                        pe.wait_ge(S["x_ready"], 2 * NT + u)
                    for k in range(KF):
                        last = T.matmul(ps[:, 7, 0:D], QHT[:, u % 2, k, :], w2t[:, k, :], start=(k == 0), stop=(k == KF - 1))
                    last.then_inc(S["out3_psum"], 1)
            pe.wait_ge(S["low_loaded"], 16 * 9)
            for s in range(NT + 1):
                if s < NT:
                    to_T(2, s, XN[:, s, :], S["xn_ready"], 3 * NT + s + 1)
                if s >= 1:
                    project(2, s - 1, s - 1, 2 + (s - 1) % 4, wdown2, 2 * LOW, S["low_psum"], S["cn_ready"], 2 * (s - 4))
            for s in range(NT):
                pe.wait_ge(S["cn_ready"], 2 * (s + 1))
                if s >= 2:
                    pe.wait_ge(S["cnT_ready"], s - 1)
                T.transpose(ps[:, s % 2, 0:P], CN[:, s, :], identf[:, :]).then_inc(S["cnT_psum"], 1)
            for j in range(8):
                half, g = j // 4, j % 4
                if j in (0, 4):
                    pe.wait_ge(S["cnT_ready"], 4 * (half + 1))
                if j == 0:
                    pe.wait_ge(S["cn_ready"], 2 * NT)
                if j >= 4:
                    pe.wait_ge(S[("upqa_ready", "upqd_ready")[j % 2]], j // 2 - 1)
                T.matmul(ps[:, 2 + j % 4, :], wupq[:, g, :, :].rearrange("p r c -> p (r c)"), CNT[:, half * 512:(half + 1) * 512],
                         start=True, stop=True).then_inc(S["upq_psum"], 1)
            pe.wait_ge(S["vmax_ready"], 1)
            for k in range(KD):
                last = T.transpose(ps[:, 6, k * P:(k + 1) * P], vmax[:, k * P:(k + 1) * P], identf[:, :])
            last.then_inc(S["vmaxT_psum"], 1)
            for t in range(NT):
                if t < 2:
                    pe.wait_ge(S[("upqa_ready", "upqd_ready")[t]], 3)
                if t >= 2:
                    pe.wait_ge(S["v4_ready"], t - 1)
                T.matmul(ps[:, 2 + t % 2, 0:D], CNT[:, t * P:(t + 1) * P], wuv[:, :], start=True, stop=True).then_inc(S["v4_psum"], 1)

            pe.wait_ge(S["vscale_ready"], 4)
            for a in range(2):
                for k in range(KD):
                    last = T.matmul(ps[:, 5, (a * KD + k) * P:(a * KD + k + 1) * P], svb[:, a * KD + k, :], identf[:, :], start=True, stop=True)
            last.then_inc(S["vrow_psum"], 1)

            def keys_up(n):
                b, half = n // 2, n % 2
                if n >= 1:
                    pe.wait_ge(S["kupa_ready"], 2 * n)
                    pe.wait_ge(S["kupd_ready"], 2 * n)
                for g in range(2):
                    done = T.matmul(ps[:, 7, g * SEQ:(g + 1) * SEQ], wupk[:, 2 * half + g, :, :].rearrange("p r c -> p (r c)"), CNT[:, b * SEQ:(b + 1) * SEQ],
                                    start=True, stop=True)
                done.then_inc(S["kup_psum"], 1)

            keys_up(0)
            keys_up(1)
            for s in range(U4 + 2):
                if s < U4:
                    b, hp = s // 8, s % 8
                    if s == 0:
                        pe.wait_ge(S["upqa_ready"], 4)
                        pe.wait_ge(S["upqd_ready"], 5)
                        pe.wait_ge(S["v4_ready"], NT)
                    if hp == 0:
                        pe.wait_ge(S["kupa_ready"], 4 * (b + 1))
                        pe.wait_ge(S["kupd_ready"], 4 * (b + 1))
                    if hp in (2, 5) and b < NB - 1:
                        if hp == 2 and b >= 1:
                            pe.wait_ge(S["s4_psum"], 8 * b)
                        keys_up(2 * (b + 1) + hp // 5)
                    if s >= 2:
                        pe.wait_ge(S["sub4_ready"], 2 * (s - 1))
                    for j in range(2):
                        hh = 2 * hp + j
                        bank = 2 * (s % 2) + j
                        q = QT4[:, hh // 4, b * SEQ:(b + 1) * SEQ]
                        k = KB4[:, b % 2, hh // 4, hh % 4, :]
                        T.matmul(ps[:, bank, 0:P], q[:, 0:P], k[:, 0:P], start=True, stop=False)
                        T.matmul(ps[:, bank, 0:P], identb[:, :], causal[:, :], start=False, stop=True)
                        T.matmul(ps[:, bank, P:3 * P], q[:, P:2 * P], k[:, :], start=True, stop=False)
                        last = T.matmul(ps[:, bank, 2 * P:3 * P], identb[:, :], causal[:, :], start=False, stop=True)
                    last.then_inc(S["s4_psum"], 1)
                if 1 <= s <= U4:
                    u = s - 1
                    pe.wait_ge(S["exp4_ready"], u + 1)
                    if u >= 1:
                        pe.wait_ge(S["p4T_ready"], u)
                    for j in range(2):
                        for m in range(3):
                            last = T.transpose(ps[:, 4 + j, m * P:(m + 1) * P], E4[:, u % 2, j, m * P:(m + 1) * P], identf[:, :])
                    last.then_inc(S["p4T_psum"], 1)
                if s >= 2:
                    u = s - 2
                    b, hp = u // 8, u % 8
                    pe.wait_ge(S["p4T_ready"], u + 1)
                    if u >= 1:
                        pe.wait_ge(S["o4_ready"], u)
                    for j in range(2):
                        hh = 2 * hp + j
                        o0 = ps[:, 6, (2 * j) * 17:(2 * j + 1) * 17]
                        o1 = ps[:, 6, (2 * j + 1) * 17:(2 * j + 2) * 17]
                        p = PT4[:, u % 2, j, :]
                        T.matmul(o0, p[:, 0:P], V4[:, 2 * b, hh, :], start=True, stop=True)
                        T.matmul(o1, p[:, P:2 * P], V4[:, 2 * b, hh, :], start=True, stop=False)
                        last = T.matmul(o1, p[:, 2 * P:3 * P], V4[:, 2 * b + 1, hh, :], start=False, stop=True)
                    last.then_inc(S["o4_psum"], 1)
            pe.wait_ge(S["w_loaded"], 16 * 7)
            for s in range(NT + 1):
                if s < NT:
                    to_T(3, s, AT[:, s, :], S["o4_ready"], 8 * (s // 2 + 1))
                if s >= 1:
                    project(3, s - 1, s - 1, 2 + (s - 1) % 2, woT, D, S["proj_psum"], S["x_ready"], 3 * NT + s - 2)
            def keys_T(lo, hi):
                pe.wait_ge(S["kq_step"], 8 * NT)
                pe.wait_ge(S["zeros_ready"], 2)
                for h in range(lo, hi):
                    if h >= 2:
                        pe.wait_ge(S["act5T_ready"], h - 1)
                    for t in range(NT):
                        c = (t * H + h) * 3 * HD
                        last = T.transpose(ps[:, 4 + h % 2, t * 64:(t + 1) * 64].bitcast(BF16), kpart_flat[:, c:c + P], identb[:, :])
                    last.then_inc(S["k5T_psum"], 1)

            keys_T(0, 7)
            for s in range(NT + 1):
                if s < NT:
                    to_T(4, s, XN[:, s, :], S["xn_ready"], 4 * NT + s + 1)
                if s >= 1:
                    project(4, s - 1, s - 1, 2 + (s - 1) % 2, wq5, D, S["q5_psum"], S["uq5_ready"], s - 2)
            keys_T(7, H)
            pe.wait_ge(S["q5i_ready"], 6)
            for h in range(H):
                if h == 2:
                    pe.wait_ge(S["act5T_ready"], H)
                if h >= 4:
                    pe.wait_ge(S[("act5T_ready", "dve5T_ready")[h % 2]], h // 2 - 1 + (0, H)[h % 2 == 0])
                for t in range(NT):
                    last = T.transpose(ps[0:48, q_bank(h), t * 64:(t + 1) * 64].bitcast(BF16), QI3[:, t, h, :, :].rearrange("p a c -> p (a c)"), identb[:, :])
                last.then_inc(S["q5T_psum"], 1)
            pe.wait_ge(S["dve5T_ready"], H // 2)
            pe.wait_ge(S["act5T_ready"], H + H // 2)
            pe.wait_ge(S["vint_ready"], 2 * NT)

            def heads(g, first, last=False):
                for i in range(STEPS if not last else LAG5):
                    h, q = 2 * g + i // NT, i % NT
                    n = h * NT + q
                    if not last:
                        wait_pos(pe, S["exp5_ready"], n - 1)
                        for c in range(2):
                            done = T.matmul(ps[:, 2 * (q % 2) + c, :], QT5[:, h, q * P:(q + 1) * P], KT5[:, h, c * 512:(c + 1) * 512], start=True, stop=True)
                        done.then_inc(S["s5_psum"], 1)
                    ready = "p5Te_ready" if i % 2 == 1 else "p5To_ready"
                    if not (first and i < 3) and not (last and i >= 3):
                        transposes(n - 3, (i + 1) % 2, (i + 1) % 4, ready, NT * g + (i - 3) // 2)
                    if not (first and i < 5):
                        j = i - 5
                        values(n - 5, j % NT, 2 * g + j // NT, (j // NT) % 2, ready, NT * g + (i - 3) // 2)

            def transposes(n, b, buf, ready, count):
                pe.wait_ge(S["pi5_ready"], n + 1)
                wait_pos(pe, S[ready], count)
                for k in range(8):
                    done = T.transpose(ps[:, 4 + b, k * 64:(k + 1) * 64].bitcast(BF16), PI5[:, buf, k * P:(k + 1) * P], identb[:, :])
                done.then_inc(S["p5T_psum"], 1)

            def values(n, q, h, bank, ready, count):
                pe.wait_ge(S[ready], count)
                if q == 0:
                    wait_pos(pe, S["o5_ready"], h - 1)
                for k in range(8):
                    done = T.matmul(ps[:, 6 + bank, q * HD:(q + 1) * HD], PT5[:, q % 2, k, :], VI[:, k, bass.ds(h * HD, HD)], start=(k == 0), stop=(k == 7))
                done.then_inc(S["p5V_done"], 1)

            heads(0, True)
            with T.Fori(1, H // 2) as g:
                heads(g, False)
            heads(H // 2, False, True)
            pe.wait_ge(S["vscale_ready"], 6)
            for s in range(NT + 1):
                if s < NT:
                    to_T(5, s, AT[:, s, :], S["o5_ready"], H)
                if s >= 1:
                    project(5, s - 1, s - 1, 2 + (s - 1) % 2, wp5, D, S["proj_psum"], S["x_ready"], 4 * NT + s - 2)
            for s in range(NT + 1):
                if s < NT:
                    to_T(6, s, XN[:, s, :], S["xn_ready"], 5 * NT + s + 1)
                if s >= 1:
                    if s == 1:
                        pe.wait_ge(S["x_ready"], 5 * NT)
                    t = s - 1
                    pe.wait_ge(S["tp_ready"], 6 * NT + s)
                    for k in range(KD):
                        last = T.matmul(ps[:, 2, t * NROUTE:(t + 1) * NROUTE], XT[:, k, t * P:(t + 1) * P], wclsT[:, k, :], start=(k == 0), stop=(k == KD - 1))
            last.then_inc(S["lg_psum"], 1)
            pe.wait_ge(S["router_ready"], 1)
            T.matmul(ps[:, 3, 0:NT * NE], lower[:, :], mr6[:, :, :].rearrange("p t e -> p (t e)"), start=True, stop=False)
            for t in range(NT - 1):
                later = NT - 1 - t
                last = T.matmul(ps[:, 3, (t + 1) * NE:NT * NE], onesb[:, :], mr6[:, t:t + 1, :].to_broadcast([P, later, NE]), start=False, stop=(t == NT - 2))
            last.then_inc(S["pos6_psum"], 1)

            def slot_list(e, lo=0, hi=8, done="list_psum"):
                pe.wait_ge(S["sel_ready"], e + 1)
                if e % EG == 0 and e >= 2 * EG:
                    pe.wait_ge(S["weight_ready"], e // EG - 1)
                for t in range(NT):
                    last = T.matmul(ps[:, 6 + (e // EG) % 2, (e % EG) * 8 + lo:(e % EG) * 8 + hi], SEL[:, e % 8, t, :], LR[:, t, e, lo:hi], start=(t == 0), stop=(t == NT - 1))
                last.then_inc(S[done], 1)

            pe.wait_ge(S["lr_const"], 5)
            for e in range(2 * EG):
                slot_list(e, 0, 4)
            for s in range(NE + 2):
                if s < NE:
                    pe.wait_ge(xe_loaded[s % 8], 16 * (s // 8 + 1))
                    if s >= 2:
                        pe.wait_ge(S["xeT_ready"], s - 1)
                    for k in range(KD):
                        last = T.transpose(ps[:, s % 2, k * P:(k + 1) * P], XE[:, s % 8, k * P:(k + 1) * P], identf[:, :])
                    last.then_inc(S["xeT_psum"], 1)
                if 1 <= s <= NE:
                    e = s - 1
                    pe.wait_ge(wg_loaded[e % 8], 32 * (e // 8 + 1))
                    pe.wait_ge(S["xeT_ready"], e + 1)
                    if e >= 2:
                        pe.wait_ge(S["he_ready"], e - 1)
                    for f in range(2):
                        for k in range(KD):
                            last = T.matmul(ps[:, 2 + e % 2, f * P:(f + 1) * P], WG[:, e % WS, k, f * P:(f + 1) * P], XET[:, e % 2, k, :], start=(k == 0), stop=(k == KD - 1))
                    last.then_inc(S["gu_psum"], 1)
                if s == 1:
                    pe.wait_ge(S["wpart_ready"], 4)
                    pe.wait_ge(S["list_ready"], 2)
                    for e in range(2 * EG):
                        slot_list(e, 4, 8, "wlist_psum")
                if s >= 2:
                    e = s - 2
                    pe.wait_ge(S["he_ready"], e + 1)
                    if e >= 2:
                        pe.wait_ge(S["ye_ready"], e - 1)
                    T.matmul(ps[:, 4 + e % 2, 0:D], HE[:, e % 2, :], WD[:, e % WS, :], start=True, stop=True).then_inc(S["ye_psum"], 1)
                for e in selects(s - 1):
                    slot_list(e)

        @block.vector
        def _(dve):
            v = nc.vector
            dve.wait_ge(S["const_ready"], 17)

            def norm_stats(n, s, count):
                order = PARITY_ORDER if n == 1 else IN_ORDER
                if s < NT:
                    if n == 0:
                        dve.wait_ge(S["x_loaded"], 16)
                    else:
                        dve.wait_ge(S["x_ready"], count + s + 1)
                    v.bn_stats(stats[:, order[s], :], X[:, order[s], :]).then_inc(S["stats_ready"], 1)
                if s >= 1:
                    dve.wait_ge(S["stats_ready"], n * NT + s)
                    v.bn_aggr(mv[:, order[s - 1], :], stats[:, order[s - 1], :]).then_inc(S["aggr_ready"], 1)

            def norm(n):
                order = PARITY_ORDER if n == 1 else IN_ORDER
                for s in range(NT):
                    t = order[s]
                    dve.wait_ge(S["rstd_ready"], 2 * n + s // 4 + 1)
                    v.tensor_scalar(XN[:, t, :], X[:, t, :], mv[:, t, 0:1], rstd[:, t:t + 1], ALU.subtract, ALU.mult).then_inc(S["xn_ready"], 1)

            def residual(s, t, bank, done, count):
                dve.wait_ge(done, count)
                v.tensor_tensor(X[:, t, :], X[:, t, :], ps[:, bank, 0:D], ALU.add).then_inc(S["x_ready"], 1)

            for s in range(NT + 1):
                norm_stats(0, s, 0)
            norm(0)
            score_products(dve, v, 0, S["prod0_ready"], range(0, 2))
            dve.wait_ge(S["w1_loaded"], 16)
            v.tensor_reduce(wsum[:, 0:1], w1stage.rearrange("p k c -> p (k c)"), AX.X, ALU.add, apply_absolute_value=True).then_inc(S["wabs_ready"], 1)
            score_products(dve, v, 0, S["prod0_ready"], range(2, 3))
            dve.wait_ge(S["w2_loaded"], 16)
            v.tensor_reduce(wsum[:, 1:2], w2stage.rearrange("p k c -> p (k c)"), AX.X, ALU.add, apply_absolute_value=True).then_inc(S["wabs_ready"], 1)
            score_products(dve, v, 0, S["prod0_ready"], range(3, 4))
            for j in range(2):
                for iq in range(4):
                    off = iq * (iq + 1) // 2
                    dve.wait_ge(S[f"prod{j}_ready"], off + iq + 1)
                    v.tensor_reduce(SC[:, j * 4 + iq, 0:iq + 1, :], prod[j][:, off:off + iq + 1, :].rearrange("p s (h d) -> p (s h) d", d=HD),
                                    AX.X, ALU.add).then_inc(S["step1"], 1)
            dve.wait_ge(S["step1"], 8)
            v.tensor_reduce(mx1[:, :, :], SC[:, :, :, :].rearrange("p a k h -> p a h k"), AX.X, ALU.max).then_inc(S["step1"], 1)
            dve.wait_ge(S["step1"], 9)
            v.tensor_tensor(SC[:, :, :, :], SC[:, :, :, :], mx1[:, :, :].unsqueeze(2).to_broadcast([P, 8, 4, H]), ALU.subtract).then_inc(S["step1"], 1)
            dve.wait_ge(S["wtot_psum"], 1)
            v.tensor_scalar(wmean[:, :], ps[:, 6, 0:2], 1.0 / (FF * D), EPS, ALU.mult, ALU.max).then_inc(S["wscale_ready"], 1)
            dve.wait_ge(S["wscale_ready"], 1)
            v.reciprocal(wrec[:, :], wmean[:, :]).then_inc(S["wscale_ready"], 1)
            v.tensor_scalar(w127[:, :], wmean[:, :], 1.0 / 127, None, ALU.mult).then_inc(S["wscale_ready"], 1)
            dve.wait_ge(S["exp1_ready"], 1)
            v.tensor_reduce(rs1[:, :, :], SC[:, :, :, :].rearrange("p a k h -> p a h k"), AX.X, ALU.add).then_inc(S["step1"], 1)
            dve.wait_ge(S["step1"], 11)
            v.reciprocal(rs1[:, :, :], rs1[:, :, :]).then_inc(S["step1"], 1)
            dve.wait_ge(S["step1"], 12)
            v.tensor_tensor(SC[:, :, :, :], SC[:, :, :, :], rs1[:, :, :].unsqueeze(2).to_broadcast([P, 8, 4, H]), ALU.mult).then_inc(S["step1"], 1)
            dve.wait_ge(S["step1"], 13)
            value_products(dve, v, 0, S["prod0_ready"])
            for j in range(2):
                for iq in range(4):
                    off = iq * (iq + 1) // 2
                    dve.wait_ge(S[f"prod{j}_ready"], 10 + off + iq + 1)
                    v.tensor_reduce(AT[:, 2 * iq + j, :], prod[j][:, off:off + iq + 1, :].rearrange("p s c -> p c s"),
                                    AX.X, ALU.add).then_inc(S["at_ready"], 1)
            for s in range(NT + 2):
                if s < NT:
                    residual(s, PARITY_ORDER[s], 2 + s % 2, S["proj_psum"], s + 1)
                if s >= 1:
                    norm_stats(1, s - 1, 0)
            norm(1)
            for s in range(NB + 2):
                if s < NB:
                    dve.wait_ge(S["s2_psum"], s + 1)
                    v.tensor_reduce(nm2[:, s % 2, :], ps[:, 2 + s % 2, :].rearrange("p (e c) -> p e c", e=2), AX.X, ALU.max, negate=True).then_inc(S["nm2_ready"], 1)
                    dve.wait_ge(S["nm2_ready"], s + 1)
                    v.tensor_scalar(b2[:, s % 2, :], nm2[:, s % 2, :], 1.0 / 16, None, ALU.mult).then_inc(S["bias2_ready"], 1)
                if 1 <= s <= NB:
                    i = s - 1
                    dve.wait_ge(S["exp2_ready"], 2 * (i + 1))
                    v.reciprocal(r2[:, i % 2, :], sum2[:, i % 2, :]).then_inc(S["r2_ready"], 1)
                    dve.wait_ge(S["r2_ready"], i + 1)
                    for e in range(2):
                        v.tensor_scalar(E2[:, i % 2, e, :], E2[:, i % 2, e, :], r2[:, i % 2, e:e + 1], None, ALU.mult).then_inc(S["attn2_ready"], 1)
                if s < 2:
                    dve.wait_ge(S["wq_step"], s + 3)
                    stage, dst = ((w1stage, w1t), (w2stage, w2t))[s]
                    v.tensor_scalar(dst[:, :, :], stage, 1.0, -1.0, ALU.min, ALU.max).then_inc(S["w_ternary"], 1)
                if s >= 2:
                    i = s - 2
                    if i == NB - 1:
                        dve.wait_ge(S["kv_ready"], NT)
                        v.tensor_reduce(kmax[:, :, :], KV[:, :, 0:D].rearrange("p t (h d) -> p t h d", h=H), AX.X, ALU.max, apply_absolute_value=True).then_inc(S["kscale_ready"], 1)
                    dve.wait_ge(S["out2_psum"], i + 1)
                    for j in range(2):
                        v.tensor_tensor(X[:, 2 * i + j, :], X[:, 2 * i + j, :], ps[:, 4 + i % 2, j * D:(j + 1) * D], ALU.add).then_inc(S["x_ready"], 1)
                    for j in range(2):
                        norm_stats(2, 2 * i + j, NT)
            norm_stats(2, NT, NT)
            norm(2)
            dve.wait_ge(S["xn_ready"], 3 * NT)
            v.tensor_reduce(am3[:, :], XN[:, :, :], AX.X, ALU.max, apply_absolute_value=True).then_inc(S["dq3_step"], 1)
            dve.wait_ge(S["dq3_step"], 1)
            v.tensor_scalar(am3[:, :], am3[:, :], EPS, None, ALU.max).then_inc(S["dq3_step"], 1)
            dve.wait_ge(S["dq3_step"], 2)
            v.reciprocal(qs3[:, :], am3[:, :]).then_inc(S["dq3_step"], 1)
            v.tensor_scalar(dq3[:, :], am3[:, :], w127[:, 0:1], None, ALU.mult).then_inc(S["dq3_step"], 1)
            dve.wait_ge(S["dq3_step"], 3)
            v.tensor_scalar(qs3[:, :], qs3[:, :], 127.0, None, ALU.mult).then_inc(S["dq3_step"], 1)
            dve.wait_ge(S["dq3_step"], 5)
            for s in range(NT + 1):
                if s < NT:
                    v.tensor_scalar(XN[:, s, :], XN[:, s, :], qs3[:, s:s + 1], ROUND, ALU.mult, ALU.add).then_inc(S["qx_step"], 1)
                if s >= 1:
                    dve.wait_ge(S["qx_step"], s)
                    v.tensor_scalar(QX[:, s - 1, :], XN[:, s - 1, :], -ROUND, None, ALU.add).then_inc(S["qx_ready"], 1)
            for s in range(NT + 1):
                if s < NT:
                    dve.wait_ge(S["gelu_ready"], s + 1)
                    g3 = G3[:, s % 2, :]
                    v.tensor_reduce(am3b[:, s:s + 1], g3, AX.X, ALU.max, apply_absolute_value=True).then_inc(S["am3_step"], 1)
                    dve.wait_ge(S["am3_step"], 5 * s + 1)
                    v.tensor_scalar(am3b[:, s:s + 1], am3b[:, s:s + 1], EPS, None, ALU.max).then_inc(S["am3_step"], 1)
                    dve.wait_ge(S["am3_step"], 5 * s + 2)
                    v.reciprocal(qs3b[:, s:s + 1], am3b[:, s:s + 1]).then_inc(S["am3_step"], 1)
                    dve.wait_ge(S["am3_step"], 5 * s + 3)
                    v.tensor_scalar(qs3b[:, s:s + 1], qs3b[:, s:s + 1], 127.0, None, ALU.mult).then_inc(S["am3_step"], 1)
                    v.tensor_scalar(dq3b[:, s:s + 1], am3b[:, s:s + 1], w127[:, 1:2], None, ALU.mult).then_inc(S["am3_step"], 1)
                    dve.wait_ge(S["am3_step"], 5 * s + 4)
                    v.tensor_scalar(g3, g3, qs3b[:, s:s + 1], ROUND, ALU.mult, ALU.add).then_inc(S["qh_step"], 1)
                    dve.wait_ge(S["qh_step"], 2 * s + 1)
                    if s >= 2:
                        dve.wait_ge(S["qhT_psum"], s - 1)
                    v.tensor_scalar(QH[:, s % 2, :], g3, -ROUND, None, ALU.add).then_inc(S["qh_step"], 1)
                    dve.wait_ge(S["qh_step"], 2 * s + 2)
                    dve.sem_inc(S["qh_ready"], 1)
                if s >= 1:
                    u = s - 1
                    dve.wait_ge(S["out3_psum"], u + 1)
                    v.scalar_tensor_tensor(X[:, u, :], ps[:, 7, 0:D], dq3b[:, u:u + 1], X[:, u, :], ALU.mult, ALU.add).then_inc(S["x_ready"], 1)
                if s >= 2:
                    norm_stats(3, s - 2, 2 * NT)
            norm_stats(3, NT - 1, 2 * NT)
            norm_stats(3, NT, 2 * NT)
            norm(3)
            for s in range(NT + 1):
                if s < NT:
                    dve.wait_ge(S["low_psum"], s + 1)
                    for k in range(2):
                        v.bn_stats(st4[:, 2 * s + k, :], ps[:, 2 + s % 4, k * LOW:(k + 1) * LOW]).then_inc(S["lstats_ready"], 1)
                    for k in range(2):
                        dve.wait_ge(S["lstats_ready"], 2 * s + k + 1)
                        v.bn_aggr(mv4[:, 2 * s + k, :], st4[:, 2 * s + k, :]).then_inc(S["laggr_ready"], 1)
                if s >= 1:
                    dve.wait_ge(S["lrstd_ready"], s)
                    for k in range(2):
                        c = 2 * (s - 1) + k
                        v.tensor_scalar(CN[:, s - 1, k * LOW:(k + 1) * LOW], ps[:, 2 + (s - 1) % 4, k * LOW:(k + 1) * LOW], mv4[:, c, 0:1], rs4[:, c:c + 1],
                                        ALU.subtract, ALU.mult).then_inc(S["cn_ready"], 1)
            dve.wait_ge(S["kscale_ready"], 1)
            v.tensor_scalar(sk[:, :, :], kmax[:, :, :], 1.0 / 127, 1e-8, ALU.mult, ALU.max).then_inc(S["kscale_ready"], 1)
            dve.wait_ge(S["kscale_ready"], 2)
            v.reciprocal(rk[:, :, :], sk[:, :, :]).then_inc(S["kscale_ready"], 1)
            v.tensor_reduce(vmax[:, :], KV[:, :, D:2 * D].rearrange("p t c -> p c t"), AX.X, ALU.max, apply_absolute_value=True).then_inc(S["vmax_ready"], 1)
            for j in range(1, 8, 2):
                dve.wait_ge(S["upq_psum"], j + 1)
                v.tensor_copy(QT4[:, j % 4, (j // 4) * 512:(j // 4 + 1) * 512], ps[:, 2 + j % 4, :]).then_inc(S["upqd_ready"], 1)
            v.memset(V4[:, :, :, HD:HD + 1], 1.0).then_inc(S["upqd_ready"], 1)

            dve.wait_ge(S["vmaxT_psum"], 1)
            v.tensor_reduce(vm2[:, :], ps[:, 6, 0:D].rearrange("p (k c) -> p k c", k=KD), AX.X, ALU.max).then_inc(S["vscale_ready"], 1)
            dve.wait_ge(S["vscale_ready"], 1)
            v.tensor_scalar(svrv[:, 0, :], vm2[:, :], 1.0 / 127, 1e-8, ALU.mult, ALU.max).then_inc(S["vscale_ready"], 1)
            dve.wait_ge(S["vscale_ready"], 2)
            v.reciprocal(svrv[:, 1, :], svrv[:, 0, :]).then_inc(S["vscale_ready"], 1)
            dve.wait_ge(S["vscale_ready"], 3)
            v.tensor_copy(svb[:, :, :], svrv[:, :, :].rearrange("p a k -> p (a k)").unsqueeze(2).to_broadcast([P, 4, P])).then_inc(S["vscale_ready"], 1)

            dve.wait_ge(S["w_loaded"], 16 * 7)
            for k in range(KD):
                v.tensor_scalar(wp5[:, k, :], wp5[:, k, :], svrv[:, 0, k:k + 1], None, ALU.mult).then_inc(S["vscale_ready"], 1)

            def keys_d(n):
                dve.wait_ge(S["kup_psum"], n + 1)
                b, half = n // 2, n % 2
                for r in range(2, 4):
                    v.tensor_copy(KB4[32 * r:32 * r + 32, b % 2, 2 * half:2 * half + 2, r, :],
                                  ps[32 * r:32 * r + 32, 7, :].rearrange("p (g c) -> p g c", g=2)).then_inc(S["kupd_ready"], 1)

            dve.wait_ge(S["kb_zero"], 2)
            keys_d(0)
            keys_d(1)
            for s in range(U4 + 2):
                if s % 8 in (3, 6) and s < 24:
                    keys_d(2 * (s // 8 + 1) + (s % 8) // 6)
                if s < U4:
                    dve.wait_ge(S["s4_psum"], s + 1)
                    sc = ps[:, 2 * (s % 2):2 * (s % 2) + 2, :]
                    v.tensor_reduce(m4[:, s % 2, 0, :], sc[:, :, 0:P], AX.X, ALU.max).then_inc(S["max4_ready"], 1)
                    v.tensor_reduce(m4[:, s % 2, 1, :], sc[:, :, P:3 * P], AX.X, ALU.max).then_inc(S["max4_ready"], 1)
                    if s >= 2:
                        dve.wait_ge(S["p4T_psum"], s - 1)
                    for q, (lo, hi) in enumerate(((0, P), (P, 3 * P))):
                        dve.wait_ge(S["max4_ready"], 2 * s + q + 1)
                        v.tensor_tensor(E4[:, s % 2, :, lo:hi], sc[:, :, lo:hi], m4[:, s % 2, q, :].unsqueeze(2).to_broadcast([P, 2, hi - lo]),
                                        ALU.subtract).then_inc(S["sub4_ready"], 1)
                if s >= 2:
                    u = s - 2
                    b, hp = u // 8, u % 8
                    dve.wait_ge(S["o4_psum"], u + 1)
                    o = ps[:, 6, 0:68].rearrange("p (a c) -> p a c", c=17)
                    v.reciprocal(r4[:, u % 2, :], o[:, :, 16]).then_inc(S["r4_ready"], 1)
                    dve.wait_ge(S["r4_ready"], u + 1)
                    v.tensor_tensor(AT[:, 2 * b:2 * b + 2, 2 * hp * HD:(2 * hp + 2) * HD].rearrange("p t (j c) -> p j t c", c=HD),
                                    o[:, :, 0:HD].rearrange("p (j t) c -> p j t c", t=2),
                                    r4[:, u % 2, :].rearrange("p (j t) -> p j t", t=2).unsqueeze(3).to_broadcast([P, 2, 2, HD]), ALU.mult).then_inc(S["o4_ready"], 1)
            for s in range(NT + 2):
                if s < NT:
                    residual(s, s, 2 + s % 2, S["proj_psum"], NT + s + 1)
                if s >= 1:
                    norm_stats(4, s - 1, 3 * NT)
            norm(4)
            for s in range(NT):
                dve.wait_ge(S["q5_psum"], s + 1)
                v.tensor_tensor(AT[:, s, :], ps[:, 2 + s % 2, 0:D], bqr[:, :], ALU.add).then_inc(S["uq5_ready"], 1)
            dve.wait_ge(S["uq5_ready"], NT)
            heads_view = AT[:, :, :].rearrange("p t (h d) -> p (t h) d", d=HD)
            v.tensor_reduce(sq5[:, :, :].rearrange("p t h -> p (t h)"), heads_view, AX.X, ALU.max, apply_absolute_value=True).then_inc(S["q5_step"], 1)
            dve.wait_ge(S["q5_step"], 1)
            v.tensor_scalar(sq5[:, :, :], sq5[:, :, :], 0.25 / 127, 1e-8, ALU.mult, ALU.max).then_inc(S["q5_step"], 1)
            dve.wait_ge(S["q5_step"], 2)
            v.reciprocal(rq5[:, :, :], sq5[:, :, :]).then_inc(S["q5_step"], 1)
            dve.wait_ge(S["q5_step"], 3)
            v.tensor_scalar(rq5[:, :, :], rq5[:, :, :], 0.25, None, ALU.mult).then_inc(S["q5_step"], 1)
            dve.wait_ge(S["q5_step"], 4)
            v.tensor_tensor(heads_view, heads_view, rq5[:, :, :].rearrange("p t h -> p (t h)").unsqueeze(2).to_broadcast([P, NT * H, HD]), ALU.mult).then_inc(S["q5_step"], 1)
            dve.wait_ge(S["q5_step"], 5)
            dve.wait_ge(S["k5T_psum"], H)
            for a in range(3):
                for half in range(2):
                    tiles = slice(4 * half, 4 * half + 4)
                    v.tensor_scalar(QI3[:, tiles, :, a, :].rearrange("p t h d -> p (t h) d"), AT[:, tiles, :].rearrange("p t (h d) -> p (t h) d", d=HD),
                                    ROUND, -ROUND, ALU.add, ALU.add).then_inc(S["q5i_ready"], 1)
            dve.wait_ge(S["pad5_ready"], 1)
            for h in range(1, H, 2):
                dve.wait_ge(S["q5T_psum"], h + 1)
                v.tensor_copy(QT5[0:48, h, :], ps[0:48, q_bank(h), :].bitcast(BF16)).then_inc(S["dve5T_ready"], 1)

            def softmax(g, first, last=False):
                for i in range(STEPS if not last else LAG5):
                    h, q = 2 * g + i // NT, i % NT
                    n = h * NT + q
                    if not last:
                        dve.wait_ge(S["s5_psum"], n + 1)
                        wait_pos(dve, S["bias5_ready"], n - 3)
                        v.tensor_reduce(nm5[:, q % 4:q % 4 + 1], ps[:, 2 * (q % 2):2 * (q % 2) + 2, :].rearrange("p a c -> p (a c)"), AX.X, ALU.max, negate=True).then_inc(S["max5_ready"], 1)
                    if i == 0 and not last:
                        wait_pos(dve, S["bias5_ready"], n)
                        v.tensor_copy(sp5[:, :, :], sq5[:, :, bass.ds(2 * g, 2)]).then_inc(S["scale5_ready"], 1)
                    if i % 2 == 1 and not (first and i < 4) and not (last and i >= 4):
                        m = n - 4
                        dve.wait_ge(S["p5T_psum"], m + 1)
                        wait_pos(dve, S["p5V_done"], m - 1)
                        v.tensor_copy(PT5[:, 1, :, :], ps[:, 5, :].bitcast(BF16).rearrange("p (k c) -> p k c", k=8)).then_inc(S["p5To_ready"], 1)
                    if not (first and i < 1) and not (last and i >= 1):
                        dve.wait_ge(S["exp5_ready"], n)
                        wait_pos(dve, S["p5T_psum"], n - 4)
                        v.tensor_copy(PI5[:, (i - 1) % 4, :], Y5[:, (i - 1) % 2, :]).then_inc(S["pi5_ready"], 1)
                    if i % NT == 6 and not (first and i < NT) and not last:
                        outputs(2 * g + i // NT - 1, (i // NT - 1) % 2)

            def outputs(h, bank):
                dve.wait_ge(S["p5V_done"], (h + 1) * NT)
                v.reciprocal(r5[:, :], sum5[:, bass.ds(h * NT, NT)]).then_inc(S["r5_ready"], 1)
                dve.wait_ge(S["r5_ready"], h + 1)
                v.tensor_tensor(AT[:, :, bass.ds(h * HD, HD)], ps[:, 6 + bank, 0:P].rearrange("p (t c) -> p t c", t=NT),
                                r5[:, :].unsqueeze(2).to_broadcast([P, NT, HD]), ALU.mult).then_inc(S["o5_ready"], 1)

            softmax(0, True)
            with v.Fori(1, H // 2) as g:
                softmax(g, False)
            softmax(H // 2, False, True)
            outputs(H - 1, 1)
            dve.wait_ge(S["xbias_ready"], NT)
            for s in range(NT + 2):
                if s < NT:
                    residual(s, s, 2 + s % 2, S["proj_psum"], 2 * NT + s + 1)
                if s >= 1:
                    norm_stats(5, s - 1, 4 * NT)
            norm(5)
            c6 = [0]

            def step(inst, last=True):
                inst.then_inc(S["step6"], 1)
                c6[0] += 1
                if last:
                    dve.wait_ge(S["step6"], c6[0])

            dve.wait_ge(S["lg_psum"], 1)
            lg = ps[:, 2, :].rearrange("p (t e) -> p t e", t=NT)
            per_tile = lambda a, n: a.unsqueeze(2).to_broadcast([P, NT, n])
            step(v.tensor_reduce(s6[:, 0, :], lg, AX.X, ALU.max))
            step(v.tensor_tensor(L6[:, :, :], lg, per_tile(s6[:, 0, :], NROUTE), ALU.subtract))
            dve.wait_ge(S["exp6_ready"], 1)
            step(v.tensor_reduce(s6[:, 1, :], L6[:, :, :], AX.X, ALU.add))
            step(v.reciprocal(s6[:, 1, :], s6[:, 1, :]))
            step(v.tensor_tensor(L6[:, :, :], L6[:, :, :], per_tile(s6[:, 1, :], NROUTE), ALU.mult))
            step(v.tensor_tensor(BI6[:, :, :], L6[:, :, :], rbias[:, :].unsqueeze(1).to_broadcast([P, NT, NROUTE]), ALU.add))
            for t in range(NT):
                step(v.max(top6[:, t, :], BI6[:, t, :]), t == NT - 1)
            for t in range(NT):
                step(v.match_replace(RP6[:, t, :], top6[:, t, :], BI6[:, t, :], NEG), t == NT - 1)
            step(v.tensor_tensor(mr6[:, :, :], BI6[:, :, 0:NE], RP6[:, :, 0:NE], ALU.not_equal))
            dve.sem_inc(S["router_ready"], 1)
            step(v.tensor_tensor(MK6[:, :, :], BI6[:, :, :], RP6[:, :, :], ALU.not_equal))
            step(v.tensor_tensor(L6[:, :, :], L6[:, :, :], MK6[:, :, :], ALU.mult))
            dve.wait_ge(S["pos6_psum"], 1)
            pos = ps[:, 3, 0:NT * NE].rearrange("p (t e) -> p t e", t=NT)
            step(v.scalar_tensor_tensor(pos6[:, :, :], mr6[:, :, :], -256.0, pos, ALU.mult, ALU.add))

            def select(e):
                if e >= 8:
                    dve.wait_ge(S["list_psum"], e - 7)
                    dve.wait_ge(S["wlist_psum"], min(e - 7, 2 * EG))
                v.tensor_tensor(SEL[:, e % 8, :, :], iota6[:, :].unsqueeze(1).to_broadcast([P, NT, CAP]),
                                pos6[:, :, e].unsqueeze(2).to_broadcast([P, NT, CAP]), ALU.is_equal).then_inc(S["sel_ready"], 1)

            def tokens(n):
                dve.wait_ge(S["list_psum"], EG * (n + 1))
                pl = ps[:, 6 + n % 2, 0:EG * 8].rearrange("p (e c) -> p e c", e=EG)
                v.tensor_scalar(empty6[:, n % 2, :], pl[:, :, 3], dump6[:, 1:2], dump6[:, 0:1], ALU.mult, ALU.add).then_inc(S["list_step"], 1)
                v.tensor_reduce(list6[:, n % 2, :], pl[:, :, 0:3], AX.X, ALU.add).then_inc(S["list_step"], 1)
                dve.wait_ge(S["list_step"], 2 * n + 2)
                v.tensor_tensor(slot_token[:, EG * n:EG * n + EG], list6[:, n % 2, :], empty6[:, n % 2, :], ALU.add).then_inc(S["list_ready"], 1)

            def weights(n):
                pl = ps[:, 6 + n % 2, 0:EG * 8].rearrange("p (e c) -> p e c", e=EG)
                v.tensor_reduce(slot_weight[:, EG * n:EG * n + EG], pl[:, :, 4:7], AX.X, ALU.add).then_inc(S["weight_ready"], 1)

            for e in range(EG):
                select(e)
            step(v.tensor_reduce(s6[:, 2, :], L6[:, :, :], AX.X, ALU.add), False)
            tokens(0)
            step(v.tensor_reduce(s6[:, 3, :], L6[:, :, NE:NROUTE], AX.X, ALU.add))
            step(v.tensor_scalar(s6[:, 2, :], s6[:, 2, :], 1e-20, None, ALU.add))
            step(v.reciprocal(s6[:, 2, :], s6[:, 2, :]))
            step(v.tensor_scalar(s6[:, 2, :], s6[:, 2, :], 1.5, None, ALU.mult))
            step(v.tensor_tensor(s6[:, 3, :], s6[:, 2, :], s6[:, 3, :], ALU.mult))
            step(v.scalar_tensor_tensor(s6[:, 4, :], s6[:, 3, :], 1.0, s6[:, 2, :], ALU.add, ALU.mult))
            v.tensor_tensor(L6[:, :, 0:NE], L6[:, :, 0:NE], per_tile(s6[:, 4, :], NE), ALU.mult).then_inc(S["router_ready"], 1)
            for e in range(EG, 2 * EG):
                select(e)
            tokens(1)
            for s in range(NE):
                for e in selects(s) if s > 0 else ():
                    select(e)
                dve.wait_ge(S["silu_ready"], s + 1)
                if s >= 2:
                    dve.wait_ge(S["ye_psum"], s - 1)
                v.tensor_tensor(HE[:, s % 2, :], SG[:, s % 2, :], ps[:, 2 + s % 2, CAP:2 * CAP], ALU.mult).then_inc(S["he_ready"], 1)
                if s == 0:
                    dve.wait_ge(S["wlist_psum"], 2 * EG)
                    weights(0)
                    weights(1)
                    for e in selects(0):
                        select(e)
                if s >= 2 and s + LEAD < NE + EG and (s + LEAD) % EG == 0:
                    tokens((s + LEAD) // EG - 1)
                    weights((s + LEAD) // EG - 1)
            for t in range(NT):
                dve.wait_ge(sums_loaded[t // 2], 32)
                v.tensor_tensor(SUM[:, 0, t, :], SUM[:, 0, t, :], SUM[:, 1, t, :], ALU.add).then_inc(S["sums_added"], 1)
                dve.wait_ge(S["sums_added"], t + 1)
                v.tensor_tensor(X[:, t, :], X[:, t, :], SUM[:, 0, t, :], ALU.add).then_inc(S["x_ready"], 1)


_ARGS = [("x", None), ("ctx_2048", None), ("ctx_2048", (2, 0, 1)), ("L0_attn_weight_qkv", (1, 0)), ("L0_attn_weight_proj", (1, 0)),
         ("L0_ffn_w1", (1, 0)), ("L0_ffn_w2", (1, 0)), ("L1_attn_W_dq", None), ("L1_attn_W_uq", None), ("L1_attn_q_ln_g", None),
         ("L1_attn_q_ln_b", None), ("L1_attn_W_dkv", None), ("L1_attn_W_ukv", None), ("L1_attn_kv_ln_g", None), ("L1_attn_kv_ln_b", None),
         ("L1_attn_W_o", (1, 0)), ("L1_xattn_Wq", None), ("L1_xattn_bq", None), ("L1_xattn_Wkv", None), ("L1_xattn_bkv", None),
         ("L1_xattn_Wp", None), ("L1_xattn_bp", None), ("L1_ffn_w_cls", (1, 0)), ("L1_ffn_bias", None), ("L1_ffn_w_gate_up", None),
         ("L1_ffn_w_down", None)]


def kernel(**inputs):
    import numpy as np
    import concourse.bacc as bacc
    from concourse.bass_utils import run_bass_kernel_spmd

    nc = bacc.Bacc("TRN2", target_bir_lowering=False, num_devices=1)
    arrays, args = {}, []
    for i, (name, order) in enumerate(_ARGS):
        a = np.asarray(inputs[name])
        if order is not None:
            a = a.transpose(order)
        if len(order or ()) == 3:
            a = a.reshape(a.shape[0], -1)
        a = np.ascontiguousarray(a)
        arrays[f"in_{i}"] = a
        args.append(nc.dram_tensor(f"in_{i}", a.shape, mybir.dt.from_np(a.dtype), kind="ExternalInput").ap())
    out = nc.dram_tensor("out_0", (NB, SEQ, D), F32, kind="ExternalOutput").ap()
    decoder_kernel(nc, *args, out)
    r = run_bass_kernel_spmd(nc, [arrays], core_ids=[0])
    return r.results[0]["out_0"]
```
